# Optimizing a Trainium2 kernel written in Bass

```python
import numpy as np
import jax
import jax.numpy as jnp

def _softmax(x, axis=-1):
    return jax.nn.softmax(x, axis=axis)

def _gelu(x):
    return jax.nn.gelu(x, approximate=True)

def _silu(x):
    return jax.nn.silu(x)

def _sigmoid(x):
    return jax.nn.sigmoid(x)

def _layernorm(x, axis=-1, eps=1e-05):
    m = jnp.mean(x, axis=axis, keepdims=True)
    v = jnp.var(x, axis=axis, keepdims=True)
    return (x - m) / jnp.sqrt(v + eps)

def _scatter_add(tgt, idx, src, axis=0):
    return tgt.at[idx].add(src)

def _segment_sum(src, seg, n):
    return jax.ops.segment_sum(src, seg, n)
kernel_name = 'mk_audio_tower_d2_tok_audfeat256_r4_65de47'

def setup_inputs(seed: int=0):
    np.random.seed(seed)
    _w = jnp.asarray

    def _rec_inputs():
        import jax
        import jax.numpy as jnp
        _rk = jax.random.key(seed)
        x = 7.22013e-05 + 1.00017 * jax.random.normal(jax.random.fold_in(_rk, 1), (8, 750, 64), jnp.float32)
        return x
    x = _rec_inputs()

    def _L0_tok_setup():
        import jax, jax.numpy as jnp
        import numpy as np
        WIN = 9
        key = jax.random.key(seed)
        ks = jax.random.split(key, 4)
        N, L, C, U = (8, 1024, 64, 64)
        x = jax.random.normal(ks[0], (N, L, C), dtype=jnp.float32)
        W_qry = jax.random.normal(ks[1], (C, U), dtype=jnp.float32) * 0.05
        W_key = jax.random.normal(ks[2], (C, U), dtype=jnp.float32) * 0.05
        v = jax.random.normal(ks[3], (U,), dtype=jnp.float32) * 0.05
        b = jnp.zeros((U,), dtype=jnp.float32)
        return {'x': x, 'W_qry': W_qry, 'W_key': W_key, 'v': v, 'b': b}
    _L0_tok_all = _L0_tok_setup()
    _L0_tok_in = {k: v for k, v in _L0_tok_all.items() if k in ('W_qry', 'W_key', 'v', 'b')}
    del _L0_tok_all

    def _L0_attn_setup():
        import jax, jax.numpy as jnp
        import numpy as np
        D_MODEL = 64
        N_HEAD = 8

        def _l1_scores(q, k):
            scale = 1.0 / np.sqrt(q.shape[-1]).astype(np.float32)
            q_sbhw = q.transpose(1, 0, 2, 3)

            def one_query(qs):
                return -jnp.sum(jnp.abs(qs[:, None, :, :] - k), axis=-1) * scale
            s = jax.lax.map(one_query, q_sbhw)
            return s.transpose(1, 0, 2, 3)
        key = jax.random.key(seed)
        ks = jax.random.split(key, 3)
        b, t = (4, 250)
        x = jax.random.normal(ks[0], (b, t, D_MODEL), jnp.float32)
        wqv_w = 0.005 * jax.random.normal(ks[1], (3 * N_HEAD * D_MODEL, D_MODEL), jnp.float32)
        wqv_b = jnp.zeros((3 * N_HEAD * D_MODEL,), jnp.float32)
        wk = 0.005 * jnp.ones((N_HEAD, D_MODEL), jnp.float32)
        fanin_w = 0.005 * jax.random.normal(ks[2], (D_MODEL, D_MODEL), jnp.float32)
        fanin_b = jnp.zeros((D_MODEL,), jnp.float32)
        return dict(x=x, wqv_w=wqv_w, wqv_b=wqv_b, wk=wk, fanin_w=fanin_w, fanin_b=fanin_b)
    _L0_attn_all = _L0_attn_setup()
    _L0_attn_in = {k: v for k, v in _L0_attn_all.items() if k in ('wqv_w', 'wqv_b', 'wk', 'fanin_w', 'fanin_b')}
    del _L0_attn_all

    def _L0_ffn_setup():
        import jax, jax.numpy as jnp
        import numpy as np
        E = 8
        K = 2
        D = 64
        H = 128
        DOUT = 64
        EPS = 1e-05
        key = jax.random.key(seed)
        ks = jax.random.split(key, 9)
        s = 0.02
        return {'x': jax.random.normal(ks[0], (4, 2048, D), jnp.float32), 'gamma': 1.0 + 0.05 * jax.random.normal(ks[1], (D,), jnp.float32), 'beta': 0.05 * jax.random.normal(ks[2], (D,), jnp.float32), 'Wr': 0.01 * jax.random.normal(ks[3], (D, E), jnp.float32), 'br': jnp.zeros((E,), jnp.float32), 'W1': s * jax.random.normal(ks[4], (E, D, H), jnp.float32), 'b1': s * jax.random.normal(ks[5], (E, H), jnp.float32), 'W2': s * jax.random.normal(ks[6], (E, H, DOUT), jnp.float32), 'b2': s * jax.random.normal(ks[7], (E, DOUT), jnp.float32)}
    _L0_ffn_all = _L0_ffn_setup()
    _L0_ffn_in = {k: v for k, v in _L0_ffn_all.items() if k in ('gamma', 'beta', 'Wr', 'br', 'W1', 'b1', 'W2', 'b2')}
    del _L0_ffn_all

    def _L1_attn_setup():
        import jax, jax.numpy as jnp
        import numpy as np
        NUM_HEADS = 8
        LOCAL_WINDOW = 16
        NEG_INF = -10000000000.0
        key = jax.random.key(seed)
        k0, k1, k2 = jax.random.split(key, 3)
        B, N, C = (2, 1024, 64)
        x = jax.random.normal(k0, (B, N, C), dtype=jnp.float32)
        w_qkv = jax.random.normal(k1, (C, 3 * C), dtype=jnp.float32) * 0.02
        w_proj = jax.random.normal(k2, (C, C), dtype=jnp.float32) * 0.02
        b_proj = jnp.zeros((C,), dtype=jnp.float32)
        return {'x': x, 'w_qkv': w_qkv, 'w_proj': w_proj, 'b_proj': b_proj}
    _L1_attn_all = _L1_attn_setup()
    _L1_attn_in = {k: v for k, v in _L1_attn_all.items() if k in ('w_qkv', 'w_proj', 'b_proj')}
    del _L1_attn_all

    def _L1_ffn_setup():
        import jax, jax.numpy as jnp
        import numpy as np
        DIM = 64
        HEADS = 8
        NUM_KEYS = 64
        NUM_KV = NUM_KEYS ** 2
        PK_TOPK = 16
        FINAL_TOPK = 16
        DIM_KEY = DIM // 2
        P = 2

        def _pk(x, Wq_pk, pk_keys):
            b, n, _ = x.shape
            q = (x @ Wq_pk).reshape(b, n, P, HEADS, DIM_KEY).transpose(2, 0, 1, 3, 4)
            sim = jnp.einsum('pbnhd,pkhd->pbnhk', q, pk_keys)
            scores, idx = jax.lax.top_k(sim, PK_TOPK)
            idx0 = idx[0]
            idx1 = idx[1] * NUM_KEYS
            index = (idx0[..., :, None] + idx1[..., None, :]).reshape(b, n, HEADS, PK_TOPK * PK_TOPK)
            score = (scores[0][..., :, None] + scores[1][..., None, :]).reshape(b, n, HEADS, PK_TOPK * PK_TOPK)
            final_scores, pk_idx = jax.lax.top_k(score, FINAL_TOPK)
            final_indices = jnp.take_along_axis(index, pk_idx, axis=-1)
            final_scores = jax.nn.softmax(final_scores, axis=-1)
            return (final_scores, final_indices)
        key = jax.random.key(seed)
        ks = jax.random.split(key, 7)
        b, n = (2, 256)
        std = 0.02
        x = jax.random.normal(ks[0], (b, n, DIM), dtype=jnp.float32)
        Wq_pk = jax.random.normal(ks[1], (DIM, P * HEADS * DIM_KEY), dtype=jnp.float32) * std
        pk_keys = jax.random.normal(ks[2], (P, NUM_KEYS, HEADS, DIM_KEY), dtype=jnp.float32) * std
        Wq = jax.random.normal(ks[3], (DIM, HEADS * DIM), dtype=jnp.float32) * std
        keys_table = jax.random.normal(ks[4], (NUM_KV * HEADS, DIM), dtype=jnp.float32) * std
        values_table = jax.random.normal(ks[5], (NUM_KV * HEADS, DIM), dtype=jnp.float32) * std
        Wo = jax.random.normal(ks[6], (DIM * HEADS, DIM), dtype=jnp.float32) * std
        return {'x': x, 'Wq_pk': Wq_pk, 'pk_keys': pk_keys, 'Wq': Wq, 'keys_table': keys_table, 'values_table': values_table, 'Wo': Wo}
    _L1_ffn_all = _L1_ffn_setup()
    _L1_ffn_in = {k: v for k, v in _L1_ffn_all.items() if k in ('Wq_pk', 'pk_keys', 'Wq', 'keys_table', 'values_table', 'Wo')}
    del _L1_ffn_all
    return {'x': x, 'L0_tok_W_qry': _L0_tok_in['W_qry'], 'L0_tok_W_key': _L0_tok_in['W_key'], 'L0_tok_v': _L0_tok_in['v'], 'L0_tok_b': _L0_tok_in['b'], 'L0_attn_wqv_w': _L0_attn_in['wqv_w'], 'L0_attn_wqv_b': _L0_attn_in['wqv_b'], 'L0_attn_wk': _L0_attn_in['wk'], 'L0_attn_fanin_w': _L0_attn_in['fanin_w'], 'L0_attn_fanin_b': _L0_attn_in['fanin_b'], 'L0_ffn_gamma': _L0_ffn_in['gamma'], 'L0_ffn_beta': _L0_ffn_in['beta'], 'L0_ffn_Wr': _L0_ffn_in['Wr'], 'L0_ffn_br': _L0_ffn_in['br'], 'L0_ffn_W1': _L0_ffn_in['W1'], 'L0_ffn_b1': _L0_ffn_in['b1'], 'L0_ffn_W2': _L0_ffn_in['W2'], 'L0_ffn_b2': _L0_ffn_in['b2'], 'L1_attn_w_qkv': _L1_attn_in['w_qkv'], 'L1_attn_w_proj': _L1_attn_in['w_proj'], 'L1_attn_b_proj': _L1_attn_in['b_proj'], 'L1_ffn_Wq_pk': _L1_ffn_in['Wq_pk'], 'L1_ffn_pk_keys': _L1_ffn_in['pk_keys'], 'L1_ffn_Wq': _L1_ffn_in['Wq'], 'L1_ffn_keys_table': _L1_ffn_in['keys_table'], 'L1_ffn_values_table': _L1_ffn_in['values_table'], 'L1_ffn_Wo': _L1_ffn_in['Wo']}

def reference(x, L0_tok_W_qry, L0_tok_W_key, L0_tok_v, L0_tok_b, L0_attn_wqv_w, L0_attn_wqv_b, L0_attn_wk, L0_attn_fanin_w, L0_attn_fanin_b, L0_ffn_gamma, L0_ffn_beta, L0_ffn_Wr, L0_ffn_br, L0_ffn_W1, L0_ffn_b1, L0_ffn_W2, L0_ffn_b2, L1_attn_w_qkv, L1_attn_w_proj, L1_attn_b_proj, L1_ffn_Wq_pk, L1_ffn_pk_keys, L1_ffn_Wq, L1_ffn_keys_table, L1_ffn_values_table, L1_ffn_Wo):
    import jax
    import jax.numpy as jnp

    def _L0_tok_ref(x, W_qry, W_key, v, b):
        import jax, jax.numpy as jnp
        import numpy as np
        WIN = 9
        N, L, C = x.shape
        n_w = L - WIN + 1
        idx = jnp.arange(n_w)[:, None] + jnp.arange(WIN)[None, :]
        x_win = x[:, idx]
        x_ctr = x[:, WIN // 2:WIN // 2 + n_w]
        key = jnp.einsum('nwsc,cu->nwsu', x_win, W_key)
        qry = jnp.einsum('nwc,cu->nwu', x_ctr, W_qry)
        score = jnp.einsum('nwsu,u->nws', jnp.tanh(qry[:, :, None, :] + key + b), v)
        weight = jax.nn.softmax(score, axis=2)
        out = jnp.einsum('nwsc,nws->nwc', x_win, weight)
        return out

    def _L0_attn_ref(x, wqv_w, wqv_b, wk, fanin_w, fanin_b):
        import jax, jax.numpy as jnp
        import numpy as np
        D_MODEL = 64
        N_HEAD = 8

        def _l1_scores(q, k):
            scale = 1.0 / np.sqrt(q.shape[-1]).astype(np.float32)
            q_sbhw = q.transpose(1, 0, 2, 3)

            def one_query(qs):
                return -jnp.sum(jnp.abs(qs[:, None, :, :] - k), axis=-1) * scale
            s = jax.lax.map(one_query, q_sbhw)
            return s.transpose(1, 0, 2, 3)
        b, t, d = x.shape
        h = N_HEAD
        v = (x @ wqv_w.T + wqv_b).reshape(b, t, 3 * h, d)
        q, vf, vb = (v[:, :, :h], v[:, :, h:2 * h], v[:, :, 2 * h:])
        k = x[:, :, None, :] * wk[None, None]
        a = _l1_scores(q, k)
        a = jnp.concatenate([a, jnp.zeros((b, 1, t, h), a.dtype)], axis=1)
        a = jax.nn.softmax(a, axis=1)[:, :t]
        bf = jnp.einsum('bsdh,bshw->bdhw', a, vf)
        bb = jnp.einsum('bdsh,bshw->bdhw', a, vb)
        o = (bf + bb).sum(axis=2).reshape(b, t, d)
        y = o * jax.nn.sigmoid(1.702 * o)
        y = y @ fanin_w.T + fanin_b
        return x + y

    def _L0_ffn_ref(x, gamma, beta, Wr, br, W1, b1, W2, b2):
        import jax, jax.numpy as jnp
        import numpy as np
        E = 8
        K = 2
        D = 64
        H = 128
        DOUT = 64
        EPS = 1e-05
        mu = jnp.mean(x, axis=-1, keepdims=True)
        var = jnp.mean(jnp.square(x - mu), axis=-1, keepdims=True)
        xn = (x - mu) * jax.lax.rsqrt(var + EPS) * gamma + beta
        logits = jnp.einsum('bsd,de->bse', xn, Wr) + br
        top_vals, top_idx = jax.lax.top_k(logits, K)
        w = jax.nn.softmax(top_vals, axis=-1)
        w_full = jnp.einsum('bsk,bske->bse', w, jax.nn.one_hot(top_idx, E, dtype=w.dtype))
        y = jnp.zeros(x.shape[:-1] + (DOUT,), x.dtype)
        for e in range(E):
            h = jax.nn.gelu(jnp.einsum('bsd,dh->bsh', xn, W1[e]) + b1[e], approximate=False)
            y_e = jnp.einsum('bsh,hd->bsd', h, W2[e]) + b2[e]
            y = y + y_e * w_full[..., e, None]
        return y

    def _L1_attn_ref(x, w_qkv, w_proj, b_proj):
        import jax, jax.numpy as jnp
        import numpy as np
        NUM_HEADS = 8
        LOCAL_WINDOW = 16
        NEG_INF = -10000000000.0
        B, N, C = x.shape
        H = NUM_HEADS
        hd = C // H
        scale = hd ** (-0.5)
        qkv = (x @ w_qkv).reshape(B, N, 3, H, hd).transpose(2, 0, 3, 1, 4)
        q, k, v = (qkv[0], qkv[1], qkv[2])
        std = jnp.std(x, axis=-1, ddof=1)
        diff = jnp.mean(jnp.abs(x[:, 1:] - x[:, :-1]), axis=-1)
        grad = jnp.concatenate([jnp.zeros((B, 1), x.dtype), diff], axis=1)
        density = (std + grad) * 0.5
        threshold = jnp.mean(density) + 0.5 * jnp.std(density, ddof=1)
        high_info = density > threshold
        pos = jnp.arange(N)
        local = jnp.abs(pos[None, :] - pos[:, None]) < LOCAL_WINDOW
        mask = jnp.where(local[None, :, :] | high_info[:, None, :], 0.0, NEG_INF)
        attn = jnp.einsum('bhid,bhjd->bhij', q, k) * scale + mask[:, None, :, :]
        attn = jax.nn.softmax(attn, axis=-1)
        out = jnp.einsum('bhij,bhjd->bhid', attn, v)
        out = out.transpose(0, 2, 1, 3).reshape(B, N, C)
        return out @ w_proj + b_proj

    def _L1_ffn_ref(x, Wq_pk, pk_keys, Wq, keys_table, values_table, Wo):
        import jax, jax.numpy as jnp
        import numpy as np
        DIM = 64
        HEADS = 8
        NUM_KEYS = 64
        NUM_KV = NUM_KEYS ** 2
        PK_TOPK = 16
        FINAL_TOPK = 16
        DIM_KEY = DIM // 2
        P = 2

        def _pk(x, Wq_pk, pk_keys):
            b, n, _ = x.shape
            q = (x @ Wq_pk).reshape(b, n, P, HEADS, DIM_KEY).transpose(2, 0, 1, 3, 4)
            sim = jnp.einsum('pbnhd,pkhd->pbnhk', q, pk_keys)
            scores, idx = jax.lax.top_k(sim, PK_TOPK)
            idx0 = idx[0]
            idx1 = idx[1] * NUM_KEYS
            index = (idx0[..., :, None] + idx1[..., None, :]).reshape(b, n, HEADS, PK_TOPK * PK_TOPK)
            score = (scores[0][..., :, None] + scores[1][..., None, :]).reshape(b, n, HEADS, PK_TOPK * PK_TOPK)
            final_scores, pk_idx = jax.lax.top_k(score, FINAL_TOPK)
            final_indices = jnp.take_along_axis(index, pk_idx, axis=-1)
            final_scores = jax.nn.softmax(final_scores, axis=-1)
            return (final_scores, final_indices)
        b, n, d = x.shape
        q = (x @ Wq).reshape(b, n, HEADS, DIM) * DIM ** (-0.5)
        kv_scores, indices = _pk(x, Wq_pk, pk_keys)
        offsets = jnp.arange(HEADS, dtype=indices.dtype) * NUM_KV
        ind = indices + offsets[None, None, :, None]
        k = jnp.einsum('bnhk,bnhkd->bnhd', kv_scores, keys_table[ind])
        v = jnp.einsum('bnhk,bnhkd->bnhd', kv_scores, values_table[ind])
        sim = jnp.einsum('bihd,bjhd->bhij', q, k)
        neg = -jnp.finfo(sim.dtype).max
        causal = jnp.tril(jnp.ones((n, n), dtype=bool))
        sim = jnp.where(causal, sim, neg)
        attn = jax.nn.softmax(sim, axis=-1)
        out = jnp.einsum('bhij,bjhd->bhid', attn, v)
        out = out.transpose(0, 2, 1, 3).reshape(b, n, HEADS * DIM)
        return out @ Wo
    h = _L0_tok_ref(x, L0_tok_W_qry, L0_tok_W_key, L0_tok_v, L0_tok_b)
    h = h + _L0_attn_ref(_layernorm(h, axis=-1), L0_attn_wqv_w, L0_attn_wqv_b, L0_attn_wk, L0_attn_fanin_w, L0_attn_fanin_b)
    h = h + _L0_ffn_ref(_layernorm(h, axis=-1), L0_ffn_gamma, L0_ffn_beta, L0_ffn_Wr, L0_ffn_br, L0_ffn_W1, L0_ffn_b1, L0_ffn_W2, L0_ffn_b2)
    h = h + _L1_attn_ref(_layernorm(h, axis=-1), L1_attn_w_qkv, L1_attn_w_proj, L1_attn_b_proj)
    h = h + _L1_ffn_ref(_layernorm(h, axis=-1), L1_ffn_Wq_pk, L1_ffn_pk_keys, L1_ffn_Wq, L1_ffn_keys_table, L1_ffn_values_table, L1_ffn_Wo)
    return h

_drawn_inputs = setup_inputs


def setup_inputs(seed=0):
    import zlib

    import numpy as np

    out = dict(_drawn_inputs(seed))
    spreads = {'L0_tok_b': (0.0, 0.8),
     'L0_attn_wqv_b': (0.0, 0.8),
     'L0_attn_wk': (0.004999999888241291, 0.6),
     'L0_attn_fanin_b': (0.0, 0.1),
     'L0_ffn_br': (0.0, 0.487),
     'L1_attn_b_proj': (0.0, 0.554)}
    factors = {'L0_attn_wqv_w': 8.0,
     'L0_attn_fanin_w': 8.0,
     'L0_ffn_gamma': 8.0,
     'L0_ffn_beta': 8.0,
     'L0_ffn_Wr': 8.0,
     'L0_ffn_W1': 5.842,
     'L0_ffn_b1': 8.0,
     'L0_ffn_W2': 5.79,
     'L0_ffn_b2': 20.205,
     'L1_attn_w_qkv': 8.0,
     'L1_attn_w_proj': 8.0,
     'L1_ffn_Wq_pk': 64.0,
     'L1_ffn_pk_keys': 64.0,
     'L1_ffn_Wq': 64.0,
     'L1_ffn_keys_table': 64.0,
     'L1_ffn_values_table': 64.0,
     'L1_ffn_Wo': 64.0}
    for name, (base, spread) in spreads.items():
        noise = np.random.default_rng([zlib.crc32(name.encode()), seed]).standard_normal(out[name].shape)
        drawn = base * np.exp(spread * noise) if base else spread * noise
        out[name] = jnp.asarray(drawn.astype(out[name].dtype))
    for name, factor in factors.items():
        out[name] = (out[name] * factor).astype(out[name].dtype)
    return out
```

```python
from contextlib import ExitStack

import numpy as np

import concourse.bass as bass
from concourse import mybir

F32 = mybir.dt.float32
U32 = mybir.dt.uint32
ALU = mybir.AluOpType
ACT = mybir.ActivationFunctionType
AX_X = mybir.AxisListType.X

N_B, L_IN, C, WIN = 8, 750, 64, 9
W = L_IN - WIN + 1
P = 106
NT = W // P
TILES = N_B * NT
HALF = W // 2
BANK = 512
assert NT * P == W


def ap(t, p0, n_p, offset, dims):
    whole = t[:]
    row = whole.ap[0][0]
    return bass.AP(whole.tensor, p0 * row + offset, [[row, n_p]] + [list(d) for d in dims])


def banks(t, n_p, cols=HALF, p0=0):
    return ap(t, p0, n_p, 0, [[BANK, 2], [1, cols]])


class Chain:

    def __init__(self, eng, sem, base=0):
        self.eng, self.sem, self.base, self.n = eng, sem, base, 0

    def __call__(self, instruction):
        self.n += 1
        instruction.then_inc(self.sem, 1)
        self.eng.wait_ge(self.sem, self.base + self.n)


def newton_rsqrt(eng, link, var, root, rstd, tmp):
    link(eng.reciprocal(rstd, root))
    link(eng.tensor_tensor(tmp, rstd, rstd, ALU.mult))
    link(eng.tensor_tensor(tmp, tmp, var, ALU.mult))
    link(eng.tensor_scalar(tmp, tmp, -0.5, 1.5, ALU.mult, ALU.add))
    link(eng.tensor_tensor(rstd, rstd, tmp, ALU.mult))


class Memory:

    def __init__(self, nc, ctx, stage):
        self.nc, self.ctx, self.stage = nc, ctx, stage

    def sb(self, name, shape, dt=F32):
        return self.ctx.enter_context(self.nc.sbuf_tensor(f"{self.stage}_{name}", shape, dt))

    def ps(self, name, shape, dt=F32):
        return self.ctx.enter_context(self.nc.psum_tensor(f"{self.stage}_{name}", shape, dt))

    def sem(self, name):
        return self.ctx.enter_context(self.nc.semaphore(f"{self.stage}_{name}"))


def local_attention(nc, H, ident, x, w_qry, w_key, v, b):
    PAIRS = N_B // 2
    CHUNK, CHUNKS = 125, L_IN // 125
    with ExitStack() as ctx:
        m = Memory(nc, ctx, "tok")
        frames = m.sb("frames", [CHUNK, CHUNKS, 2 * C])
        windows = m.sb("windows", [P, 2 * NT, WIN * C])
        wkey2 = m.sb("wkey2", [128, 128])
        wqry2 = m.sb("wqry2", [128, 128])
        v2 = m.sb("v2", [128, 2])
        b2 = m.sb("b2", [128, 1])
        xt = m.sb("xt", [128, L_IN])
        qry = m.sb("qry", [128, W])
        key = m.sb("key", [128, L_IN])
        arg = m.sb("arg", [128, WIN, W])
        soft = m.sb("soft", [P, 2 * NT, WIN])
        top = m.sb("top", [P, 2 * NT])
        total = m.sb("total", [P, 2 * NT])
        p_xt = m.ps("p_xt", [128, 2 * BANK])
        p_key = m.ps("p_key", [128, 2 * BANK])
        p_qry = m.ps("p_qry", [128, 2 * BANK])
        p_score = m.ps("p_score", [P, BANK])
        weights_in, frames_in, windows_in = m.sem("weights_in"), m.sem("frames_in"), m.sem("windows_in")
        blocks_zero, id_ready = m.sem("blocks_zero"), m.sem("id_ready")
        xt_done, xt_copied, proj_done, key_copied = m.sem("xt_done"), m.sem("xt_copied"), m.sem("proj_done"), m.sem("key_copied")
        arg_ready, tanh_done, score_done, centred = m.sem("arg_ready"), m.sem("tanh_done"), m.sem("score_done"), m.sem("centred")
        exp_done, windows_used, chain = m.sem("exp_done"), m.sem("windows_used"), m.sem("chain")
        CHAIN = 7
        block = ctx.enter_context(nc.Block())

        @block.gpsimd
        def _(pool):
            pool.memset(ident[:], 0.0).then_inc(id_ready, 1)
            pool.wait_ge(id_ready, 1)
            pool.affine_select(out=ident[:], in_=ident[:], compare_op=ALU.not_equal, fill=1.0, base=0,
                               pattern=[[-1, 128]], channel_multiplier=1).then_inc(id_ready, 1)

        @block.sync
        def _(sp):
            sp.wait_ge(blocks_zero, 3)
            for j in range(2):
                s = slice(C * j, C * j + C)
                sp.dma_start(wkey2[s, s], w_key).then_inc(weights_in, 16)
                sp.dma_start(wqry2[s, s], w_qry).then_inc(weights_in, 16)
                sp.dma_start(v2[s, j:j + 1], v.rearrange("(c a) -> c a", a=1)).then_inc(weights_in, 16)
                sp.dma_start(b2[s, :], b.rearrange("(c a) -> c a", a=1)).then_inc(weights_in, 16)
            for i in range(PAIRS):
                if i:
                    sp.wait_ge(xt_done, i)
                for j in range(2):
                    sp.dma_start(frames[:, :, C * j:C * j + C],
                                 x[2 * i + j].rearrange("(c p) d -> p c d", p=CHUNK)).then_inc(frames_in, 16)
                if i:
                    sp.wait_ge(windows_used, i)
                for j in range(2):
                    src = x[2 * i + j]
                    src = bass.AP(src.tensor, src.offset, [[C, P], [P * C, NT], [1, WIN * C]])
                    sp.dma_start(windows[:, NT * j:NT * j + NT, :], src).then_inc(windows_in, 16)

        @block.tensor
        def _(pe):
            pe.wait_ge(id_ready, 2)
            pe.wait_ge(weights_in, 8 * 16)
            with pe.Fori(0, PAIRS) as i:
                pe.wait_ge(frames_in, i * 32 + 32)
                for c in range(CHUNKS):
                    col = (c // 4) * BANK + (c % 4) * CHUNK
                    last = pe.transpose(p_xt[:, col:col + CHUNK], frames[:, c, :], ident[0:CHUNK, 0:CHUNK])
                last.then_inc(xt_done, 1)
                pe.wait_ge(xt_copied, i * 2 + 2)
                for h in range(2):
                    pe.matmul(p_key[:, h * BANK:h * BANK + L_IN // 2], wkey2[:],
                              xt[:, h * (L_IN // 2):(h + 1) * (L_IN // 2)], start=True, stop=True)
                for h in range(2):
                    a = WIN // 2 + h * HALF
                    last = pe.matmul(p_qry[:, h * BANK:h * BANK + HALF], wqry2[:], xt[:, a:a + HALF],
                                     start=True, stop=True)
                last.then_inc(proj_done, 1)
                for s in range(WIN):
                    pe.wait_ge(tanh_done, i * WIN + s + 1)
                    for t in range(NT):
                        out = ap(p_score, 0, P, t * WIN + s, [[NT * WIN, 2]])
                        last = pe.matmul(out, arg[:, s, t * P:(t + 1) * P], v2[:], start=True, stop=True)
                last.then_inc(score_done, 1)

        @block.vector
        def _(dve):
            dve.memset(wkey2[:], 0.0).then_inc(blocks_zero, 1)
            dve.memset(wqry2[:], 0.0).then_inc(blocks_zero, 1)
            dve.memset(v2[:], 0.0).then_inc(blocks_zero, 1)
            with dve.Fori(0, PAIRS) as i:
                link = Chain(dve, chain, i * CHAIN)
                dve.wait_ge(xt_done, i + 1)
                for h, n in ((0, 4), (1, 2)):
                    dve.tensor_copy(xt[:, 4 * h * CHUNK:4 * h * CHUNK + n * CHUNK],
                                    p_xt[:, h * BANK:h * BANK + n * CHUNK]).then_inc(xt_copied, 1)
                dve.wait_ge(proj_done, i + 1)
                link(dve.tensor_copy(key[:].rearrange("p (h n) -> p h n", h=2), banks(p_key, 128, L_IN // 2)))
                link(dve.tensor_copy(qry[:].rearrange("p (h n) -> p h n", h=2), banks(p_qry, 128)))
                for s in range(WIN):
                    dve.tensor_tensor(arg[:, s, :], qry[:], key[:, s:s + W], ALU.add).then_inc(arg_ready, 1)
                dve.wait_ge(score_done, i + 1)
                score = p_score[:, 0:2 * NT * WIN].rearrange("p (t s) -> p t s", s=WIN)
                link(dve.tensor_reduce(top[:], score, AX_X, ALU.max))
                dve.tensor_tensor(soft[:], score, top[:].unsqueeze(2).to_broadcast([P, 2 * NT, WIN]),
                                  ALU.subtract).then_inc(centred, 1)
                dve.wait_ge(exp_done, i + 1)
                link(dve.tensor_reduce(total[:], soft[:], AX_X, ALU.add))
                link(dve.reciprocal(total[:], total[:]))
                link(dve.tensor_tensor(soft[:], soft[:], total[:].unsqueeze(2).to_broadcast([P, 2 * NT, WIN]),
                                       ALU.mult))
                dve.wait_ge(windows_in, i * 32 + 32)
                rows = windows[:].rearrange("p t (s c) -> p (t s) c", c=C)
                link(dve.tensor_tensor(rows, rows, soft[:].rearrange("p t s -> p (t s)").unsqueeze(2)
                                       .to_broadcast([P, 2 * NT * WIN, C]), ALU.mult))
                dve.tensor_reduce(H[:, bass.ds(i * 2 * NT, 2 * NT), :],
                                  windows[:].rearrange("p t (s c) -> p t c s", c=C), AX_X,
                                  ALU.add).then_inc(windows_used, 1)
                assert link.n == CHAIN

        @block.scalar
        def _(act):
            act.wait_ge(weights_in, 8 * 16)
            with act.Fori(0, PAIRS) as i:
                for s in range(WIN):
                    act.wait_ge(arg_ready, i * WIN + s + 1)
                    act.activation(arg[:, s, :], arg[:, s, :], ACT.Tanh, bias=b2[:, 0:1]).then_inc(tanh_done, 1)
                act.wait_ge(centred, i + 1)
                act.activation(soft[:], soft[:], ACT.Exp).then_inc(exp_done, 1)

HEADS = 8
GROUPS = 4
TILE_PAIRS = P // 2
ROUNDS = -(-TILE_PAIRS // GROUPS)
PAIR_LIST = [(r, g) for r in range(ROUNDS) for g in range(GROUPS) if GROUPS * r + g < TILE_PAIRS]
VECTOR_FROM = {0: 0, 1: 0, 2: 10, 3: ROUNDS}


def on_vector(r, g):
    return r >= VECTOR_FROM[g]


def group_rows(g):
    return 2 * len([1 for r, gg in PAIR_LIST if gg == g])


V_PAIRS = sum(on_vector(r, g) for r, g in PAIR_LIST)
A_PAIRS = TILE_PAIRS - V_PAIRS
V_RING, A_RING = 6, 7
assert NT * V_PAIRS % V_RING == 0 and NT * A_PAIRS % A_RING == 0
ROUNDS_HEAD = NT * ROUNDS


def tiles_upto(t, r, vector):
    per = V_PAIRS if vector else A_PAIRS
    return per * t + sum(on_vector(rr, g) == vector for rr, g in PAIR_LIST if rr <= r)


def round_of(n, vector):
    per = V_PAIRS if vector else A_PAIRS
    back, n = divmod(n, per * NT)
    own = [r for r, g in PAIR_LIST if on_vector(r, g) == vector]
    return back * ROUNDS_HEAD + (n // per) * ROUNDS + own[n % per]


def permuted(dst, src, n_p, to_rows, tiles, dst_step, src_step, p0=0):
    out = []
    for g in range(GROUPS):
        n = len([1 for r, gg in PAIR_LIST if gg == g])
        for r0, k in ((0, ROUNDS - 1), (ROUNDS - 1, n - ROUNDS + 1)):
            if k <= 0:
                continue
            nat, row = 2 * GROUPS * r0 + 2 * g, 32 * g + 2 * r0
            dims = lambda step, s: [[step, tiles], [s, k], [1, 2]]
            natural, rows = (nat, 2 * GROUPS), (row, 2)
            (d0, ds), (s0, ss) = (rows, natural) if to_rows else (natural, rows)
            out.append((ap(dst, p0, n_p, d0, dims(dst_step, ds)), ap(src, p0, n_p, s0, dims(src_step, ss))))
    return out


def l1_attention(nc, H, ident, wqv_w, wqv_b, wk, fanin_w, fanin_b, batches=N_B):
    FEATURES = 3 * HEADS * C
    CH = FEATURES // 128
    QCUT = 372
    with ExitStack() as ctx:
        m = Memory(nc, ctx, "l1")
        sel1 = m.sb("sel1", [128, ROUNDS, 32])
        sel2 = m.sb("sel2", [128, ROUNDS, 32])
        rows_mask = m.sb("rows_mask", [128, 96])
        exp_mask_row = m.sb("exp_mask_row", [1, 128])
        exp_mask = m.sb("exp_mask", [128, 1])
        to_natural = m.sb("to_natural", [128, P])
        wqv_in = m.sb("wqv_in", [128, CH, C])
        fanin_in = m.sb("fanin_in", [C, C])
        wq2 = m.sb("wq2", [C + 1, HEADS, 2 * C])
        wqsum = m.sb("wqsum", [C + 1, HEADS])
        wv = m.sb("wv", [C + 1, 2 * HEADS * C])
        wfan = m.sb("wfan", [C + 1, C])
        wkc = m.sb("wkc", [128, HEADS])
        xn = m.sb("xn", [P, NT, C])
        stat = m.sb("stat", [P, 5, NT])
        xdup = m.sb("xdup", [P, NT, 2, C])
        xt2 = m.sb("xt2", [128, W])
        xt1 = m.sb("xt1", [C + 1, W])
        xtp = m.sb("xtp", [C + 1, NT, 128])
        keys = m.sb("keys", [128, HEADS, W])
        qcol = m.sb("qcol", [128, HEADS, NT * TILE_PAIRS])
        qbias = m.sb("qbias", [128, NT, HEADS])
        vf = m.sb("vf", [128, NT, HEADS, C + 1])
        vb = m.sb("vb", [P, NT, HEADS, C])
        wkneg = m.sb("wkneg", [128, 96])
        diff_v = m.sb("diff_v", [128, V_RING, W])
        diff_a = m.sb("diff_a", [128, A_RING, W])
        expd = m.sb("expd", [128, NT, W])
        expt = m.sb("expt", [P, NT, NT, 128])
        rz = m.sb("rz", [P, NT])
        vbz = m.sb("vbz", [P, NT, C])
        scaled = m.sb("scaled", [P, NT, C])
        o_fwd = m.sb("o_fwd", [P, NT, C])
        o_back = m.sb("o_back", [128, NT, C])
        gate = m.sb("gate", [P, NT, C])
        yt = m.sb("yt", [C + 1, W])
        p_dist = m.ps("p_dist", [128, 4 * BANK])
        p_fwd = m.ps("p_fwd", [128, BANK])
        p_back = m.ps("p_back", [128, BANK])
        p_turn = m.ps("p_turn", [128, 2 * BANK])
        names = ("loaded consts ready_w turned_w sums_w mask_turned xn_ready var_ready root_ready xt_done "
                 "xt_ready q_done q_low q_high v_done v_copied_v v_copied_a qsum_done batch_ready keys_ready "
                 "wkneg_ready correction_done tiles_v tiles_a rounds exps posts turned_out vbz_ready back_done "
                 "back_added perm_done o_ready gate_exp y_ready yt_done yt_ready fan_done "
                 "chain_w chain_b chain_h chain_e id_ready").split()
        s = {n: m.sem(n) for n in names}
        EXP_CREDIT = 2
        block = ctx.enter_context(nc.Block())

        @block.sync
        def _(sp):
            sp.dma_start(wqv_in[:], wqv_w.rearrange("(c p) d -> p c d", p=128)).then_inc(s["loaded"], 16)
            sp.dma_start(fanin_in[:], fanin_w).then_inc(s["loaded"], 16)
            for j in range(2):
                sp.dma_start(wkc[C * j:C * j + C, :], wk.rearrange("h c -> c h"), allow_slow_non_contiguous=True).then_inc(s["loaded"], 16)
                sp.dma_start(wq2[C:C + 1, :, C * j:C * j + C],
                             wqv_b[0:HEADS * C].rearrange("(a h c) -> a h c", a=1, h=HEADS)).then_inc(s["loaded"], 16)
            sp.dma_start(wv[C:C + 1, :], wqv_b[HEADS * C:FEATURES].rearrange("(a n) -> a n", a=1)).then_inc(s["loaded"], 16)
            sp.dma_start(wfan[C:C + 1, :], fanin_b.rearrange("(a n) -> a n", a=1)).then_inc(s["loaded"], 16)

        LOADED = 8 * 16

        @block.tensor
        def _(pe):
            pe.wait_ge(s["loaded"], LOADED)
            for c in range(CH):
                col = (c // 4) * BANK + (c % 4) * 128
                pe.transpose(p_dist[0:C, col:col + 128], wqv_in[:, c, :], ident[:])
            pe.transpose(p_turn[0:C, 0:C], fanin_in[:], ident[0:C, 0:C])
            pe.wait_ge(s["consts"], 1)
            pe.matmul(p_back[:, 0:1], exp_mask_row[:], ident[0:1, 0:1], start=True, stop=True)
            pe.matmul(p_fwd[:, 0:1], xtp[C:C + 1, 0, :], xt1[C:C + 1, 0:1], start=True, stop=True).then_inc(s["turned_w"], 1)
            pe.sem_inc(s["rounds"], ROUNDS_HEAD)
            pe.sem_inc(s["posts"], NT)
            pe.sem_inc(s["correction_done"], 1)
            pe.wait_ge(s["ready_w"], 1)

            def distances(it, t):
                if t == 0:
                    pe.wait_ge(s["exps"], it * NT + EXP_CREDIT)
                    pe.wait_ge(s["wkneg_ready"], it + 1)
                elif t >= 2:
                    pe.wait_ge(s["exps"], it * NT + t - 1 + EXP_CREDIT)
                base = (t % 2) * 2 * BANK
                for h in range(2):
                    for g in range(3):
                        last = pe.matmul(p_dist[32 * g:32 * g + 32, base + h * BANK:base + h * BANK + HALF],
                                         wkneg[:, 32 * g:32 * g + 32], xt2[:, h * HALF:(h + 1) * HALF],
                                         start=True, stop=False, skip_group_check=True)
                last.then_inc(s["correction_done"], 1)
                nv, na = tiles_upto(t, -1, True), tiles_upto(t, -1, False)
                for r in range(ROUNDS):
                    gs = [g for rr, g in PAIR_LIST if rr == r]
                    slot = {}
                    for g in gs:
                        if on_vector(r, g):
                            slot[g] = diff_v[:, nv % V_RING, :]
                            nv += 1
                        else:
                            slot[g] = diff_a[:, na % A_RING, :]
                            na += 1
                    pe.wait_ge(s["tiles_v"], it * (NT * V_PAIRS) + nv)
                    if any(not on_vector(r, g) for g in gs):
                        pe.wait_ge(s["tiles_a"], it * (NT * A_PAIRS) + na)
                    for h in range(2):
                        for g in gs:
                            sel = sel2 if on_vector(r, g) else sel1
                            last = pe.matmul(p_dist[32 * g:32 * g + 32, base + h * BANK:base + h * BANK + HALF],
                                             sel[:, r, :], slot[g][:, h * HALF:(h + 1) * HALF],
                                             start=(g == 3 and r == 0), stop=(r == max(rr for rr, gg in PAIR_LIST if gg == g)),
                                             skip_group_check=True)
                    last.then_inc(s["rounds"], 1)

            def forward(it, h, t):
                pe.wait_ge(s["exps"], it * NT + t + 1 + EXP_CREDIT)
                pe.wait_ge(s["turned_out"], it * (2 * NT) + 2 * t + 2)
                for k in range(NT):
                    pe.matmul(p_fwd[0:P, k * (C + 1):(k + 1) * (C + 1)], expd[:, t, k * P:(k + 1) * P],
                              vf[:, t, h, :], start=(t == 0 and k == 0), stop=(t == NT - 1), skip_group_check=True)
                for k in range(NT):
                    col = (k // 4) * BANK + (k % 4) * 128
                    last = pe.transpose(p_turn[0:P, col:col + 128], expd[:, t, k * P:(k + 1) * P], ident[:])
                last.then_inc(s["posts"], 1)

            def backward(it):
                pe.wait_ge(s["vbz_ready"], it + 1)
                pe.wait_ge(s["turned_out"], it * (2 * NT) + 2 * NT + 2)
                for t in range(NT):
                    for k in range(NT):
                        last = pe.matmul(p_back[:, t * C:(t + 1) * C], expt[:, k, t, :], vbz[:, k, :],
                                         start=(k == 0), stop=(k == NT - 1))
                last.then_inc(s["back_done"], 1)

            def head(it, h, first):
                for t in range(NT):
                    distances(it, t)
                    if t == 0 and not first:
                        forward(it - 1, h - 1, NT - 1)
                    if t == 1 and not first:
                        backward(it - 1)
                    if t >= 1:
                        forward(it, h, t - 1)

            with pe.Fori(0, batches) as b:
                pe.wait_ge(s["xn_ready"], b + 1)
                for t in range(NT):
                    col = (t // 4) * BANK + (t % 4) * P
                    last = pe.transpose(p_dist[:, col:col + P], xdup[:, t, :, :].rearrange("p a c -> p (a c)"),
                                        ident[0:P, 0:P])
                last.then_inc(s["xt_done"], 1)
                pe.wait_ge(s["xt_ready"], b + 1)
                for h in range(HEADS):
                    if h >= 2:
                        pe.wait_ge(s["q_low"], b * HEADS + h - 1)
                        pe.wait_ge(s["q_high"], b * HEADS + h - 1)
                    base = (h % 2) * 2 * BANK
                    pe.matmul(p_dist[:, base:base + QCUT], wq2[:, h, :], xt1[:, 0:QCUT], start=True, stop=True)
                    pe.matmul(p_dist[:, base + BANK:base + BANK + W - QCUT], wq2[:, h, :], xt1[:, QCUT:W],
                              start=True, stop=True).then_inc(s["q_done"], 1)
                for t in range(NT):
                    last = pe.matmul(p_fwd[:, t * HEADS:(t + 1) * HEADS], xtp[:, t, :], wqsum[:], start=True, stop=True)
                last.then_inc(s["qsum_done"], 1)
                pe.wait_ge(s["q_low"], b * HEADS + HEADS)
                pe.wait_ge(s["q_high"], b * HEADS + HEADS)
                for t in range(NT):
                    if t >= 2:
                        pe.wait_ge(s["v_copied_a"], b * NT + t - 1)
                        pe.wait_ge(s["v_copied_v"], b * NT + t - 1)
                    base = (t % 2) * 2 * BANK
                    pe.matmul(p_dist[:, base:base + BANK], xtp[:, t, :], wv[:, 0:HEADS * C], start=True, stop=True)
                    pe.matmul(p_dist[0:P, base + BANK:base + 2 * BANK], xt1[:, t * P:(t + 1) * P],
                              wv[:, HEADS * C:2 * HEADS * C], start=True, stop=True).then_inc(s["v_done"], 1)
                pe.wait_ge(s["v_copied_a"], b * NT + NT)
                pe.wait_ge(s["v_copied_v"], b * NT + NT)
                pe.wait_ge(s["batch_ready"], b + 1)
                head(b * HEADS, 0, True)
                with pe.Fori(1, HEADS) as h:
                    head(b * HEADS + h, h, False)
                forward(b * HEADS + HEADS - 1, HEADS - 1, NT - 1)
                backward(b * HEADS + HEADS - 1)
                pe.wait_ge(s["back_added"], b * HEADS + HEADS)
                pe.matmul(p_fwd[0:P, 0:NT * C], to_natural[:], o_back[:].rearrange("p t c -> p (t c)"),
                          start=True, stop=True).then_inc(s["perm_done"], 1)
                pe.wait_ge(s["y_ready"], b + 1)
                turn_tiles(pe, p_turn, gate, ident).then_inc(s["yt_done"], 1)
                pe.wait_ge(s["yt_ready"], b + 1)
                for t in range(NT):
                    last = pe.matmul(p_back[0:P, t * C:(t + 1) * C], yt[:, t * P:(t + 1) * P], wfan[:], start=True, stop=True)
                last.then_inc(s["fan_done"], 1)

        @block.vector
        def _(dve):
            link = Chain(dve, s["chain_w"])
            link(dve.memset(sel1[:], 0.0))
            for t_, v_ in ((sel1, 1.0), (sel2, 2.0)):
                if t_ is sel2:
                    link(dve.memset(sel2[:], 0.0))
                for hf in range(2):
                    link(dve.memset(ap(t_, C * hf, C, hf, [[34, ROUNDS]]), v_))
            link(dve.memset(rows_mask[:], 0.0))
            link(dve.memset(wkneg[:], 0.0))
            link(dve.memset(exp_mask_row[:], 0.0))
            for g in range(3):
                a = 32 * g + 2 * VECTOR_FROM[g]
                e = 32 * g + group_rows(g)
                link(dve.memset(rows_mask[:, a:e], -1.0))
                link(dve.memset(exp_mask_row[:, a:e], -0.125))
            link(dve.memset(to_natural[:], 0.0))
            for dst, src in permuted(to_natural, ident, 128, False, 1, 0, 0):
                link(dve.tensor_copy(dst, src))
            link(dve.memset(xt1[C:C + 1, :], 1.0))
            link(dve.memset(yt[C:C + 1, :], 1.0))
            link(dve.memset(xtp[:], 0.0))
            ones = permuted(xtp, xt1, 1, True, NT, 128, P, p0=C)
            for dst, src in ones:
                link(dve.tensor_copy(dst, src))
            dve.nop().then_inc(s["consts"], 1)
            dve.wait_ge(s["turned_w"], 1)
            w3 = [ap(p_dist, 0, C, k * BANK, [[C, HEADS], [1, C]]) for k in range(3)]
            for j in range(2):
                link(dve.tensor_copy(wq2[0:C, :, C * j:C * j + C], w3[0]))
            for k in range(2):
                link(dve.tensor_copy(wv[0:C, k * BANK:(k + 1) * BANK], p_dist[0:C, (k + 1) * BANK:(k + 2) * BANK]))
            link(dve.tensor_copy(wfan[0:C, :], p_turn[0:C, 0:C]))
            link(dve.tensor_copy(exp_mask[:], p_back[:, 0:1]))
            link(dve.tensor_copy(ap(vf, 0, 128, C, [[C + 1, NT * HEADS]]), p_fwd[:, 0:1].to_broadcast([128, NT * HEADS])))
            dve.wait_ge(s["loaded"], LOADED)
            link(dve.tensor_reduce(wqsum[:], wq2[:, :, 0:C], AX_X, ALU.add))
            dve.nop().then_inc(s["ready_w"], 1)
            dve.sem_inc(s["turned_out"], 2)

            def turned_copy(it, t):
                dve.wait_ge(s["posts"], it * NT + t + 1 + NT)
                for k0, n in ((0, 4), (4, 3)):
                    dve.tensor_copy(expt[:, k0:k0 + n, t, :],
                                    ap(p_turn, 0, P, (k0 // 4) * BANK, [[128, n], [1, 128]])).then_inc(s["turned_out"], 1)

            def normalise(it, h, link):
                z = ap(p_fwd, 0, P, C, [[C + 1, NT]])
                link(dve.tensor_scalar(rz[:], z, 1.0, None, ALU.add))
                link(dve.reciprocal(rz[:], rz[:]))
                wide = rz[:].unsqueeze(2).to_broadcast([P, NT, C])
                link(dve.tensor_tensor(scaled[:], ap(p_fwd, 0, P, 0, [[C + 1, NT], [1, C]]), wide, ALU.mult))
                link(dve.tensor_tensor(o_fwd[:], o_fwd[:], scaled[:], ALU.add))
                dve.tensor_tensor(vbz[:], vb[:, :, h, :], wide, ALU.mult).then_inc(s["vbz_ready"], 1)

            def add_back(it):
                dve.wait_ge(s["back_done"], it + 1)
                dve.tensor_tensor(o_back[:], o_back[:], ap(p_back, 0, 128, 0, [[C, NT], [1, C]]),
                                  ALU.add).then_inc(s["back_added"], 1)

            HEAD_CHAIN = 4

            def head(it, h, first):
                dve.wait_ge(s["correction_done"], it * NT + 1)
                dve.tensor_scalar(wkneg[0:C, :], rows_mask[0:C, :], wkc[0:C, bass.ds(h, 1)], None,
                                  ALU.mult).then_inc(s["wkneg_ready"], 1)
                for t in range(NT):
                    n = tiles_upto(t, -1, True)
                    for r in range(ROUNDS):
                        gs = [g for rr, g in PAIR_LIST if rr == r and on_vector(rr, g)]
                        dve.wait_ge(s["rounds"], it * ROUNDS_HEAD + round_of(n + len(gs) - 1 - V_RING, True) + 1 + ROUNDS_HEAD)
                        for g in gs:
                            pair = TILE_PAIRS * t + GROUPS * r + g
                            dve.tensor_scalar(diff_v[:, n % V_RING, :], keys[:, h, :], qcol[:, h, pair:pair + 1],
                                              0.0, ALU.subtract, ALU.max).then_inc(s["tiles_v"], 1)
                            n += 1
                        if r == 4:
                            if t == 0 and not first:
                                turned_copy(it - 1, NT - 2)
                            if t == 1 and not first:
                                turned_copy(it - 1, NT - 1)
                                normalise(it - 1, h - 1, Chain(dve, s["chain_h"], (it - 1) * HEAD_CHAIN))
                            if t == 2 and not first:
                                add_back(it - 1)
                            if t >= 2:
                                turned_copy(it, t - 2)

            BATCH_CHAIN = 32
            END_CHAIN = 6
            with dve.Fori(0, batches) as b:
                link = Chain(dve, s["chain_b"], b * BATCH_CHAIN)
                hb = H[:, bass.ds(b * NT, NT), :]
                mean, var, root, rstd, tmp = (stat[:, k, :] for k in range(5))
                wide = [P, NT, C]
                link(dve.tensor_reduce(mean, hb, AX_X, ALU.add))
                link(dve.tensor_scalar(mean, mean, 1.0 / C, None, ALU.mult))
                link(dve.tensor_tensor(xn[:], hb, mean.unsqueeze(2).to_broadcast(wide), ALU.subtract))
                link(dve.tensor_tensor(gate[:], xn[:], xn[:], ALU.mult))
                link(dve.tensor_reduce(var, gate[:], AX_X, ALU.add))
                dve.tensor_scalar(var, var, 1.0 / C, 1e-5, ALU.mult, ALU.add).then_inc(s["var_ready"], 1)
                dve.wait_ge(s["root_ready"], b + 1)
                newton_rsqrt(dve, link, var, root, rstd, tmp)
                link(dve.tensor_tensor(xn[:], xn[:], rstd.unsqueeze(2).to_broadcast(wide), ALU.mult))
                for j in range(2):
                    last = dve.tensor_copy(xdup[:, :, j, :], xn[:])
                    if j == 0:
                        link(last)
                last.then_inc(s["xn_ready"], 1)
                dve.wait_ge(s["xt_done"], b + 1)
                for k, (c0, n) in enumerate(((0, 4 * P), (4 * P, 3 * P))):
                    link(dve.tensor_copy(xt2[:, c0:c0 + n], p_dist[:, k * BANK:k * BANK + n]))
                    link(dve.tensor_copy(xt1[0:C, c0:c0 + n], p_dist[0:C, k * BANK:k * BANK + n]))
                for dst, src in permuted(xtp, xt1, C, True, NT, 128, P):
                    link(dve.tensor_copy(dst, src))
                dve.nop().then_inc(s["xt_ready"], 1)
                for h in range(HEADS):
                    dve.wait_ge(s["q_done"], b * HEADS + h + 1)
                    base = (h % 2) * 2 * BANK
                    link(dve.tensor_copy(qcol[C:128, h, 0:QCUT // 2], ap(p_dist, C, C, base + 1, [[2, QCUT // 2]])))
                    dve.tensor_copy(qcol[C:128, h, QCUT // 2:HALF],
                                    ap(p_dist, C, C, base + BANK + 1, [[2, HALF - QCUT // 2]])).then_inc(s["q_high"], 1)
                dve.wait_ge(s["qsum_done"], b + 1)
                link(dve.tensor_scalar(qbias[:].rearrange("p t h -> p (t h)"), p_fwd[:, 0:NT * HEADS], exp_mask[:, 0:1],
                                       None, ALU.mult))
                for t in range(NT):
                    dve.wait_ge(s["v_done"], b * NT + t + 1)
                    base = (t % 2) * 2 * BANK + BANK
                    dve.tensor_copy(vb[:, t, :, :].rearrange("p h c -> p (h c)"), p_dist[0:P, base:base + BANK])\
                       .then_inc(s["v_copied_v"], 1)
                link(dve.memset(o_fwd[:], 0.0))
                link(dve.memset(o_back[:], 0.0))
                for h in range(HEADS):
                    dve.tensor_scalar(keys[:, h, :], xt2[:], wkc[:, h:h + 1], None, ALU.mult).then_inc(s["keys_ready"], 1)
                dve.wait_ge(s["keys_ready"], b * HEADS + HEADS)
                dve.wait_ge(s["q_low"], b * HEADS + HEADS)
                dve.nop().then_inc(s["batch_ready"], 1)
                dve.wait_ge(s["q_high"], b * HEADS + HEADS)
                assert link.n == BATCH_CHAIN, link.n

                head(b * HEADS, 0, True)
                with dve.Fori(1, HEADS) as h:
                    head(b * HEADS + h, h, False)
                it = b * HEADS + HEADS - 1
                turned_copy(it, NT - 2)
                turned_copy(it, NT - 1)
                normalise(it, HEADS - 1, Chain(dve, s["chain_h"], it * HEAD_CHAIN))
                add_back(it)

                link = Chain(dve, s["chain_e"], b * END_CHAIN)
                dve.wait_ge(s["perm_done"], b + 1)
                dve.tensor_tensor(o_fwd[:], o_fwd[:], ap(p_fwd, 0, P, 0, [[C, NT], [1, C]]), ALU.add).then_inc(s["o_ready"], 1)
                dve.wait_ge(s["gate_exp"], b + 1)
                link(dve.tensor_scalar(gate[:], gate[:], 1.0, None, ALU.add))
                link(dve.reciprocal(gate[:], gate[:]))
                dve.tensor_tensor(gate[:], gate[:], o_fwd[:], ALU.mult).then_inc(s["y_ready"], 1)
                dve.wait_ge(s["yt_done"], b + 1)
                link(dve.tensor_copy(yt[0:C, 0:4 * P], p_turn[0:C, 0:4 * P]))
                link(dve.tensor_copy(yt[0:C, 4 * P:W], p_turn[0:C, BANK:BANK + 3 * P]))
                dve.nop().then_inc(s["yt_ready"], 1)
                dve.wait_ge(s["fan_done"], b + 1)
                link(dve.tensor_tensor(xn[:], xn[:], ap(p_back, 0, P, 0, [[C, NT], [1, C]]), ALU.add))
                link(dve.tensor_tensor(hb, hb, xn[:], ALU.add))
                assert link.n == END_CHAIN, link.n

        @block.scalar
        def _(act):
            act.sem_inc(s["exps"], EXP_CREDIT)

            def exponentials(it, h, t):
                act.wait_ge(s["rounds"], it * ROUNDS_HEAD + ROUNDS * (t + 1) + ROUNDS_HEAD)
                act.wait_ge(s["posts"], it * NT + t + 1)
                act.activation(expd[:, t, :].rearrange("p (h n) -> p h n", h=2),
                               ap(p_dist, 0, 128, (t % 2) * 2 * BANK, [[BANK, 2], [1, HALF]]), ACT.Exp,
                               bias=qbias[:, t, bass.ds(h, 1)], scale=-0.125).then_inc(s["exps"], 1)

            def head(it, h, first):
                for t in range(NT):
                    n = tiles_upto(t, -1, False)
                    for r in range(ROUNDS):
                        gs = [g for rr, g in PAIR_LIST if rr == r and not on_vector(rr, g)]
                        if gs:
                            act.wait_ge(s["rounds"], it * ROUNDS_HEAD + round_of(n + len(gs) - 1 - A_RING, False) + 1 + ROUNDS_HEAD)
                        for g in gs:
                            pair = TILE_PAIRS * t + GROUPS * r + g
                            act.activation(diff_a[:, n % A_RING, :], keys[:, h, :], ACT.Abs,
                                           bias=qcol[:, h, pair:pair + 1], scale=-1.0).then_inc(s["tiles_a"], 1)
                            n += 1
                        if r == 2 and (t or not first):
                            if t:
                                exponentials(it, h, t - 1)
                            else:
                                exponentials(it - 1, h - 1, NT - 1)

            with act.Fori(0, batches) as b:
                act.wait_ge(s["var_ready"], b + 1)
                act.activation(stat[:, 2, :], stat[:, 1, :], ACT.Sqrt).then_inc(s["root_ready"], 1)
                for h in range(HEADS):
                    act.wait_ge(s["q_done"], b * HEADS + h + 1)
                    base = (h % 2) * 2 * BANK
                    act.activation(qcol[0:C, h, 0:QCUT // 2], ap(p_dist, 0, C, base, [[2, QCUT // 2]]), ACT.Copy)
                    act.activation(qcol[0:C, h, QCUT // 2:HALF], ap(p_dist, 0, C, base + BANK, [[2, HALF - QCUT // 2]]),
                                   ACT.Copy).then_inc(s["q_low"], 1)
                for t in range(NT):
                    act.wait_ge(s["v_done"], b * NT + t + 1)
                    base = (t % 2) * 2 * BANK
                    act.activation(vf[:, t, :, 0:C], ap(p_dist, 0, 128, base, [[C, HEADS], [1, C]]), ACT.Copy)\
                       .then_inc(s["v_copied_a"], 1)
                act.wait_ge(s["batch_ready"], b + 1)
                head(b * HEADS, 0, True)
                with act.Fori(1, HEADS) as h:
                    head(b * HEADS + h, h, False)
                exponentials(b * HEADS + HEADS - 1, HEADS - 1, NT - 1)
                act.wait_ge(s["o_ready"], b + 1)
                act.activation(gate[:], o_fwd[:], ACT.Exp, scale=-1.702).then_inc(s["gate_exp"], 1)

def norm_tiles(dve, link, hb, xn, square, stat, var_ready, root_ready, root_value):
    mean, var, root, rstd, tmp = (stat[:, k, :] for k in range(5))
    wide = list(hb.shape)
    link(dve.tensor_reduce(mean, hb, AX_X, ALU.add))
    link(dve.tensor_scalar(mean, mean, 1.0 / C, None, ALU.mult))
    link(dve.tensor_tensor(xn, hb, mean.unsqueeze(2).to_broadcast(wide), ALU.subtract))
    link(dve.tensor_tensor(square, xn, xn, ALU.mult))
    link(dve.tensor_reduce(var, square, AX_X, ALU.add))
    dve.tensor_scalar(var, var, 1.0 / C, 1e-5, ALU.mult, ALU.add).then_inc(var_ready, 1)
    dve.wait_ge(root_ready, root_value)
    newton_rsqrt(dve, link, var, root, rstd, tmp)
    link(dve.tensor_tensor(xn, xn, rstd.unsqueeze(2).to_broadcast(wide), ALU.mult))


NORM_CHAIN = 11


def turn_tiles(pe, dst, src, ident):
    for t in range(NT):
        col = (t // 4) * BANK + (t % 4) * P
        if t == 0:
            pe.matmul(dst[0:C, col:col + P], src[:, t, :], ident[0:P, 0:P], start=True, stop=True)
        else:
            last = pe.transpose(dst[0:C, col:col + P], src[:, t, :], ident[0:P, 0:P])
    return last


def expert_ffn(nc, H, ident, gamma, beta, w_r, b_r, w_1, b_1, w_2, b_2, batches=N_B):
    E, HID = 8, 128
    with ExitStack() as ctx:
        m = Memory(nc, ctx, "moe")
        gb = m.sb("gb", [C, 2])
        wr = m.sb("wr", [C + 1, E])
        w1 = m.sb("w1", [C, E, HID])
        b1 = m.sb("b1", [HID, E])
        w2 = m.sb("w2", [HID, E, C])
        b2 = m.sb("b2", [1, E * C])
        ones = m.sb("ones", [1, P])
        expert_ids = m.sb("expert_ids", [P, NT, E])
        ids_int = m.sb("ids_int", [P, NT, E], mybir.dt.int32)
        xn = m.sb("xn", [P, NT, C])
        square = m.sb("square", [P, NT, C])
        stat = m.sb("stat", [P, 5, NT])
        xt = m.sb("xt", [C + 1, W])
        logits = m.sb("logits", [P, NT, E])
        best = m.sb("best", [P, NT, 8])
        best_at = m.sb("best_at", [P, NT, 8], U32)
        pause = m.sb("pause", [P, 2])
        best_id = m.sb("best_id", [P, NT, 8])
        pw = m.sb("pw", [P, 4, NT])
        weight = m.sb("weight", [P, NT, E])
        weight2 = m.sb("weight2", [P, NT, E])
        hidden = m.sb("hidden", [HID, E, W])
        weighted = m.sb("weighted", [P, 2, E * C])
        y = m.sb("y", [P, NT, C])
        p_t = m.ps("p_t", [C, 2 * BANK])
        p_h = m.ps("p_h", [HID, 4 * BANK])
        p_y = m.ps("p_y", [P, 2 * BANK])
        names = ("loaded ids_ready consts var_ready root_ready xn_ready xt_done xt_ready logits_done h_done gelu_done "
                 "y_done y_read pair_diff pair_exp chain_c chain_b").split()
        s = {n: m.sem(n) for n in names}
        block = ctx.enter_context(nc.Block())
        LOADED = 8 * 16

        @block.sync
        def _(sp):
            one = lambda v: v.rearrange("(a n) -> a n", a=1)
            col = lambda v: v.rearrange("(n a) -> n a", a=1)
            sp.dma_start(gb[:, 0:1], col(gamma)).then_inc(s["loaded"], 16)
            sp.dma_start(gb[:, 1:2], col(beta)).then_inc(s["loaded"], 16)
            sp.dma_start(wr[0:C, :], w_r).then_inc(s["loaded"], 16)
            sp.dma_start(wr[C:C + 1, :], one(b_r)).then_inc(s["loaded"], 16)
            sp.dma_start(w1[:], w_1.rearrange("e d h -> d e h")).then_inc(s["loaded"], 16)
            sp.dma_start(b1[:], b_1.rearrange("e h -> h e"), allow_slow_non_contiguous=True).then_inc(s["loaded"], 16)
            sp.dma_start(w2[:], w_2.rearrange("e h d -> h e d")).then_inc(s["loaded"], 16)
            sp.dma_start(b2[:], b_2.rearrange("(a e) d -> a (e d)", a=1)).then_inc(s["loaded"], 16)

        @block.gpsimd
        def _(pool):
            pool.iota(ids_int[:], [[0, NT], [1, E]], base=0, channel_multiplier=0).then_inc(s["ids_ready"], 1)

        @block.tensor
        def _(pe):
            pe.wait_ge(s["loaded"], LOADED)
            pe.wait_ge(s["consts"], 1)
            with pe.Fori(0, batches) as b:
                pe.wait_ge(s["xn_ready"], b + 1)
                turn_tiles(pe, p_t, xn, ident).then_inc(s["xt_done"], 1)
                pe.wait_ge(s["xt_ready"], b + 1)
                for t in range(NT):
                    last = pe.matmul(p_y[:, t * E:(t + 1) * E], xt[:, t * P:(t + 1) * P], wr[:], start=True, stop=True)
                last.then_inc(s["logits_done"], 1)
                for e in range(E):
                    if e >= 2:
                        pe.wait_ge(s["gelu_done"], b * E + e - 1)
                    for h in range(2):
                        a = (e % 2) * 2 * BANK + h * BANK
                        last = pe.matmul(p_h[:, a:a + HALF], w1[:, e, :], xt[0:C, h * HALF:(h + 1) * HALF],
                                         start=True, stop=True)
                    last.then_inc(s["h_done"], 1)
                pe.wait_ge(s["gelu_done"], b * E + E)
                for t in range(NT):
                    pe.wait_ge(s["y_read"], b * (NT + 1) + max(t, 1))
                    a = (t % 2) * BANK
                    pe.matmul(p_y[:, a:a + BANK], ones[:], b2[:], start=True, stop=False, skip_group_check=True)
                    for e in range(E):
                        last = pe.matmul(p_y[:, a + e * C:a + (e + 1) * C], hidden[:, e, t * P:(t + 1) * P], w2[:, e, :],
                                         start=False, stop=(e == E - 1), skip_group_check=True)
                    last.then_inc(s["y_done"], 1)

        @block.vector
        def _(dve):
            link = Chain(dve, s["chain_c"])
            dve.wait_ge(s["loaded"], LOADED)
            link(dve.memset(xt[C:C + 1, :], 1.0))
            link(dve.memset(ones[:], 1.0))
            dve.wait_ge(s["ids_ready"], 1)
            link(dve.tensor_copy(expert_ids[:], ids_int[:]))
            dve.nop().then_inc(s["consts"], 1)
            CHAIN = 2 * NORM_CHAIN + 2 * NT + 15
            with dve.Fori(0, batches) as b:
                link = Chain(dve, s["chain_b"], b * CHAIN)
                hb = H[:, bass.ds(b * NT, NT), :]
                norm_tiles(dve, link, hb, xn[:], square[:], stat, s["var_ready"], s["root_ready"], b * 2 + 1)
                norm_tiles(dve, link, xn[:], xn[:], square[:], stat, s["var_ready"], s["root_ready"], b * 2 + 2)
                dve.nop().then_inc(s["xn_ready"], 1)
                dve.wait_ge(s["xt_done"], b + 1)
                for k, (c0, n) in enumerate(((0, 4 * P), (4 * P, 3 * P))):
                    link(dve.tensor_scalar(xt[0:C, c0:c0 + n], p_t[:, k * BANK:k * BANK + n], gb[:, 0:1], gb[:, 1:2],
                                           ALU.mult, ALU.add))
                dve.nop().then_inc(s["xt_ready"], 1)
                dve.wait_ge(s["logits_done"], b + 1)
                link(dve.tensor_copy(logits[:].rearrange("p t e -> p (t e)"), p_y[:, 0:NT * E]))
                dve.nop().then_inc(s["y_read"], 1)
                dve.memset(pause[:, 0:1], 0.0)
                for t in range(NT):
                    best_one = dve.max(best[:, t, :], logits[:, t, :])
                link(best_one)
                dve.memset(pause[:, 1:2], 0.0)
                for t in range(NT):
                    best_one = dve.max_index(best_at[:, t, :], best[:, t, :], logits[:, t, :])
                link(best_one)
                dve.tensor_tensor(pw[:, 0, :], best[:, :, 1], best[:, :, 0], ALU.subtract).then_inc(s["pair_diff"], 1)
                link(dve.tensor_copy(best_id[:], best_at[:]))
                dve.wait_ge(s["pair_exp"], b + 1)
                link(dve.tensor_scalar(pw[:, 2, :], pw[:, 1, :], 1.0, None, ALU.add))
                link(dve.reciprocal(pw[:, 2, :], pw[:, 2, :]))
                link(dve.tensor_tensor(pw[:, 3, :], pw[:, 2, :], pw[:, 1, :], ALU.mult))
                for k, w_ in ((0, weight), (1, weight2)):
                    link(dve.tensor_tensor(w_[:], expert_ids[:], best_id[:, :, k:k + 1].to_broadcast([P, NT, E]), ALU.is_equal))
                for k, w_ in ((0, weight), (1, weight2)):
                    link(dve.tensor_tensor(w_[:], w_[:], pw[:, 2 + k, :].unsqueeze(2).to_broadcast([P, NT, E]), ALU.mult))
                link(dve.tensor_tensor(weight[:], weight[:], weight2[:], ALU.add))
                for t in range(NT):
                    dve.wait_ge(s["y_done"], b * NT + t + 1)
                    a = (t % 2) * BANK
                    wt = weighted[:, t % 2, :]
                    link(dve.tensor_tensor(wt.rearrange("p (e c) -> p e c", e=E),
                                           p_y[:, a:a + BANK].rearrange("p (e c) -> p e c", e=E),
                                           weight[:, t, :].unsqueeze(2).to_broadcast([P, E, C]), ALU.mult))
                    link(dve.tensor_reduce(y[:, t, :], wt.rearrange("p (e c) -> p c e", e=E), AX_X, ALU.add))
                    dve.nop().then_inc(s["y_read"], 1)
                link(dve.tensor_tensor(hb, hb, y[:], ALU.add))
                assert link.n == CHAIN, (link.n, CHAIN)

        @block.scalar
        def _(act):
            act.wait_ge(s["loaded"], LOADED)
            with act.Fori(0, batches) as b:
                for k in range(2):
                    act.wait_ge(s["var_ready"], b * 2 + k + 1)
                    act.activation(stat[:, 2, :], stat[:, 1, :], ACT.Sqrt).then_inc(s["root_ready"], 1)
                for e in range(E):
                    act.wait_ge(s["h_done"], b * E + e + 1)
                    act.activation(hidden[:, e, :].rearrange("p (h n) -> p h n", h=2),
                                   ap(p_h, 0, HID, (e % 2) * 2 * BANK, [[BANK, 2], [1, HALF]]), ACT.Gelu,
                                   bias=b1[:, e:e + 1]).then_inc(s["gelu_done"], 1)
                act.wait_ge(s["pair_diff"], b + 1)
                act.activation(pw[:, 1, :], pw[:, 0, :], ACT.Exp).then_inc(s["pair_exp"], 1)

def density_attention(nc, H, ident, w_qkv, w_proj, b_proj, batches=N_B):
    HD, BAND, N_TOKENS = C // HEADS, 16, N_B * W
    ITEMS = HEADS * NT
    with ExitStack() as ctx:
        m = Memory(nc, ctx, "den")
        xn = m.sb("xn", [P, TILES, C])
        before = m.sb("before", [P, TILES, C])
        stat = m.sb("stat", [P, 9, TILES])
        col = m.sb("col", [128, 8])
        ones = m.sb("ones", [P, 128])
        closed = m.sb("closed", [P, TILES])
        pause = m.sb("pause", [P, 1])
        qkv_in = m.sb("qkv_in", [C, 3, HEADS, HD])
        wqk = m.sb("wqk", [C, 2, 2, 4, 32])
        wproj = m.sb("wproj", [C + 1, C])
        outside = m.sb("outside", [P, NT, W])
        mask = m.sb("mask", [P, NT, W])
        xt = m.sb("xt", [C, W])
        xstage = m.sb("xstage", [P, NT, C])
        closed_wide = m.sb("closed_wide", [P, NT, P])
        closed_row = m.sb("closed_row", [P, W])
        qk = m.sb("qk", [128, 2, 2, W])
        val = m.sb("val", [P, NT, C])
        probs = m.sb("probs", [P, 4, W])
        neg_max = m.sb("neg_max", [P, ITEMS])
        top = m.sb("top", [P, ITEMS])
        total = m.sb("total", [P, NT, HEADS])
        turned = m.sb("turned", [P, 2, NT, P])
        o = m.sb("o", [P, NT, C])
        ot = m.sb("ot", [C + 1, W])
        p_s = m.ps("p_s", [128, 4 * BANK])
        p_t = m.ps("p_t", [128, 2 * BANK])
        p_o = m.ps("p_o", [P, BANK])
        p_x = m.ps("p_x", [P, BANK])
        names = ("loaded shifted xn_out var_ready root_ready ones_ready sums_ready sums_done closed_ready band_ready "
                 "consts x_ready xt_done xt_ready closed_done proj_done qk_v qk_a v_done v_copied mask_ready "
                 "s_done max_done neg_done exp_done turned_done copied_v copied_a pv_done o_all o_ready ot_done "
                 "ot_ready out_done batch_out chain_c chain_b chain_n band weights_zero").split()
        s = {n: m.sem(n) for n in names}
        LOADED = 3 * 16
        block = ctx.enter_context(nc.Block())

        @block.sync
        def _(sp):
            sp.dma_start(qkv_in[:].rearrange("p a h c -> p (a h c)"), w_qkv).then_inc(s["loaded"], 16)
            sp.dma_start(wproj[0:C, :], w_proj).then_inc(s["loaded"], 16)
            sp.dma_start(wproj[C:C + 1, :], b_proj.rearrange("(a n) -> a n", a=1)).then_inc(s["loaded"], 16)
            sp.wait_ge(s["xn_out"], 1)
            sp.dma_start(before[1:P, :, :], xn[0:P - 1, :, :]).then_inc(s["shifted"], 16)
            seam = lambda t, p, k, n: ap(t, p, 1, k * C, [[NT * C, N_B], [1, n * C]])
            sp.dma_start(seam(before, 0, 1, NT - 1), seam(xn, P - 1, 0, NT - 1)).then_inc(s["shifted"], 16)
            sp.dma_start(seam(before, 0, 0, 1), seam(xn, 0, 0, 1)).then_inc(s["shifted"], 16)

        @block.gpsimd
        def _(pool):
            pool.memset(outside[:], 1.0).then_inc(s["band"], 1)
            for k, sign in enumerate((1, -1)):
                pool.wait_ge(s["band"], k + 1)
                pool.affine_select(out=outside[:], in_=outside[:], compare_op=ALU.is_gt, fill=0.0, base=BAND,
                                   pattern=[[sign * P, NT], [-sign, W]], channel_multiplier=sign).then_inc(s["band"], 1)

        @block.tensor
        def _(pe):
            for k in range(2):
                pe.wait_ge(s["sums_ready"], k + 1)
                pe.matmul(p_x[:, k:k + 1], ones[:, 0:P], col[0:P, k:k + 1], start=True, stop=True).then_inc(s["sums_done"], 1)
            pe.wait_ge(s["consts"], 1)

            def scores(b, i):
                h, t = divmod(i, NT)
                g, j = h % 4, h // 4
                if i >= 2:
                    pe.wait_ge(s["max_done"], b * ITEMS + i - 1)
                for half in range(2):
                    a = (i % 2) * 2 * BANK + half * BANK
                    last = pe.matmul(p_s[0:P, a:a + HALF], qk[32 * g:32 * g + HD, 0, j, t * P:(t + 1) * P],
                                     qk[32 * g:32 * g + HD, 1, j, half * HALF:(half + 1) * HALF], start=True, stop=True)
                last.then_inc(s["s_done"], 1)

            with pe.Fori(0, batches) as b:
                pe.wait_ge(s["x_ready"], b + 1)
                turn_tiles(pe, p_t, xstage, ident).then_inc(s["xt_done"], 1)
                for t in range(NT):
                    c0 = (t // 4) * BANK + (t % 4) * P
                    last = pe.matmul(p_s[0:P, c0:c0 + P], closed_wide[:, t, :], ident[0:P, 0:P], start=True, stop=True)
                last.then_inc(s["closed_done"], 1)
                pe.wait_ge(s["xt_ready"], b + 1)
                for t in range(NT):
                    last = pe.matmul(p_x[:, t * C:(t + 1) * C], xt[:, t * P:(t + 1) * P],
                                     qkv_in[:, 2, :, :].rearrange("p h c -> p (h c)"), start=True, stop=True)
                last.then_inc(s["v_done"], 1)
                for n, (a, j) in enumerate(((0, 0), (1, 0), (0, 1), (1, 1))):
                    buf = 1 if n % 2 == 0 else 0
                    if n == 1:
                        pe.wait_ge(s["mask_ready"], b * 2 + 1)
                    if n >= 2:
                        pe.wait_ge(s["qk_v"] if n % 2 == 0 else s["qk_a"], b * 2 + 1)
                    for half in range(2):
                        c0 = buf * 2 * BANK + half * BANK
                        last = pe.matmul(p_s[:, c0:c0 + HALF], wqk[:, a, j, :, :].rearrange("p g c -> p (g c)"),
                                         xt[:, half * HALF:(half + 1) * HALF], start=True, stop=True)
                    last.then_inc(s["proj_done"], 1)
                pe.wait_ge(s["qk_v"], b * 2 + 2)
                pe.wait_ge(s["qk_a"], b * 2 + 2)
                scores(b, 0)
                scores(b, 1)
                for i in range(ITEMS):
                    h, t = divmod(i, NT)
                    pe.wait_ge(s["exp_done"], b * ITEMS + i + 1)
                    if i:
                        pe.wait_ge(s["copied_v"], b * ITEMS + i)
                        pe.wait_ge(s["copied_a"], b * ITEMS + i)
                    for k in range(NT):
                        c0 = (k // 4) * BANK + (k % 4) * P
                        last = pe.transpose(p_t[0:P, c0:c0 + P], probs[:, i % 4, k * P:(k + 1) * P], ident[0:P, 0:P])
                    last.then_inc(s["turned_done"], 1)
                    if i + 2 < ITEMS:
                        scores(b, i + 2)
                    pe.wait_ge(s["copied_v"], b * ITEMS + i + 1)
                    pe.wait_ge(s["copied_a"], b * ITEMS + i + 1)
                    for k in range(NT):
                        last = pe.matmul(p_o[:, (t * HEADS + h) * HD:(t * HEADS + h + 1) * HD],
                                         turned[:, i % 2, k, :], val[:, k, h * HD:(h + 1) * HD],
                                         start=(k == 0), stop=(k == NT - 1))
                    last.then_inc(s["pv_done"], 1)
                pe.wait_ge(s["o_ready"], b + 1)
                turn_tiles(pe, p_t, o, ident).then_inc(s["ot_done"], 1)
                pe.wait_ge(s["ot_ready"], b + 1)
                for t in range(NT):
                    last = pe.matmul(p_x[:, t * C:(t + 1) * C], ot[:, t * P:(t + 1) * P], wproj[:], start=True, stop=True)
                last.then_inc(s["out_done"], 1)

        @block.vector
        def _(dve):
            link = Chain(dve, s["chain_c"])
            link(dve.memset(ones[:], 1.0))
            link(dve.memset(ot[C:C + 1, :], 1.0))
            link(dve.memset(wqk[:], 0.0))
            norm_tiles(dve, link, H[:], xn[:], before[:], stat, s["var_ready"], s["root_ready"], 1)
            dve.nop().then_inc(s["xn_out"], 1)
            mean, var, root, rstd, tmp, safe, grad, dens, work = (stat[:, k, :] for k in range(9))
            wide = [P, TILES, C]
            dve.wait_ge(s["shifted"], 3 * 16)
            link(dve.tensor_tensor(before[:], xn[:], before[:], ALU.subtract))
            link(dve.tensor_reduce(grad, before[:], AX_X, ALU.add, apply_absolute_value=True))
            link(dve.tensor_reduce(mean, xn[:], AX_X, ALU.add))
            link(dve.tensor_scalar(mean, mean, 1.0 / C, None, ALU.mult))
            link(dve.tensor_tensor(before[:], xn[:], mean.unsqueeze(2).to_broadcast(wide), ALU.subtract))
            link(dve.tensor_tensor(before[:], before[:], before[:], ALU.mult))
            link(dve.tensor_reduce(work, before[:], AX_X, ALU.add))
            link(dve.tensor_scalar(work, work, 1.0 / (C - 1), None, ALU.mult))
            dve.tensor_scalar(var, work, 1e-30, None, ALU.max).then_inc(s["var_ready"], 1)
            dve.wait_ge(s["root_ready"], 2)
            newton_rsqrt(dve, link, var, root, rstd, tmp)
            link(dve.tensor_tensor(work, work, rstd, ALU.mult))
            link(dve.tensor_scalar(grad, grad, 1.0 / C, None, ALU.mult))
            link(dve.tensor_tensor(dens, work, grad, ALU.add))
            link(dve.tensor_scalar(dens, dens, 0.5, None, ALU.mult))
            dve.tensor_reduce(col[0:P, 0:1], dens, AX_X, ALU.add).then_inc(s["sums_ready"], 1)
            dve.wait_ge(s["sums_done"], 1)
            link(dve.tensor_scalar(col[0:P, 2:3], p_x[:, 0:1], 1.0 / N_TOKENS, None, ALU.mult))
            link(dve.tensor_scalar(work, dens, col[0:P, 2:3], None, ALU.subtract))
            link(dve.tensor_tensor(work, work, work, ALU.mult))
            dve.tensor_reduce(col[0:P, 1:2], work, AX_X, ALU.add).then_inc(s["sums_ready"], 1)
            dve.wait_ge(s["sums_done"], 2)
            link(dve.tensor_scalar(col[0:P, 3:4], p_x[:, 1:2], 1.0 / (N_TOKENS - 1), None, ALU.mult))
            dve.tensor_scalar(var[:, 0:1], col[0:P, 3:4], 1e-30, None, ALU.max).then_inc(s["var_ready"], 1)
            dve.wait_ge(s["root_ready"], 3)
            newton_rsqrt(dve, link, var[:, 0:1], root[:, 0:1], rstd[:, 0:1], tmp[:, 0:1])
            link(dve.tensor_tensor(col[0:P, 4:5], col[0:P, 3:4], rstd[:, 0:1], ALU.mult))
            link(dve.tensor_scalar(col[0:P, 4:5], col[0:P, 4:5], 0.5, None, ALU.mult))
            link(dve.tensor_tensor(col[0:P, 4:5], col[0:P, 4:5], col[0:P, 2:3], ALU.add))
            link(dve.tensor_scalar(closed[:], dens, col[0:P, 4:5], -1e10, ALU.is_le, ALU.mult))
            dve.wait_ge(s["band"], 3)
            link(dve.tensor_scalar(outside[:], outside[:], -1.0, 1.0, ALU.mult, ALU.add))
            dve.wait_ge(s["loaded"], LOADED)
            for a in range(2):
                for j in range(2):
                    last = dve.tensor_copy(wqk[:, a, j, :, 0:HD], qkv_in[:, a, 4 * j:4 * j + 4, :])
            link(last)
            dve.nop().then_inc(s["consts"], 1)

            def row_max(b, i):
                t = i % NT
                dve.wait_ge(s["s_done"], b * ITEMS + i + 1)
                if i >= 4:
                    dve.wait_ge(s["turned_done"], b * ITEMS + i - 3)
                dve.memset(pause[:], 0.0)
                dve.tensor_tensor_reduce(probs[:, i % 4, :].rearrange("p (h n) -> p h n", h=2),
                                         ap(p_s, 0, P, (i % 2) * 2 * BANK, [[BANK, 2], [1, HALF]]),
                                         mask[:, t, :].rearrange("p (h n) -> p h n", h=2),
                                         1.0, -3e38, ALU.add, ALU.max, top[:, i:i + 1]).then_inc(s["max_done"], 1)
                dve.wait_ge(s["max_done"], b * ITEMS + i + 1)
                dve.tensor_scalar(neg_max[:, i:i + 1], top[:, i:i + 1], -1.0, None, ALU.mult).then_inc(s["neg_done"], 1)

            CHAIN = 9
            with dve.Fori(0, batches) as b:
                link = Chain(dve, s["chain_b"], b * CHAIN)
                hb = H[:, bass.ds(b * NT, NT), :]
                dve.tensor_copy(xstage[:], xn[:, bass.ds(b * NT, NT), :])
                dve.tensor_scalar(closed_wide[:], closed[:, bass.ds(b * NT, NT)].unsqueeze(2).to_broadcast([P, NT, P]),
                                  1.0, None, ALU.mult).then_inc(s["x_ready"], 1)
                dve.wait_ge(s["xt_done"], b + 1)
                link(dve.tensor_copy(xt[:, 0:4 * P], p_t[0:C, 0:4 * P]))
                link(dve.tensor_copy(xt[:, 4 * P:W], p_t[0:C, BANK:BANK + 3 * P]))
                dve.nop().then_inc(s["xt_ready"], 1)
                dve.wait_ge(s["closed_done"], b + 1)
                link(dve.tensor_copy(closed_row[:, 0:4 * P], p_s[0:P, 0:4 * P]))
                link(dve.tensor_copy(closed_row[:, 4 * P:W], p_s[0:P, BANK:BANK + 3 * P]))
                dve.nop().then_inc(s["mask_ready"], 1)
                link(dve.tensor_tensor(mask[:], outside[:], closed_row[:].unsqueeze(1).to_broadcast([P, NT, W]), ALU.mult))
                dve.nop().then_inc(s["mask_ready"], 1)
                dve.wait_ge(s["v_done"], b + 1)
                dve.tensor_copy(val[:], p_x[:, 0:NT * C].rearrange("p (t c) -> p t c", c=C)).then_inc(s["v_copied"], 1)
                for j in range(2):
                    dve.wait_ge(s["proj_done"], b * 4 + 2 * j + 1)
                    dve.tensor_scalar(qk[:, 0, j, :].rearrange("p (h n) -> p h n", h=2),
                                      ap(p_s, 0, 128, 2 * BANK, [[BANK, 2], [1, HALF]]), HD ** -0.5, None,
                                      ALU.mult).then_inc(s["qk_v"], 1)
                row_max(b, 0)
                for i in range(ITEMS):
                    if i + 1 < ITEMS:
                        row_max(b, i + 1)
                    dve.wait_ge(s["turned_done"], b * ITEMS + i + 1)
                    if i >= 2:
                        dve.wait_ge(s["pv_done"], b * ITEMS + i - 1)
                    dve.tensor_copy(turned[:, i % 2, 0:4, :],
                                    p_t[0:P, 0:4 * P].rearrange("p (k q) -> p k q", q=P)).then_inc(s["copied_v"], 1)
                dve.wait_ge(s["exp_done"], b * ITEMS + ITEMS)
                link(dve.reciprocal(total[:], total[:]))
                dve.wait_ge(s["pv_done"], b * ITEMS + ITEMS)
                dve.tensor_tensor(o[:].rearrange("p t (h c) -> p (t h) c", c=HD), p_o[:, 0:NT * C].rearrange("p (n c) -> p n c", c=HD),
                                  total[:].rearrange("p t h -> p (t h)").unsqueeze(2).to_broadcast([P, NT * HEADS, HD]),
                                  ALU.mult).then_inc(s["o_ready"], 1)
                dve.wait_ge(s["ot_done"], b + 1)
                link(dve.tensor_copy(ot[0:C, 0:4 * P], p_t[0:C, 0:4 * P]))
                link(dve.tensor_copy(ot[0:C, 4 * P:W], p_t[0:C, BANK:BANK + 3 * P]))
                dve.nop().then_inc(s["ot_ready"], 1)
                dve.wait_ge(s["out_done"], b + 1)
                link(dve.tensor_tensor(hb, hb, p_x[:, 0:NT * C].rearrange("p (t c) -> p t c", c=C), ALU.add))
                assert link.n == CHAIN, link.n

        @block.scalar
        def _(act):
            act.wait_ge(s["var_ready"], 1)
            act.activation(stat[:, 2, :], stat[:, 1, :], ACT.Sqrt).then_inc(s["root_ready"], 1)
            act.wait_ge(s["var_ready"], 2)
            act.activation(stat[:, 2, :], stat[:, 1, :], ACT.Sqrt).then_inc(s["root_ready"], 1)
            act.wait_ge(s["var_ready"], 3)
            act.activation(stat[:, 2, 0:1], stat[:, 1, 0:1], ACT.Sqrt).then_inc(s["root_ready"], 1)

            def exponentials(b, i):
                h, t = divmod(i, NT)
                act.wait_ge(s["neg_done"], b * ITEMS + i + 1)
                act.activation(probs[:, i % 4, :], probs[:, i % 4, :], ACT.Exp, bias=neg_max[:, i:i + 1],
                               accum_out=ap(total, 0, P, t * HEADS + h, [[1, 1]])).then_inc(s["exp_done"], 1)

            with act.Fori(0, batches) as b:
                for j in range(2):
                    act.wait_ge(s["proj_done"], b * 4 + 2 * j + 2)
                    act.activation(qk[:, 1, j, :].rearrange("p (h n) -> p h n", h=2),
                                   ap(p_s, 0, 128, 0, [[BANK, 2], [1, HALF]]), ACT.Copy).then_inc(s["qk_a"], 1)
                exponentials(b, 0)
                for i in range(ITEMS):
                    if i + 1 < ITEMS:
                        exponentials(b, i + 1)
                    act.wait_ge(s["turned_done"], b * ITEMS + i + 1)
                    if i >= 2:
                        act.wait_ge(s["pv_done"], b * ITEMS + i - 1)
                    act.activation(turned[:, i % 2, 4:7, :],
                                   p_t[0:P, BANK:BANK + 3 * P].rearrange("p (k q) -> p k q", q=P),
                                   ACT.Copy).then_inc(s["copied_a"], 1)

def memory_attention(nc, H, ident, w_pk, pk_keys, w_q, table, w_o, batches=N_B):
    K1, DK, TOP = 64, 32, 16
    CANDS, n_c = [], 0
    for a0, na in ((0, 1), (1, 1), (2, 1), (3, 1), (4, 1), (5, 3), (8, 8)):
        nb = TOP // (a0 + 1)
        assert TOP // (a0 + na) == nb
        CANDS.append((a0, na, nb, n_c))
        n_c += na * nb
    SLOTS = 4
    assert HEADS % SLOTS == 0
    LOW = -3.0e38
    with ExitStack() as ctx:
        m = Memory(nc, ctx, "mem")
        keys_in = m.sb("keys_in", [K1, 2, HEADS * DK])
        wpk = m.sb("wpk", [C, 4, 128])
        wq = m.sb("wq", [C, 4, 128])
        wo = m.sb("wo", [128, 4, C])
        keys_bd = m.sb("keys_bd", [128, 4, 4 * K1])
        causal = m.sb("causal", [P, P])
        cand_int = m.sb("cand_int", [P, n_c], mybir.dt.int32)
        cand_no = m.sb("cand_no", [P, n_c])
        head_int = m.sb("head_int", [P, HEADS], mybir.dt.int32)
        head_off = m.sb("head_off", [P, HEADS])
        pause = m.sb("pause", [P, 1])
        xn = m.sb("xn", [P, NT, C])
        square = m.sb("square", [P, NT, C])
        stat = m.sb("stat", [P, 5, NT])
        xt = m.sb("xt", [C, W])
        qpk = m.sb("qpk", [128, 4, W])
        qat = m.sb("qat", [128, 4, W])
        kat = m.sb("kat", [128, 4, W])
        sim = m.sb("sim", [P, 2, HEADS, K1])
        rest = m.sb("rest", [P, 2, HEADS, K1])
        s16 = m.sb("s16", [P, 2, HEADS, TOP])
        i16 = m.sb("i16", [P, 2, HEADS, TOP], U32)
        f16 = m.sb("f16", [P, 2, HEADS, TOP])
        cand = m.sb("cand", [P, HEADS, n_c])
        cand_rest = m.sb("cand_rest", [P, HEADS, n_c])
        cand_row = m.sb("cand_row", [P, HEADS, n_c])
        best = m.sb("best", [P, HEADS, TOP])
        best_at = m.sb("best_at", [P, HEADS, TOP], U32)
        best_no = m.sb("best_no", [P, HEADS, TOP])
        match = m.sb("match", [P, HEADS * TOP, n_c])
        rows_f = m.sb("rows_f", [P, HEADS, TOP])
        expo = m.sb("expo", [P, HEADS, TOP])
        esum = m.sb("esum", [P, HEADS])
        rows = m.sb("rows", [P, NT, HEADS, TOP], U32)
        share = m.sb("share", [P, NT, HEADS, TOP])
        got = m.sb("got", [P, SLOTS, TOP, 2 * C])
        kv = m.sb("kv", [P, NT, 2, HEADS, C])
        probs = m.sb("probs", [P, 2, W])
        top = m.sb("top", [P, NT, HEADS])
        total = m.sb("total", [P, NT, HEADS])
        turned = m.sb("turned", [P, 2, NT, P])
        o = m.sb("o", [P, 4, 2 * C])
        ot = m.sb("ot", [128, 4, P])
        p_s = m.ps("p_s", [128, 4 * BANK])
        p_t = m.ps("p_t", [128, 2 * BANK])
        p_o = m.ps("p_o", [P, BANK])
        p_x = m.ps("p_x", [128, BANK])
        names = ("loaded made ready_c keys_turned var_ready root_ready xn_ready xt_done xt_ready proj_done proj_copied "
                 "x_done x_read fin_diff fin_exp rows_ready sums_done kat_ready s_done neg_done exp_done turned_done "
                 "slots_taken turned_copied pv_done o_ready ot_done ot_ready chain_c chain_b h_added").split()
        s = {n: m.sem(n) for n in names}
        got_in = [m.sem(f"got_in{k}") for k in range(SLOTS)]
        LOADED = 4 * 16
        X_USES = 4 * NT
        block = ctx.enter_context(nc.Block())

        @block.sync
        def _(sp):
            sp.dma_start(keys_in[:], pk_keys.rearrange("p k h d -> k p (h d)")).then_inc(s["loaded"], 16)
            sp.dma_start(wpk[:].rearrange("p a n -> p (a n)"), w_pk).then_inc(s["loaded"], 16)
            sp.dma_start(wq[:].rearrange("p a n -> p (a n)"), w_q).then_inc(s["loaded"], 16)
            sp.dma_start(wo[:], w_o.rearrange("(a p) n -> p a n", p=128)).then_inc(s["loaded"], 16)

        @block.gpsimd
        def _(pool):
            pool.memset(causal[:], 0.0).then_inc(s["made"], 1)
            pool.iota(cand_int[:], [[1, n_c]], base=0, channel_multiplier=0).then_inc(s["made"], 1)
            pool.iota(head_int[:], [[K1 * K1, HEADS]], base=0, channel_multiplier=0).then_inc(s["made"], 1)
            pool.wait_ge(s["made"], 3)
            pool.affine_select(out=causal[:], in_=causal[:], compare_op=ALU.is_ge, fill=-1e30, base=0,
                               pattern=[[-1, P]], channel_multiplier=1).then_inc(s["made"], 1)
            pool.sem_inc(s["sums_done"], SLOTS)
            with pool.Fori(0, batches) as b:
                for t in range(NT):
                    pool.wait_ge(s["rows_ready"], b * NT + t + 1)
                    for h in range(HEADS):
                        pool.wait_ge(s["sums_done"], (b * NT + t) * HEADS + h + 1)
                        pool.sem_inc(s["slots_taken"], 1)
                        for k in range(TOP):
                            pool.indirect_dma_start(got[:, h % SLOTS, k, :], None, table,
                                                    bass.IndirectOffsetOnAxis(ap=rows[:, t, h, k:k + 1], axis=0))\
                                .then_inc(got_in[h % SLOTS], 16)

        @block.tensor
        def _(pe):
            pe.wait_ge(s["loaded"], LOADED)
            for a in range(4):
                last = pe.transpose(p_x[:, a * K1:(a + 1) * K1], keys_in[:, a // 2, (a % 2) * 128:(a % 2) * 128 + 128],
                                    ident[0:K1, 0:K1])
            last.then_inc(s["keys_turned"], 1)
            pe.wait_ge(s["ready_c"], 1)
            x_use = [0]

            def x_bank(b):
                pe.wait_ge(s["x_read"], b * X_USES + x_use[0] + 1)
                x_use[0] += 1

            def similarities(b, t):
                for p in range(2):
                    x_bank(b)
                    for c in range(2):
                        last = pe.matmul(p_x[0:P, c * 256:(c + 1) * 256], qpk[:, 2 * p + c, t * P:(t + 1) * P],
                                         keys_bd[:, 2 * p + c, :], start=True, stop=True)
                    last.then_inc(s["x_done"], 1)

            def scores(b, t, h):
                it = b * NT + t
                if h >= 2:
                    pe.wait_ge(s["exp_done"], it * HEADS + h - 1)
                r, n = C * (h % 2), (t + 1) * P
                base = (h % 2) * 2 * BANK
                parts = ((base, 0, P),) if t == 0 else ((base, 0, n // 2), (base + BANK, n // 2, n // 2))
                for c0, k0, w_ in parts:
                    last_part = k0 + w_ == n
                    pe.matmul(p_s[0:P, c0:c0 + w_], qat[r:r + C, h // 2, t * P:(t + 1) * P],
                              kat[r:r + C, h // 2, k0:k0 + w_], start=True, stop=not last_part, skip_group_check=True)
                pe.matmul(p_s[0:P, c0 + w_ - P:c0 + w_], ident[0:P, 0:P], causal[:], start=False, stop=True,
                          skip_group_check=True).then_inc(s["s_done"], 1)

            def turn(b, t, h):
                it = b * NT + t
                pe.wait_ge(s["exp_done"], it * HEADS + h + 1)
                pe.wait_ge(s["turned_copied"], it * HEADS + h + 1)
                for k in range(t + 1):
                    c0 = (k // 4) * BANK + (k % 4) * P
                    last = pe.transpose(p_t[0:P, c0:c0 + P], probs[:, h % 2, k * P:(k + 1) * P], ident[0:P, 0:P])
                last.then_inc(s["turned_done"], 1)

            def weigh(b, t, h):
                it = b * NT + t
                pe.wait_ge(s["turned_copied"], it * HEADS + h + 2)
                if h == 0:
                    pe.wait_ge(s["o_ready"], it + 1)
                for k in range(t + 1):
                    last = pe.matmul(p_o[:, h * C:(h + 1) * C], turned[:, h % 2, k, :], kv[:, k, 1, h, :],
                                     start=(k == 0), stop=(k == t))
                last.then_inc(s["pv_done"], 1)

            def attend(b, t):
                it = b * NT + t
                pe.wait_ge(s["kat_ready"], it + 1)
                scores(b, t, 0)
                for h in range(HEADS):
                    if h + 1 < HEADS:
                        scores(b, t, h + 1)
                    turn(b, t, h)
                    if h:
                        weigh(b, t, h - 1)
                weigh(b, t, HEADS - 1)
                pe.wait_ge(s["o_ready"], it + 2)
                for a in range(4):
                    last = pe.transpose(p_t[:, a * P:(a + 1) * P], o[:, a, :], ident[0:P, 0:P])
                last.then_inc(s["ot_done"], 1)
                x_bank(b)
                pe.wait_ge(s["ot_ready"], it + 1)
                for a in range(4):
                    last = pe.matmul(p_x[0:P, 0:C], ot[:, a, :], wo[:, a, :], start=(a == 0), stop=(a == 3))
                last.then_inc(s["x_done"], 1)

            with pe.Fori(0, batches) as b:
                x_use[0] = 0
                pe.wait_ge(s["xn_ready"], b + 1)
                turn_tiles(pe, p_t, xn, ident).then_inc(s["xt_done"], 1)
                pe.wait_ge(s["xt_ready"], b + 1)
                for a in range(8):
                    w_ = wpk[:, a, :] if a < 4 else wq[:, a - 4, :]
                    if a >= 2:
                        pe.wait_ge(s["proj_copied"], b * 8 + a - 1)
                    for half in range(2):
                        c0 = (a % 2) * 2 * BANK + half * BANK
                        last = pe.matmul(p_s[:, c0:c0 + HALF], w_, xt[:, half * HALF:(half + 1) * HALF], start=True, stop=True)
                    last.then_inc(s["proj_done"], 1)
                pe.wait_ge(s["proj_copied"], b * 8 + 8)
                similarities(b, 0)
                for t in range(NT + 1):
                    if t + 1 < NT:
                        similarities(b, t + 1)
                    if t:
                        attend(b, t - 1)
                    if t < NT:
                        x_bank(b)
                        pe.wait_ge(s["sums_done"], (b * NT + t + 1) * HEADS + SLOTS)
                        for a in range(4):
                            last = pe.transpose(p_x[:, a * P:(a + 1) * P],
                                                kv[:, t, 0, 2 * a:2 * a + 2, :].rearrange("p h c -> p (h c)"), ident[0:P, 0:P])
                        last.then_inc(s["x_done"], 1)
                assert x_use[0] == X_USES

        @block.vector
        def _(dve):
            link = Chain(dve, s["chain_c"])
            link(dve.memset(keys_bd[:], 0.0))
            dve.wait_ge(s["keys_turned"], 1)
            for g in range(4):
                link(dve.tensor_copy(keys_bd[DK * g:DK * g + DK, :, K1 * g:K1 * g + K1],
                                     ap(p_x, DK * g, DK, 0, [[K1, 4], [1, K1]])))
            dve.wait_ge(s["made"], 4)
            link(dve.tensor_copy(cand_no[:], cand_int[:]))
            link(dve.tensor_copy(head_off[:], head_int[:]))
            dve.nop().then_inc(s["x_read"], 1)
            dve.nop().then_inc(s["ready_c"], 1)
            dve.nop().then_inc(s["o_ready"], 1)

            def flat(v):
                return v.rearrange("p a b -> p (a b)")

            def top16(link, values, left, out, at, n):
                dve.memset(pause[:], 0.0)
                for v, w_ in zip(values, out):
                    last = dve.max(w_[:, 0:8], v)
                link(last)
                dve.memset(pause[:], 0.0)
                for v, r, w_ in zip(values, left, out):
                    last = dve.match_replace(r, w_[:, 0:8], v, LOW)
                link(last)
                dve.memset(pause[:], 0.0)
                for r, w_ in zip(left, out):
                    last = dve.max(w_[:, 8:16], r)
                link(last)
                dve.memset(pause[:], 0.0)
                for v, r, w_, i in zip(values, left, out, at):
                    dve.max_index(i[:, 0:8], w_[:, 0:8], v)
                    last = dve.max_index(i[:, 8:16], w_[:, 8:16], r)
                link(last)

            x_seen = [0]

            def x_wait(b):
                dve.wait_ge(s["x_done"], b * X_USES + x_seen[0] + 1)
                x_seen[0] += 1

            def select(b, t, link):
                for p in range(2):
                    x_wait(b)
                    dve.tensor_copy(sim[:, p, :, :], p_x[0:P, :].rearrange("p (h k) -> p h k", h=HEADS)).then_inc(s["x_read"], 1)
                dve.wait_ge(s["x_read"], b * X_USES + x_seen[0] + 1)
                ph = [(p, h) for p in range(2) for h in range(HEADS)]
                top16(link, [sim[:, p, h, :] for p, h in ph], [rest[:, p, h, :] for p, h in ph],
                      [s16[:, p, h, :] for p, h in ph], [i16[:, p, h, :] for p, h in ph], K1)
                link(dve.tensor_copy(f16[:], i16[:]))
                link(dve.scalar_tensor_tensor(out=f16[:, 1, :, :], in0=f16[:, 1, :, :], scalar=float(K1),
                                              in1=head_off[:].unsqueeze(2).to_broadcast([P, HEADS, TOP]),
                                              op0=ALU.mult, op1=ALU.add))
                for src, dst in ((s16, cand), (f16, cand_row)):
                    for a0, na, nb, at in CANDS:
                        first = ap(src, 0, P, a0, [[TOP, HEADS], [1, na], [0, nb]])
                        second = ap(src, 0, P, HEADS * TOP, [[TOP, HEADS], [0, na], [1, nb]])
                        last = dve.tensor_tensor(ap(dst, 0, P, at, [[n_c, HEADS], [nb, na], [1, nb]]), first, second, ALU.add)
                link(last)
                hs_ = range(HEADS)
                top16(link, [cand[:, h, :] for h in hs_], [cand_rest[:, h, :] for h in hs_],
                      [best[:, h, :] for h in hs_], [best_at[:, h, :] for h in hs_], n_c)
                dve.tensor_tensor(expo[:], best[:], best[:, :, 0:1].to_broadcast([P, HEADS, TOP]), ALU.subtract).then_inc(s["fin_diff"], 1)
                link(dve.tensor_copy(best_no[:], best_at[:]))
                link(dve.tensor_tensor(match[:], cand_no[:].unsqueeze(1).to_broadcast([P, HEADS * TOP, n_c]),
                                       flat(best_no[:]).unsqueeze(2).to_broadcast([P, HEADS * TOP, n_c]), ALU.is_equal))
                link(dve.tensor_tensor(match[:].rearrange("p (h k) c -> p h k c", h=HEADS),
                                       match[:].rearrange("p (h k) c -> p h k c", h=HEADS),
                                       cand_row[:].unsqueeze(2).to_broadcast([P, HEADS, TOP, n_c]), ALU.mult))
                link(dve.tensor_reduce(flat(rows_f[:]), match[:], AX_X, ALU.add))
                dve.tensor_copy(rows[:, t, :, :], rows_f[:]).then_inc(s["rows_ready"], 1)
                dve.wait_ge(s["fin_exp"], b * NT + t + 1)
                link(dve.tensor_reduce(esum[:], expo[:], AX_X, ALU.add))
                link(dve.reciprocal(esum[:], esum[:]))
                link(dve.tensor_tensor(share[:, t, :, :], expo[:], esum[:].unsqueeze(2).to_broadcast([P, HEADS, TOP]), ALU.mult))

            def sum_rows(b, t, h, link):
                dve.wait_ge(got_in[h % SLOTS], ((b * NT + t) * (HEADS // SLOTS) + h // SLOTS + 1) * 16 * TOP)
                g = got[:, h % SLOTS, :, :]
                link(dve.tensor_tensor(g, g, share[:, t, h, :].unsqueeze(2).to_broadcast([P, TOP, 2 * C]), ALU.mult))
                dve.tensor_reduce(ap(kv, 0, P, (t * 2 * HEADS + h) * C, [[HEADS * C, 2], [1, C]]),
                                  g.rearrange("p k (a c) -> p a c k", a=2), AX_X, ALU.add).then_inc(s["sums_done"], 1)

            def row_max(b, t, h):
                it = b * NT + t
                dve.wait_ge(s["s_done"], it * HEADS + h + 1)
                n, base = (t + 1) * P, (h % 2) * 2 * BANK
                src = p_s[0:P, base:base + P] if t == 0 else ap(p_s, 0, P, base, [[BANK, 2], [1, n // 2]])
                axis = AX_X if t == 0 else mybir.AxisListType.XY
                dve.tensor_reduce(top[:, t, h:h + 1], src, axis, ALU.max, negate=True).then_inc(s["neg_done"], 1)

            CHAIN = 202
            with dve.Fori(0, batches) as b:
                x_seen[0] = 0
                link = Chain(dve, s["chain_b"], b * CHAIN)
                hb = H[:, bass.ds(b * NT, NT), :]
                norm_tiles(dve, link, hb, xn[:], square[:], stat, s["var_ready"], s["root_ready"], b + 1)
                dve.nop().then_inc(s["xn_ready"], 1)
                dve.wait_ge(s["xt_done"], b + 1)
                link(dve.tensor_copy(xt[:, 0:4 * P], p_t[0:C, 0:4 * P]))
                link(dve.tensor_copy(xt[:, 4 * P:W], p_t[0:C, BANK:BANK + 3 * P]))
                dve.nop().then_inc(s["xt_ready"], 1)
                select(b, 0, link)
                for t in range(NT + 1):
                    if t + 1 < NT:
                        select(b, t + 1, link)
                    for h in range(HEADS):
                        if t:
                            row_max(b, t - 1, h)
                        if t < NT:
                            sum_rows(b, t, h, link)
                    if t:
                        it = b * NT + t - 1
                        dve.wait_ge(s["exp_done"], it * HEADS + HEADS)
                        link(dve.reciprocal(total[:, t - 1, :], total[:, t - 1, :]))
                        dve.wait_ge(s["pv_done"], it * HEADS + HEADS)
                        dve.tensor_tensor(o[:].rearrange("p a (h c) -> p (a h) c", c=C),
                                          p_o[:].rearrange("p (h c) -> p h c", h=HEADS),
                                          total[:, t - 1, :].unsqueeze(2).to_broadcast([P, HEADS, C]), ALU.mult).then_inc(s["o_ready"], 1)
                        x_wait(b)
                        hrow = H[:, bass.ds(b * NT + t - 1, 1), :].rearrange("p a c -> p (a c)")
                        dve.tensor_tensor(hrow, hrow, p_x[0:P, 0:C], ALU.add).then_inc(s["x_read"], 1)
                    if t < NT:
                        x_wait(b)
                        dve.tensor_copy(kat[:, :, t * P:(t + 1) * P],
                                        p_x[:, 0:4 * P].rearrange("p (a q) -> p a q", a=4)).then_inc(s["x_read"], 1)
                        dve.wait_ge(s["x_read"], b * X_USES + x_seen[0] + 1)
                        dve.nop().then_inc(s["kat_ready"], 1)
                assert link.n == CHAIN, link.n

        @block.scalar
        def _(act):
            def final_exp(b, t):
                act.wait_ge(s["fin_diff"], b * NT + t + 1)
                act.activation(expo[:], expo[:], ACT.Exp).then_inc(s["fin_exp"], 1)

            act.sem_inc(s["turned_copied"], 1)
            with act.Fori(0, batches) as b:
                act.wait_ge(s["var_ready"], b + 1)
                act.activation(stat[:, 2, :], stat[:, 1, :], ACT.Sqrt).then_inc(s["root_ready"], 1)
                for a in range(8):
                    act.wait_ge(s["proj_done"], b * 8 + a + 1)
                    dst = qpk[:, a, :] if a < 4 else qat[:, a - 4, :]
                    act.activation(dst.rearrange("p (h n) -> p h n", h=2),
                                   ap(p_s, 0, 128, (a % 2) * 2 * BANK, [[BANK, 2], [1, HALF]]), ACT.Copy,
                                   scale=1.0 if a < 4 else C ** -0.5).then_inc(s["proj_copied"], 1)
                final_exp(b, 0)
                for t in range(NT + 1):
                    if t + 1 < NT:
                        final_exp(b, t + 1)
                    if t:
                        q, it = t - 1, b * NT + t - 1
                        n = t * P
                        for h in range(HEADS):
                            act.wait_ge(s["neg_done"], it * HEADS + h + 1)
                            if h >= 2:
                                act.wait_ge(s["turned_done"], it * HEADS + h - 1)
                            base = (h % 2) * 2 * BANK
                            if q == 0:
                                dst, src = probs[:, h % 2, 0:P], p_s[0:P, base:base + P]
                            else:
                                dst = probs[:, h % 2, 0:n].rearrange("p (h n) -> p h n", h=2)
                                src = ap(p_s, 0, P, base, [[BANK, 2], [1, n // 2]])
                            act.activation(dst, src, ACT.Exp, bias=top[:, q, h:h + 1],
                                           accum_out=total[:, q, h:h + 1]).then_inc(s["exp_done"], 1)
                            act.wait_ge(s["turned_done"], it * HEADS + h + 1)
                            if h >= 2:
                                act.wait_ge(s["pv_done"], it * HEADS + h - 1)
                            k4 = min(t, 4)
                            last = act.activation(turned[:, h % 2, 0:k4, :],
                                                  p_t[0:P, 0:k4 * P].rearrange("p (k q) -> p k q", q=P), ACT.Copy)
                            if t > 4:
                                last = act.activation(turned[:, h % 2, 4:t, :],
                                                      p_t[0:P, BANK:BANK + (t - 4) * P].rearrange("p (k q) -> p k q", q=P), ACT.Copy)
                            last.then_inc(s["turned_copied"], 1)
                        act.wait_ge(s["ot_done"], it + 1)
                        act.activation(ot[:], p_t[:, 0:4 * P].rearrange("p (a q) -> p a q", a=4), ACT.Copy).then_inc(s["ot_ready"], 1)

def audio_tower(nc, out, x, tok, l1, ffn, density, memory):
    with ExitStack() as ctx:
        H = ctx.enter_context(nc.sbuf_tensor("H", [P, TILES, C], F32))
        ident = ctx.enter_context(nc.sbuf_tensor("ident", [128, 128], F32))
        out_written = ctx.enter_context(nc.semaphore("out_written"))
        local_attention(nc, H, ident, x, *tok)
        l1_attention(nc, H, ident, *l1)
        expert_ffn(nc, H, ident, *ffn)
        density_attention(nc, H, ident, *density)
        memory_attention(nc, H, ident, *memory)
        with nc.Block() as block:
            @block.sync
            def _(sp):
                sp.dma_start(out.rearrange("b (t p) c -> p (b t) c", p=P), H[:]).then_inc(out_written, 16)
                sp.wait_ge(out_written, 16)


STAGE_INPUTS = [
    ("L0_tok_W_qry", "L0_tok_W_key", "L0_tok_v", "L0_tok_b"),
    ("L0_attn_wqv_w", "L0_attn_wqv_b", "L0_attn_wk", "L0_attn_fanin_w", "L0_attn_fanin_b"),
    ("L0_ffn_gamma", "L0_ffn_beta", "L0_ffn_Wr", "L0_ffn_br", "L0_ffn_W1", "L0_ffn_b1", "L0_ffn_W2", "L0_ffn_b2"),
    ("L1_attn_w_qkv", "L1_attn_w_proj", "L1_attn_b_proj"),
    ("L1_ffn_Wq_pk", "L1_ffn_pk_keys", "L1_ffn_Wq", "L1_ffn_table", "L1_ffn_Wo")]


def kernel(**inputs):
    import concourse.bacc as bacc
    from concourse.bass_utils import run_bass_kernel_spmd

    inputs = dict(inputs)
    inputs["L1_ffn_table"] = np.concatenate([np.asarray(inputs.pop("L1_ffn_keys_table")),
                                             np.asarray(inputs.pop("L1_ffn_values_table"))], axis=1)
    nc = bacc.Bacc("TRN2", target_bir_lowering=False, num_devices=1)
    arrays, drams = {}, {}
    for name in ["x"] + [n for names in STAGE_INPUTS for n in names]:
        a = np.ascontiguousarray(inputs[name])
        arrays[f"in_{name}_dram"] = a
        drams[name] = nc.dram_tensor(f"in_{name}_dram", a.shape, mybir.dt.from_np(a.dtype), kind="ExternalInput").ap()
    out = nc.dram_tensor("out_dram", (N_B, W, C), F32, kind="ExternalOutput").ap()
    audio_tower(nc, out, drams["x"], *[[drams[n] for n in names] for names in STAGE_INPUTS])
    r = run_bass_kernel_spmd(nc, [arrays], core_ids=[0])
    return r.results[0]["out_dram"]
```

```python
from contextlib import ExitStack

import numpy as np

import concourse.bass as bass
from concourse import mybir

F32 = mybir.dt.float32
U32 = mybir.dt.uint32
ALU = mybir.AluOpType
ACT = mybir.ActivationFunctionType
AX_X = mybir.AxisListType.X

N_B, L_IN, C, WIN = 8, 750, 64, 9
W = L_IN - WIN + 1
P = 106
NT = W // P
TILES = N_B * NT
HALF = W // 2
BANK = 512
assert NT * P == W


def ap(t, p0, n_p, offset, dims):
    whole = t[:]
    row = whole.ap[0][0]
    return bass.AP(whole.tensor, p0 * row + offset, [[row, n_p]] + [list(d) for d in dims])


def banks(t, n_p, cols=HALF, p0=0):
    return ap(t, p0, n_p, 0, [[BANK, 2], [1, cols]])


class Chain:

    def __init__(self, eng, sem, base=0):
        self.eng, self.sem, self.base, self.n = eng, sem, base, 0

    def __call__(self, instruction):
        self.n += 1
        instruction.then_inc(self.sem, 1)
        self.eng.wait_ge(self.sem, self.base + self.n)


def newton_rsqrt(eng, link, var, root, rstd, tmp):
    link(eng.reciprocal(rstd, root))
    link(eng.tensor_tensor(tmp, rstd, rstd, ALU.mult))
    link(eng.tensor_tensor(tmp, tmp, var, ALU.mult))
    link(eng.tensor_scalar(tmp, tmp, -0.5, 1.5, ALU.mult, ALU.add))
    link(eng.tensor_tensor(rstd, rstd, tmp, ALU.mult))


class Memory:

    def __init__(self, nc, ctx, stage):
        self.nc, self.ctx, self.stage = nc, ctx, stage

    def sb(self, name, shape, dt=F32):
        return self.ctx.enter_context(self.nc.sbuf_tensor(f"{self.stage}_{name}", shape, dt))

    def ps(self, name, shape, dt=F32):
        return self.ctx.enter_context(self.nc.psum_tensor(f"{self.stage}_{name}", shape, dt))

    def sem(self, name):
        return self.ctx.enter_context(self.nc.semaphore(f"{self.stage}_{name}"))


def local_attention(nc, H, ident, x, w_qry, w_key, v, b):
    PAIRS = N_B // 2
    CHUNK, CHUNKS = 125, L_IN // 125
    with ExitStack() as ctx:
        m = Memory(nc, ctx, "tok")
        frames = m.sb("frames", [CHUNK, CHUNKS, 2 * C])
        windows = m.sb("windows", [P, 2 * NT, WIN * C])
        wkey2 = m.sb("wkey2", [128, 128])
        wqry2 = m.sb("wqry2", [128, 128])
        v2 = m.sb("v2", [128, 2])
        b2 = m.sb("b2", [128, 1])
        xt = m.sb("xt", [128, L_IN])
        qry = m.sb("qry", [128, W])
        key = m.sb("key", [128, L_IN])
        arg = m.sb("arg", [128, WIN, W])
        soft = m.sb("soft", [P, 2 * NT, WIN])
        top = m.sb("top", [P, 2 * NT])
        total = m.sb("total", [P, 2 * NT])
        p_xt = m.ps("p_xt", [128, 2 * BANK])
        p_key = m.ps("p_key", [128, 2 * BANK])
        p_qry = m.ps("p_qry", [128, 2 * BANK])
        p_score = m.ps("p_score", [P, BANK])
        weights_in, frames_in, windows_in = m.sem("weights_in"), m.sem("frames_in"), m.sem("windows_in")
        blocks_zero, id_ready = m.sem("blocks_zero"), m.sem("id_ready")
        xt_done, xt_copied, proj_done, key_copied = m.sem("xt_done"), m.sem("xt_copied"), m.sem("proj_done"), m.sem("key_copied")
        arg_ready, tanh_done, score_done, centred = m.sem("arg_ready"), m.sem("tanh_done"), m.sem("score_done"), m.sem("centred")
        exp_done, windows_used, chain = m.sem("exp_done"), m.sem("windows_used"), m.sem("chain")
        CHAIN = 7
        block = ctx.enter_context(nc.Block())

        @block.gpsimd
        def _(pool):
            pool.memset(ident[:], 0.0).then_inc(id_ready, 1)
            pool.wait_ge(id_ready, 1)
            pool.affine_select(out=ident[:], in_=ident[:], compare_op=ALU.not_equal, fill=1.0, base=0,
                               pattern=[[-1, 128]], channel_multiplier=1).then_inc(id_ready, 1)

        @block.sync
        def _(sp):
            sp.wait_ge(blocks_zero, 3)
            for j in range(2):
                s = slice(C * j, C * j + C)
                sp.dma_start(wkey2[s, s], w_key).then_inc(weights_in, 16)
                sp.dma_start(wqry2[s, s], w_qry).then_inc(weights_in, 16)
                sp.dma_start(v2[s, j:j + 1], v.rearrange("(c a) -> c a", a=1)).then_inc(weights_in, 16)
                sp.dma_start(b2[s, :], b.rearrange("(c a) -> c a", a=1)).then_inc(weights_in, 16)
            for i in range(PAIRS):
                if i:
                    sp.wait_ge(xt_done, i)
                for j in range(2):
                    sp.dma_start(frames[:, :, C * j:C * j + C],
                                 x[2 * i + j].rearrange("(c p) d -> p c d", p=CHUNK)).then_inc(frames_in, 16)
                if i:
                    sp.wait_ge(windows_used, i)
                for j in range(2):
                    src = x[2 * i + j]
                    src = bass.AP(src.tensor, src.offset, [[C, P], [P * C, NT], [1, WIN * C]])
                    sp.dma_start(windows[:, NT * j:NT * j + NT, :], src).then_inc(windows_in, 16)

        @block.tensor
        def _(pe):
            pe.wait_ge(id_ready, 2)
            pe.wait_ge(weights_in, 8 * 16)
            with pe.Fori(0, PAIRS) as i:
                pe.wait_ge(frames_in, i * 32 + 32)
                for c in range(CHUNKS):
                    col = (c // 4) * BANK + (c % 4) * CHUNK
                    last = pe.transpose(p_xt[:, col:col + CHUNK], frames[:, c, :], ident[0:CHUNK, 0:CHUNK])
                last.then_inc(xt_done, 1)
                pe.wait_ge(xt_copied, i * 2 + 2)
                for h in range(2):
                    pe.matmul(p_key[:, h * BANK:h * BANK + L_IN // 2], wkey2[:],
                              xt[:, h * (L_IN // 2):(h + 1) * (L_IN // 2)], start=True, stop=True)
                for h in range(2):
                    a = WIN // 2 + h * HALF
                    last = pe.matmul(p_qry[:, h * BANK:h * BANK + HALF], wqry2[:], xt[:, a:a + HALF],
                                     start=True, stop=True)
                last.then_inc(proj_done, 1)
                for s in range(WIN):
                    pe.wait_ge(tanh_done, i * WIN + s + 1)
                    for t in range(NT):
                        out = ap(p_score, 0, P, t * WIN + s, [[NT * WIN, 2]])
                        last = pe.matmul(out, arg[:, s, t * P:(t + 1) * P], v2[:], start=True, stop=True)
                last.then_inc(score_done, 1)

        @block.vector
        def _(dve):
            dve.memset(wkey2[:], 0.0).then_inc(blocks_zero, 1)
            dve.memset(wqry2[:], 0.0).then_inc(blocks_zero, 1)
            dve.memset(v2[:], 0.0).then_inc(blocks_zero, 1)
            with dve.Fori(0, PAIRS) as i:
                link = Chain(dve, chain, i * CHAIN)
                dve.wait_ge(xt_done, i + 1)
                for h, n in ((0, 4), (1, 2)):
                    dve.tensor_copy(xt[:, 4 * h * CHUNK:4 * h * CHUNK + n * CHUNK],
                                    p_xt[:, h * BANK:h * BANK + n * CHUNK]).then_inc(xt_copied, 1)
                dve.wait_ge(proj_done, i + 1)
                link(dve.tensor_copy(key[:].rearrange("p (h n) -> p h n", h=2), banks(p_key, 128, L_IN // 2)))
                link(dve.tensor_copy(qry[:].rearrange("p (h n) -> p h n", h=2), banks(p_qry, 128)))
                for s in range(WIN):
                    dve.tensor_tensor(arg[:, s, :], qry[:], key[:, s:s + W], ALU.add).then_inc(arg_ready, 1)
                dve.wait_ge(score_done, i + 1)
                score = p_score[:, 0:2 * NT * WIN].rearrange("p (t s) -> p t s", s=WIN)
                link(dve.tensor_reduce(top[:], score, AX_X, ALU.max))
                dve.tensor_tensor(soft[:], score, top[:].unsqueeze(2).to_broadcast([P, 2 * NT, WIN]),
                                  ALU.subtract).then_inc(centred, 1)
                dve.wait_ge(exp_done, i + 1)
                link(dve.tensor_reduce(total[:], soft[:], AX_X, ALU.add))
                link(dve.reciprocal(total[:], total[:]))
                link(dve.tensor_tensor(soft[:], soft[:], total[:].unsqueeze(2).to_broadcast([P, 2 * NT, WIN]),
                                       ALU.mult))
                dve.wait_ge(windows_in, i * 32 + 32)
                rows = windows[:].rearrange("p t (s c) -> p (t s) c", c=C)
                link(dve.tensor_tensor(rows, rows, soft[:].rearrange("p t s -> p (t s)").unsqueeze(2)
                                       .to_broadcast([P, 2 * NT * WIN, C]), ALU.mult))
                dve.tensor_reduce(H[:, bass.ds(i * 2 * NT, 2 * NT), :],
                                  windows[:].rearrange("p t (s c) -> p t c s", c=C), AX_X,
                                  ALU.add).then_inc(windows_used, 1)
                assert link.n == CHAIN

        @block.scalar
        def _(act):
            act.wait_ge(weights_in, 8 * 16)
            with act.Fori(0, PAIRS) as i:
                for s in range(WIN):
                    act.wait_ge(arg_ready, i * WIN + s + 1)
                    act.activation(arg[:, s, :], arg[:, s, :], ACT.Tanh, bias=b2[:, 0:1]).then_inc(tanh_done, 1)
                act.wait_ge(centred, i + 1)
                act.activation(soft[:], soft[:], ACT.Exp).then_inc(exp_done, 1)

HEADS = 8
GROUPS = 4
TILE_PAIRS = P // 2
ROUNDS = -(-TILE_PAIRS // GROUPS)
PAIR_LIST = [(s, g, s - (g > 0)) for s in range(ROUNDS) for g in range(GROUPS)
             if s >= (g > 0) and GROUPS * (s - (g > 0)) + g < TILE_PAIRS]
CORRECTED = range(1, GROUPS)
assert len(PAIR_LIST) == TILE_PAIRS and all(s < ROUNDS for s, _, _ in PAIR_LIST)


def on_vector(r, g):
    return g >= 2 or (g == 1 and r in (1, 4, 7))


def group_rows(g):
    return 2 * len([1 for _, gg, _ in PAIR_LIST if gg == g])


V_PAIRS = sum(on_vector(r, g) for _, g, r in PAIR_LIST)
A_PAIRS = TILE_PAIRS - V_PAIRS
V_RING, A_RING = 7, 8
assert NT * V_PAIRS % V_RING == 0 and NT * A_PAIRS % A_RING == 0
ROUNDS_HEAD = NT * ROUNDS
SIDE_ROUNDS = (4, 5, 6, 7, 8, 9, 10)


def pairs_of(s, vector):
    return [(g, r) for ss, g, r in PAIR_LIST if ss == s and on_vector(r, g) == vector]


def tiles_upto(t, s, vector):
    per = V_PAIRS if vector else A_PAIRS
    return per * t + sum(len(pairs_of(ss, vector)) for ss in range(s + 1))


def round_of(n, vector):
    per = V_PAIRS if vector else A_PAIRS
    back, n = divmod(n, per * NT)
    own = [s for s in range(ROUNDS) for _ in pairs_of(s, vector)]
    return back * ROUNDS_HEAD + (n // per) * ROUNDS + own[n % per]


def permuted(dst, src, n_p, to_rows, tiles, dst_step, src_step, p0=0):
    out = []
    for g in range(GROUPS):
        n = group_rows(g) // 2
        for r0, k in ((0, ROUNDS - 1), (ROUNDS - 1, n - ROUNDS + 1)):
            if k <= 0:
                continue
            nat, row = 2 * GROUPS * r0 + 2 * g, 32 * g + 2 * r0
            dims = lambda step, s: [[step, tiles], [s, k], [1, 2]]
            natural, rows = (nat, 2 * GROUPS), (row, 2)
            (d0, ds), (s0, ss) = (rows, natural) if to_rows else (natural, rows)
            out.append((ap(dst, p0, n_p, d0, dims(dst_step, ds)), ap(src, p0, n_p, s0, dims(src_step, ss))))
    return out


def l1_attention(nc, H, ident, wqv_w, wqv_b, wk, fanin_w, fanin_b, batches=N_B):
    FEATURES = 3 * HEADS * C
    CH = FEATURES // 128
    with ExitStack() as ctx:
        m = Memory(nc, ctx, "l1")
        sel1 = m.sb("sel1", [128, ROUNDS, 32])
        sel2 = m.sb("sel2", [128, ROUNDS, 32])
        rows_mask = m.sb("rows_mask", [128, 128])
        exp_mask_row = m.sb("exp_mask_row", [1, 128])
        exp_mask = m.sb("exp_mask", [128, 1])
        zeros = m.sb("zeros", [128, C])
        wqv_in = m.sb("wqv_in", [128, CH, C])
        fanin_in = m.sb("fanin_in", [C, C])
        wq1 = m.sb("wq1", [C + 1, HEADS, C])
        wqsum = m.sb("wqsum", [C + 1, HEADS])
        wv = m.sb("wv", [C + 1, 2 * HEADS * C])
        wfan = m.sb("wfan", [C + 1, C])
        wkc = m.sb("wkc", [128, HEADS])
        xn = m.sb("xn", [P, NT, C])
        stat = m.sb("stat", [P, 5, NT])
        xdup = m.sb("xdup", [P, NT, 2, C])
        xt2 = m.sb("xt2", [128, W])
        xt1 = m.sb("xt1", [C + 1, W])
        xtp = m.sb("xtp", [C + 1, NT, 128])
        keys = m.sb("keys", [128, HEADS, W])
        qcol = m.sb("qcol", [128, HEADS, NT * TILE_PAIRS])
        qbias = m.sb("qbias", [128, NT, HEADS])
        vf = m.sb("vf", [128, NT, HEADS, C + 1])
        vb = m.sb("vb", [P, NT, HEADS, C])
        wkneg = m.sb("wkneg", [128, 128])
        diff_v = m.sb("diff_v", [128, V_RING, W])
        diff_a = m.sb("diff_a", [128, A_RING, W])
        expd = m.sb("expd", [128, NT, W])
        expt = m.sb("expt", [P, NT, NT, 128])
        rz = m.sb("rz", [P, NT])
        vbz = m.sb("vbz", [P, NT, C])
        scaled = m.sb("scaled", [P, NT, C])
        o_fwd = m.sb("o_fwd", [P, NT, C])
        o_back = m.sb("o_back", [128, 4 * P])
        gate = m.sb("gate", [P, NT, C])
        yt = m.sb("yt", [C + 1, W])
        p_dist = m.ps("p_dist", [128, 4 * BANK])
        p_fwd = m.ps("p_fwd", [128, BANK])
        p_back = m.ps("p_back", [128, BANK])
        p_turn = m.ps("p_turn", [128, 2 * BANK])
        names = ("loaded consts ready_w turned_w xn_ready var_ready root_ready xt_done "
                 "xt_ready q_done q_even q_odd v_done v_copied_v v_copied_a qsum_done batch_ready keys_ready "
                 "wkneg_ready tiles_v tiles_a rounds exps posts turned_out vbz_ready back_done "
                 "back_copied perm_done o_ready gate_exp y_ready yt_done yt_ready fan_done "
                 "chain_w chain_b chain_h chain_e ").split()
        s = {n: m.sem(n) for n in names}
        q_copied = s["q_even"], s["q_odd"]
        EXP_CREDIT = 2
        BACK_PARTS = ((0, 0, 4), (C, 4, NT - 4))
        BACK_VIEWS = [v for p0, _, n in BACK_PARTS for v in permuted(o_back, p_back, C, False, n, P, 128, p0=p0)]
        BACK_COPIES = len(BACK_VIEWS)
        block = ctx.enter_context(nc.Block())

        @block.sync
        def _(sp):
            sp.dma_start(wqv_in[:], wqv_w.rearrange("(c p) d -> p c d", p=128)).then_inc(s["loaded"], 16)
            sp.dma_start(fanin_in[:], fanin_w).then_inc(s["loaded"], 16)
            for j in range(2):
                sp.dma_start(wkc[C * j:C * j + C, :], wk.rearrange("h c -> c h"), allow_slow_non_contiguous=True).then_inc(s["loaded"], 16)
            sp.dma_start(wq1[C:C + 1, :, :],
                         wqv_b[0:HEADS * C].rearrange("(a h c) -> a h c", a=1, h=HEADS)).then_inc(s["loaded"], 16)
            sp.dma_start(wv[C:C + 1, :], wqv_b[HEADS * C:FEATURES].rearrange("(a n) -> a n", a=1)).then_inc(s["loaded"], 16)
            sp.dma_start(wfan[C:C + 1, :], fanin_b.rearrange("(a n) -> a n", a=1)).then_inc(s["loaded"], 16)

        LOADED = 7 * 16

        @block.tensor
        def _(pe):
            pe.wait_ge(s["loaded"], LOADED)
            for c in range(CH):
                col = (c // 4) * BANK + (c % 4) * 128
                pe.transpose(p_dist[0:C, col:col + 128], wqv_in[:, c, :], ident[:])
            pe.transpose(p_turn[0:C, 0:C], fanin_in[:], ident[0:C, 0:C])
            pe.wait_ge(s["consts"], 1)
            pe.matmul(p_back[:, 0:1], exp_mask_row[:], ident[0:1, 0:1], start=True, stop=True)
            pe.matmul(p_fwd[:, 0:1], xtp[C:C + 1, 0, :], xt1[C:C + 1, 0:1], start=True, stop=True).then_inc(s["turned_w"], 1)
            pe.sem_inc(s["rounds"], ROUNDS_HEAD)
            pe.sem_inc(s["posts"], NT)
            pe.wait_ge(s["ready_w"], 1)

            def distances(it, h, t, first):
                if t == 0:
                    pe.wait_ge(s["exps"], it * NT + EXP_CREDIT)
                    pe.wait_ge(s["wkneg_ready"], it + 1)
                elif t >= 2:
                    pe.wait_ge(s["exps"], it * NT + t - 1 + EXP_CREDIT)
                base = (t % 2) * 2 * BANK
                nv, na = tiles_upto(t, -1, True), tiles_upto(t, -1, False)
                for r in range(ROUNDS):
                    products = {}
                    for g, pair in pairs_of(r, True):
                        products[g] = sel2[:, pair, :], diff_v[:, nv % V_RING, :], False
                        nv += 1
                    for g, pair in pairs_of(r, False):
                        products[g] = sel1[:, pair, :], diff_a[:, na % A_RING, :], g == 0 and pair == 0
                        na += 1
                    if r == 0:
                        for g in CORRECTED:
                            products[g] = wkneg[:, 32 * g:32 * g + 32], xt2[:], True
                    if pairs_of(r, True):
                        pe.wait_ge(s["tiles_v"], it * (NT * V_PAIRS) + nv)
                    if pairs_of(r, False):
                        pe.wait_ge(s["tiles_a"], it * (NT * A_PAIRS) + na)
                    for half in range(2):
                        for g in sorted(products):
                            weights, tile, is_first = products[g]
                            last = pe.matmul(p_dist[32 * g:32 * g + 32, base + half * BANK:base + half * BANK + HALF],
                                             weights, tile[:, half * HALF:(half + 1) * HALF], start=is_first,
                                             stop=(r == ROUNDS - 1), skip_group_check=True)
                    last.then_inc(s["rounds"], 1)
                    if r in SIDE_ROUNDS:
                        k = SIDE_ROUNDS.index(r)
                        if t == 0 and not first:
                            forward(it - 1, h - 1, NT - 1, k)
                        if t == 1 and not first:
                            backward(it - 1, k)
                        if t >= 1:
                            forward(it, h, t - 1, k)

            def forward(it, h, t, k):
                if k == 0:
                    pe.wait_ge(s["exps"], it * NT + t + 1 + EXP_CREDIT)
                    pe.wait_ge(s["turned_out"], it * (2 * NT) + 2 * t + 2)
                pe.matmul(p_fwd[0:P, k * (C + 1):(k + 1) * (C + 1)], expd[:, t, k * P:(k + 1) * P],
                          vf[:, t, h, :], start=(t == 0 and k == 0), stop=(t == NT - 1), skip_group_check=True)
                col = (k // 4) * BANK + (k % 4) * 128
                last = pe.transpose(p_turn[0:P, col:col + 128], expd[:, t, k * P:(k + 1) * P], ident[:])
                if k == NT - 1:
                    last.then_inc(s["posts"], 1)

            def backward(it, k):
                if k == 0:
                    pe.wait_ge(s["vbz_ready"], it + 1)
                    pe.wait_ge(s["turned_out"], it * (2 * NT) + 2 * NT + 2)
                for p0, t0, n in BACK_PARTS:
                    last = pe.matmul(p_back[p0:p0 + C, 0:n * 128], vbz[:, k, :],
                                     expt[:, k, t0:t0 + n, :].rearrange("p t q -> p (t q)"),
                                     start=False, stop=False, skip_group_check=True)
                if k == NT - 1:
                    last.then_inc(s["back_done"], 1)

            def head(it, h, first):
                for t in range(NT):
                    distances(it, h, t, first)

            with pe.Fori(0, batches) as b:
                pe.wait_ge(s["xn_ready"], b + 1)
                for t in range(NT):
                    col = (t // 4) * BANK + (t % 4) * P
                    last = pe.transpose(p_dist[:, col:col + P], xdup[:, t, :, :].rearrange("p a c -> p (a c)"),
                                        ident[0:P, 0:P])
                last.then_inc(s["xt_done"], 1)
                pe.wait_ge(s["xt_ready"], b + 1)
                for h in range(HEADS):
                    if h >= 4:
                        pe.wait_ge(q_copied[h % 2], b * (HEADS // 2) + h // 2 - 1)
                    for odd in range(2):
                        last = pe.matmul(p_dist[C * odd:C * odd + C, (h % 4) * BANK:(h % 4) * BANK + HALF], wq1[:, h, :],
                                         ap(xt1, 0, C + 1, odd, [[2, HALF]]), start=True, stop=True)
                    last.then_inc(s["q_done"], 1)
                for t in range(NT):
                    last = pe.matmul(p_fwd[:, t * HEADS:(t + 1) * HEADS], xtp[:, t, :], wqsum[:], start=True, stop=True)
                last.then_inc(s["qsum_done"], 1)
                for copied in q_copied:
                    pe.wait_ge(copied, (b + 1) * (HEADS // 2))
                for t in range(NT):
                    if t >= 2:
                        pe.wait_ge(s["v_copied_a"], b * NT + t - 1)
                        pe.wait_ge(s["v_copied_v"], b * NT + t - 1)
                    base = (t % 2) * 2 * BANK
                    pe.matmul(p_dist[:, base:base + BANK], xtp[:, t, :], wv[:, 0:HEADS * C], start=True, stop=True)
                    pe.matmul(p_dist[0:P, base + BANK:base + 2 * BANK], xt1[:, t * P:(t + 1) * P],
                              wv[:, HEADS * C:2 * HEADS * C], start=True, stop=True).then_inc(s["v_done"], 1)
                pe.wait_ge(s["v_copied_a"], b * NT + NT)
                pe.wait_ge(s["v_copied_v"], b * NT + NT)
                pe.wait_ge(s["batch_ready"], b + 1)
                for p0, _, n in BACK_PARTS:
                    pe.matmul(p_back[p0:p0 + C, 0:n * 128], zeros[:], keys[:, 0, 0:n * 128], start=True, stop=False,
                              skip_group_check=True)
                head(b * HEADS, 0, True)
                with pe.Fori(1, HEADS) as h:
                    head(b * HEADS + h, h, False)
                for k in range(NT):
                    forward(b * HEADS + HEADS - 1, HEADS - 1, NT - 1, k)
                for k in range(NT):
                    backward(b * HEADS + HEADS - 1, k)
                pe.wait_ge(s["back_copied"], b * BACK_COPIES + BACK_COPIES)
                for t in range(4):
                    n = 128 if t + 4 < NT else C
                    last = pe.matmul(p_fwd[0:P, t * 128:t * 128 + n], o_back[0:n, t * P:(t + 1) * P], ident[0:n, 0:n],
                                     start=True, stop=True)
                last.then_inc(s["perm_done"], 1)
                pe.wait_ge(s["y_ready"], b + 1)
                turn_tiles(pe, p_turn, gate, ident).then_inc(s["yt_done"], 1)
                pe.wait_ge(s["yt_ready"], b + 1)
                for t in range(NT):
                    last = pe.matmul(p_back[0:P, t * C:(t + 1) * C], yt[:, t * P:(t + 1) * P], wfan[:], start=True, stop=True)
                last.then_inc(s["fan_done"], 1)

        @block.vector
        def _(dve):
            link = Chain(dve, s["chain_w"])
            link(dve.memset(sel1[:], 0.0))
            for t_, v_ in ((sel1, 1.0), (sel2, 2.0)):
                if t_ is sel2:
                    link(dve.memset(sel2[:], 0.0))
                for hf in range(2):
                    link(dve.memset(ap(t_, C * hf, C, hf, [[34, ROUNDS]]), v_))
            link(dve.memset(rows_mask[:], 0.0))
            link(dve.memset(wkneg[:], 0.0))
            link(dve.memset(exp_mask_row[:], 0.0))
            for g in CORRECTED:
                mine = [r for r in range(group_rows(g) // 2) if on_vector(r, g)]
                assert mine == list(range(mine[0], mine[-1] + 1, mine[1] - mine[0]))
                rows = 32 * g + 2 * mine[0], [[2 * (mine[1] - mine[0]), len(mine)], [1, 2]]
                link(dve.memset(ap(rows_mask, 0, 128, *rows), -1.0))
                link(dve.memset(ap(exp_mask_row, 0, 1, *rows), -0.125))
            link(dve.memset(zeros[:], 0.0))
            link(dve.memset(xt1[C:C + 1, :], 1.0))
            link(dve.memset(yt[C:C + 1, :], 1.0))
            link(dve.memset(xtp[:], 0.0))
            ones = permuted(xtp, xt1, 1, True, NT, 128, P, p0=C)
            for dst, src in ones:
                link(dve.tensor_copy(dst, src))
            dve.nop().then_inc(s["consts"], 1)
            dve.wait_ge(s["turned_w"], 1)
            w3 = [ap(p_dist, 0, C, k * BANK, [[C, HEADS], [1, C]]) for k in range(3)]
            link(dve.tensor_copy(wq1[0:C, :, :], w3[0]))
            for k in range(2):
                link(dve.tensor_copy(wv[0:C, k * BANK:(k + 1) * BANK], p_dist[0:C, (k + 1) * BANK:(k + 2) * BANK]))
            link(dve.tensor_copy(wfan[0:C, :], p_turn[0:C, 0:C]))
            link(dve.tensor_copy(exp_mask[:], p_back[:, 0:1]))
            link(dve.tensor_copy(ap(vf, 0, 128, C, [[C + 1, NT * HEADS]]), p_fwd[:, 0:1].to_broadcast([128, NT * HEADS])))
            dve.wait_ge(s["loaded"], LOADED)
            link(dve.tensor_reduce(wqsum[:], wq1[:], AX_X, ALU.add))
            dve.nop().then_inc(s["ready_w"], 1)
            dve.sem_inc(s["turned_out"], 2)

            def turned_copy(it, t):
                dve.wait_ge(s["posts"], it * NT + t + 1 + NT)
                for k0, n in ((0, 4), (4, 3)):
                    dve.tensor_copy(expt[:, k0:k0 + n, t, :],
                                    ap(p_turn, 0, P, (k0 // 4) * BANK, [[128, n], [1, 128]])).then_inc(s["turned_out"], 1)

            def normalise(it, h, link):
                z = ap(p_fwd, 0, P, C, [[C + 1, NT]])
                link(dve.tensor_scalar(rz[:], z, 1.0, None, ALU.add))
                link(dve.reciprocal(rz[:], rz[:]))
                wide = rz[:].unsqueeze(2).to_broadcast([P, NT, C])
                link(dve.tensor_tensor(scaled[:], ap(p_fwd, 0, P, 0, [[C + 1, NT], [1, C]]), wide, ALU.mult))
                link(dve.tensor_tensor(o_fwd[:], o_fwd[:], scaled[:], ALU.add))
                dve.tensor_tensor(vbz[:], vb[:, :, h, :], wide, ALU.mult).then_inc(s["vbz_ready"], 1)

            HEAD_CHAIN = 4

            def head(it, h, first):
                dve.wait_ge(s["rounds"], it * ROUNDS_HEAD + ROUNDS_HEAD - ROUNDS + 1)
                dve.tensor_scalar(wkneg[0:C, :], rows_mask[0:C, :], wkc[0:C, bass.ds(h, 1)], None,
                                  ALU.mult).then_inc(s["wkneg_ready"], 1)
                for t in range(NT):
                    n = tiles_upto(t, -1, True)
                    for r in range(ROUNDS):
                        gs = pairs_of(r, True)
                        if gs:
                            dve.wait_ge(s["rounds"], it * ROUNDS_HEAD + round_of(n + len(gs) - 1 - V_RING, True) + 1 + ROUNDS_HEAD)
                        for g, nth in gs:
                            pair = TILE_PAIRS * t + GROUPS * nth + g
                            dve.tensor_scalar(diff_v[:, n % V_RING, :], keys[:, h, :], qcol[:, h, pair:pair + 1],
                                              0.0, ALU.subtract, ALU.max).then_inc(s["tiles_v"], 1)
                            n += 1
                        if r == 1:
                            if t == 0 and not first:
                                turned_copy(it - 1, NT - 2)
                            if t == 1 and not first:
                                turned_copy(it - 1, NT - 1)
                                normalise(it - 1, h - 1, Chain(dve, s["chain_h"], (it - 1) * HEAD_CHAIN))
                            if t == 2 and not first:
                                dve.wait_ge(s["back_done"], it)
                            if t >= 2:
                                turned_copy(it, t - 2)

            BATCH_CHAIN = 23
            END_CHAIN = 6
            with dve.Fori(0, batches) as b:
                link = Chain(dve, s["chain_b"], b * BATCH_CHAIN)
                hb = H[:, bass.ds(b * NT, NT), :]
                mean, var, root, rstd, tmp = (stat[:, k, :] for k in range(5))
                wide = [P, NT, C]
                link(dve.tensor_reduce(mean, hb, AX_X, ALU.add))
                link(dve.tensor_scalar(mean, mean, 1.0 / C, None, ALU.mult))
                link(dve.tensor_tensor(xn[:], hb, mean.unsqueeze(2).to_broadcast(wide), ALU.subtract))
                link(dve.tensor_tensor(gate[:], xn[:], xn[:], ALU.mult))
                link(dve.tensor_reduce(var, gate[:], AX_X, ALU.add))
                dve.tensor_scalar(var, var, 1.0 / C, 1e-5, ALU.mult, ALU.add).then_inc(s["var_ready"], 1)
                dve.wait_ge(s["root_ready"], b + 1)
                newton_rsqrt(dve, link, var, root, rstd, tmp)
                link(dve.tensor_tensor(xn[:], xn[:], rstd.unsqueeze(2).to_broadcast(wide), ALU.mult))
                for j in range(2):
                    last = dve.tensor_copy(xdup[:, :, j, :], xn[:])
                    if j == 0:
                        link(last)
                last.then_inc(s["xn_ready"], 1)
                dve.wait_ge(s["xt_done"], b + 1)
                for k, (c0, n) in enumerate(((0, 4 * P), (4 * P, 3 * P))):
                    link(dve.tensor_copy(xt2[:, c0:c0 + n], p_dist[:, k * BANK:k * BANK + n]))
                    link(dve.tensor_copy(xt1[0:C, c0:c0 + n], p_dist[0:C, k * BANK:k * BANK + n]))
                for dst, src in permuted(xtp, xt1, C, True, NT, 128, P):
                    link(dve.tensor_copy(dst, src))
                dve.nop().then_inc(s["xt_ready"], 1)
                for h in range(HEADS):
                    dve.tensor_scalar(keys[:, h, :], xt2[:], wkc[:, h:h + 1], None, ALU.mult).then_inc(s["keys_ready"], 1)
                    if h % 2:
                        dve.wait_ge(s["q_done"], b * HEADS + h + 1)
                        dve.tensor_copy(qcol[:, h, :], p_dist[:, (h % 4) * BANK:(h % 4) * BANK + HALF]).then_inc(q_copied[1], 1)
                link(dve.memset(o_fwd[:], 0.0))
                dve.wait_ge(s["qsum_done"], b + 1)
                link(dve.tensor_scalar(qbias[:].rearrange("p t h -> p (t h)"), p_fwd[:, 0:NT * HEADS], exp_mask[:, 0:1],
                                       None, ALU.mult))
                for t in range(NT):
                    dve.wait_ge(s["v_done"], b * NT + t + 1)
                    base = (t % 2) * 2 * BANK + BANK
                    dve.tensor_copy(vb[:, t, :, :].rearrange("p h c -> p (h c)"), p_dist[0:P, base:base + BANK])\
                       .then_inc(s["v_copied_v"], 1)
                dve.wait_ge(s["keys_ready"], b * HEADS + HEADS)
                for copied in q_copied:
                    dve.wait_ge(copied, (b + 1) * (HEADS // 2))
                dve.nop().then_inc(s["batch_ready"], 1)
                assert link.n == BATCH_CHAIN, link.n

                head(b * HEADS, 0, True)
                with dve.Fori(1, HEADS) as h:
                    head(b * HEADS + h, h, False)
                it = b * HEADS + HEADS - 1
                turned_copy(it, NT - 2)
                turned_copy(it, NT - 1)
                normalise(it, HEADS - 1, Chain(dve, s["chain_h"], it * HEAD_CHAIN))
                dve.wait_ge(s["back_done"], it + 1)
                for dst, src in BACK_VIEWS:
                    dve.tensor_copy(dst, src).then_inc(s["back_copied"], 1)

                link = Chain(dve, s["chain_e"], b * END_CHAIN)
                dve.wait_ge(s["perm_done"], b + 1)
                for t0, n in ((0, 4), (4, NT - 4)):
                    last = dve.tensor_tensor(o_fwd[:, t0:t0 + n, :], o_fwd[:, t0:t0 + n, :],
                                             ap(p_fwd, 0, P, (t0 // 4) * C, [[2 * C, n], [1, C]]), ALU.add)
                last.then_inc(s["o_ready"], 1)
                dve.wait_ge(s["gate_exp"], b + 1)
                link(dve.tensor_scalar(gate[:], gate[:], 1.0, None, ALU.add))
                link(dve.reciprocal(gate[:], gate[:]))
                dve.tensor_tensor(gate[:], gate[:], o_fwd[:], ALU.mult).then_inc(s["y_ready"], 1)
                dve.wait_ge(s["yt_done"], b + 1)
                link(dve.tensor_copy(yt[0:C, 0:4 * P], p_turn[0:C, 0:4 * P]))
                link(dve.tensor_copy(yt[0:C, 4 * P:W], p_turn[0:C, BANK:BANK + 3 * P]))
                dve.nop().then_inc(s["yt_ready"], 1)
                dve.wait_ge(s["fan_done"], b + 1)
                link(dve.tensor_tensor(xn[:], xn[:], ap(p_back, 0, P, 0, [[C, NT], [1, C]]), ALU.add))
                link(dve.tensor_tensor(hb, hb, xn[:], ALU.add))
                assert link.n == END_CHAIN, link.n

        @block.scalar
        def _(act):
            act.sem_inc(s["exps"], EXP_CREDIT)

            def exponentials(it, h, t):
                act.wait_ge(s["rounds"], it * ROUNDS_HEAD + ROUNDS * (t + 1) + ROUNDS_HEAD)
                act.wait_ge(s["posts"], it * NT + t + 1)
                act.activation(expd[:, t, :].rearrange("p (h n) -> p h n", h=2),
                               ap(p_dist, 0, 128, (t % 2) * 2 * BANK, [[BANK, 2], [1, HALF]]), ACT.Exp,
                               bias=qbias[:, t, bass.ds(h, 1)], scale=-0.125).then_inc(s["exps"], 1)

            def head(it, h, first):
                for t in range(NT):
                    n = tiles_upto(t, -1, False)
                    for r in range(ROUNDS):
                        gs = pairs_of(r, False)
                        if gs:
                            act.wait_ge(s["rounds"], it * ROUNDS_HEAD + round_of(n + len(gs) - 1 - A_RING, False) + 1 + ROUNDS_HEAD)
                        for g, nth in gs:
                            pair = TILE_PAIRS * t + GROUPS * nth + g
                            act.activation(diff_a[:, n % A_RING, :], keys[:, h, :], ACT.Abs,
                                           bias=qcol[:, h, pair:pair + 1], scale=-1.0).then_inc(s["tiles_a"], 1)
                            n += 1
                        if r == 1 and (t or not first):
                            if t:
                                exponentials(it, h, t - 1)
                            else:
                                exponentials(it - 1, h - 1, NT - 1)

            with act.Fori(0, batches) as b:
                act.wait_ge(s["var_ready"], b + 1)
                act.activation(stat[:, 2, :], stat[:, 1, :], ACT.Sqrt).then_inc(s["root_ready"], 1)
                for h in range(0, HEADS, 2):
                    act.wait_ge(s["q_done"], b * HEADS + h + 1)
                    act.activation(qcol[:, h, :], p_dist[:, (h % 4) * BANK:(h % 4) * BANK + HALF], ACT.Copy)\
                       .then_inc(q_copied[0], 1)
                for t in range(NT):
                    act.wait_ge(s["v_done"], b * NT + t + 1)
                    base = (t % 2) * 2 * BANK
                    act.activation(vf[:, t, :, 0:C], ap(p_dist, 0, 128, base, [[C, HEADS], [1, C]]), ACT.Copy)\
                       .then_inc(s["v_copied_a"], 1)
                act.wait_ge(s["batch_ready"], b + 1)
                head(b * HEADS, 0, True)
                with act.Fori(1, HEADS) as h:
                    head(b * HEADS + h, h, False)
                exponentials(b * HEADS + HEADS - 1, HEADS - 1, NT - 1)
                act.wait_ge(s["o_ready"], b + 1)
                act.activation(gate[:], o_fwd[:], ACT.Exp, scale=-1.702).then_inc(s["gate_exp"], 1)

def norm_tiles(dve, link, hb, xn, square, stat, var_ready, root_ready, root_value):
    mean, var, root, rstd, tmp = (stat[:, k, :] for k in range(5))
    wide = list(hb.shape)
    link(dve.tensor_reduce(mean, hb, AX_X, ALU.add))
    link(dve.tensor_scalar(mean, mean, 1.0 / C, None, ALU.mult))
    link(dve.tensor_tensor(xn, hb, mean.unsqueeze(2).to_broadcast(wide), ALU.subtract))
    link(dve.tensor_tensor(square, xn, xn, ALU.mult))
    link(dve.tensor_reduce(var, square, AX_X, ALU.add))
    dve.tensor_scalar(var, var, 1.0 / C, 1e-5, ALU.mult, ALU.add).then_inc(var_ready, 1)
    dve.wait_ge(root_ready, root_value)
    newton_rsqrt(dve, link, var, root, rstd, tmp)
    link(dve.tensor_tensor(xn, xn, rstd.unsqueeze(2).to_broadcast(wide), ALU.mult))


NORM_CHAIN = 11


def turn_tiles(pe, dst, src, ident):
    for t in range(NT):
        col = (t // 4) * BANK + (t % 4) * P
        if t == 0:
            pe.matmul(dst[0:C, col:col + P], src[:, t, :], ident[0:P, 0:P], start=True, stop=True)
        else:
            last = pe.transpose(dst[0:C, col:col + P], src[:, t, :], ident[0:P, 0:P])
    return last


def turn_back(pe, dst, src, ident):
    for t in range(NT):
        last = pe.matmul(dst[0:P, t * C:(t + 1) * C], src[:, t * P:(t + 1) * P], ident[0:C, 0:C], start=True, stop=True)
    return last


def expert_ffn(nc, H, ident, gamma, beta, w_r, b_r, w_1, b_1, w_2, b_2, batches=N_B):
    E, HID = 8, 128
    with ExitStack() as ctx:
        m = Memory(nc, ctx, "moe")
        gb = m.sb("gb", [C, 2])
        wr = m.sb("wr", [C + 1, E])
        w1 = m.sb("w1", [C, E, HID])
        b1 = m.sb("b1", [HID, E])
        w2 = m.sb("w2", [HID, E, C])
        b2 = m.sb("b2", [NT * E, NT * C])
        weight_t = m.sb("weight_t", [NT * E, P])
        expert_ids = m.sb("expert_ids", [P, NT, E])
        ids_int = m.sb("ids_int", [P, NT, E], mybir.dt.int32)
        xn = m.sb("xn", [P, NT, C])
        square = m.sb("square", [P, NT, C])
        stat = m.sb("stat", [P, 5, NT])
        xt = m.sb("xt", [C + 1, W])
        logits = m.sb("logits", [P, NT, E])
        best = m.sb("best", [P, NT, 8])
        best_at = m.sb("best_at", [P, NT, 8], U32)
        pause = m.sb("pause", [P, 2])
        best_id = m.sb("best_id", [P, NT, 8])
        pw = m.sb("pw", [P, 4, NT])
        weight = m.sb("weight", [P, NT, E])
        weight2 = m.sb("weight2", [P, NT, E])
        hidden = m.sb("hidden", [HID, E, W])
        weighted = m.sb("weighted", [P, 2, E * C])
        y = m.sb("y", [P, NT, C])
        p_t = m.ps("p_t", [C, 2 * BANK])
        p_h = m.ps("p_h", [HID, 4 * BANK])
        p_y = m.ps("p_y", [P, 2 * BANK])
        BIAS_AFTER = 2
        names = ("loaded b2_zero weights_ready weights_turned weights_copied bias_done "
                 "ids_ready consts var_ready root_ready xn_ready xt_done xt_ready logits_done h_done gelu_done "
                 "y_done y_read pair_diff pair_exp chain_c chain_b").split()
        s = {n: m.sem(n) for n in names}
        block = ctx.enter_context(nc.Block())
        LOADED = (7 + NT) * 16

        @block.sync
        def _(sp):
            one = lambda v: v.rearrange("(a n) -> a n", a=1)
            col = lambda v: v.rearrange("(n a) -> n a", a=1)
            sp.dma_start(gb[:, 0:1], col(gamma)).then_inc(s["loaded"], 16)
            sp.dma_start(gb[:, 1:2], col(beta)).then_inc(s["loaded"], 16)
            sp.dma_start(wr[0:C, :], w_r).then_inc(s["loaded"], 16)
            sp.dma_start(wr[C:C + 1, :], one(b_r)).then_inc(s["loaded"], 16)
            sp.dma_start(w1[:], w_1.rearrange("e d h -> d e h")).then_inc(s["loaded"], 16)
            sp.dma_start(b1[:], b_1.rearrange("e h -> h e"), allow_slow_non_contiguous=True).then_inc(s["loaded"], 16)
            sp.dma_start(w2[:], w_2.rearrange("e h d -> h e d")).then_inc(s["loaded"], 16)
            sp.wait_ge(s["b2_zero"], 1)
            for t in range(NT):
                sp.dma_start(b2[t * E:(t + 1) * E, t * C:(t + 1) * C], b_2).then_inc(s["loaded"], 16)

        @block.gpsimd
        def _(pool):
            pool.iota(ids_int[:], [[0, NT], [1, E]], base=0, channel_multiplier=0).then_inc(s["ids_ready"], 1)

        @block.tensor
        def _(pe):
            pe.wait_ge(s["loaded"], LOADED)
            pe.wait_ge(s["consts"], 1)
            with pe.Fori(0, batches) as b:
                pe.wait_ge(s["xn_ready"], b + 1)
                turn_tiles(pe, p_t, xn, ident).then_inc(s["xt_done"], 1)
                pe.wait_ge(s["xt_ready"], b + 1)
                for t in range(NT):
                    last = pe.matmul(p_y[:, t * E:(t + 1) * E], xt[:, t * P:(t + 1) * P], wr[:], start=True, stop=True)
                last.then_inc(s["logits_done"], 1)
                for e in range(E):
                    if e >= 2:
                        pe.wait_ge(s["gelu_done"], b * E + e - 1)
                    for h in range(2):
                        a = (e % 2) * 2 * BANK + h * BANK
                        last = pe.matmul(p_h[:, a:a + HALF], w1[:, e, :], xt[0:C, h * HALF:(h + 1) * HALF],
                                         start=True, stop=True)
                    last.then_inc(s["h_done"], 1)
                pe.wait_ge(s["gelu_done"], b * E + E)
                for t in range(NT):
                    pe.wait_ge(s["y_read"], b * (NT + 1) + max(t, 1))
                    a = (t % 2) * BANK
                    for e in range(E):
                        last = pe.matmul(p_y[:, a + e * C:a + (e + 1) * C], hidden[:, e, t * P:(t + 1) * P], w2[:, e, :],
                                         start=True, stop=True)
                    last.then_inc(s["y_done"], 1)
                    if t == BIAS_AFTER:
                        pe.wait_ge(s["weights_ready"], b + 1)
                        pe.matmul(p_h[0:NT * E, 0:P], weight[:].rearrange("p t e -> p (t e)"), ident[0:P, 0:P],
                                  start=True, stop=True).then_inc(s["weights_turned"], 1)
                    if t == BIAS_AFTER + 2:
                        pe.wait_ge(s["weights_copied"], b + 1)
                        pe.matmul(p_h[0:P, BANK:BANK + NT * C], weight_t[:], b2[:], start=True, stop=True)\
                          .then_inc(s["bias_done"], 1)

        @block.vector
        def _(dve):
            link = Chain(dve, s["chain_c"])
            dve.memset(b2[:], 0.0).then_inc(s["b2_zero"], 1)
            dve.wait_ge(s["loaded"], LOADED)
            link(dve.memset(xt[C:C + 1, :], 1.0))
            dve.wait_ge(s["ids_ready"], 1)
            link(dve.tensor_copy(expert_ids[:], ids_int[:]))
            dve.nop().then_inc(s["consts"], 1)
            CHAIN = 2 * NORM_CHAIN + 2 * NT + 16
            with dve.Fori(0, batches) as b:
                link = Chain(dve, s["chain_b"], b * CHAIN)
                hb = H[:, bass.ds(b * NT, NT), :]
                norm_tiles(dve, link, hb, xn[:], square[:], stat, s["var_ready"], s["root_ready"], b * 2 + 1)
                norm_tiles(dve, link, xn[:], xn[:], square[:], stat, s["var_ready"], s["root_ready"], b * 2 + 2)
                dve.nop().then_inc(s["xn_ready"], 1)
                dve.wait_ge(s["xt_done"], b + 1)
                for k, (c0, n) in enumerate(((0, 4 * P), (4 * P, 3 * P))):
                    link(dve.tensor_scalar(xt[0:C, c0:c0 + n], p_t[:, k * BANK:k * BANK + n], gb[:, 0:1], gb[:, 1:2],
                                           ALU.mult, ALU.add))
                dve.nop().then_inc(s["xt_ready"], 1)
                dve.wait_ge(s["logits_done"], b + 1)
                link(dve.tensor_copy(logits[:].rearrange("p t e -> p (t e)"), p_y[:, 0:NT * E]))
                dve.nop().then_inc(s["y_read"], 1)
                dve.memset(pause[:, 0:1], 0.0)
                for t in range(NT):
                    best_one = dve.max(best[:, t, :], logits[:, t, :])
                link(best_one)
                dve.memset(pause[:, 1:2], 0.0)
                for t in range(NT):
                    best_one = dve.max_index(best_at[:, t, :], best[:, t, :], logits[:, t, :])
                link(best_one)
                dve.tensor_tensor(pw[:, 0, :], best[:, :, 1], best[:, :, 0], ALU.subtract).then_inc(s["pair_diff"], 1)
                link(dve.tensor_copy(best_id[:], best_at[:]))
                dve.wait_ge(s["pair_exp"], b + 1)
                link(dve.tensor_scalar(pw[:, 2, :], pw[:, 1, :], 1.0, None, ALU.add))
                link(dve.reciprocal(pw[:, 2, :], pw[:, 2, :]))
                link(dve.tensor_tensor(pw[:, 3, :], pw[:, 2, :], pw[:, 1, :], ALU.mult))
                for k, w_ in ((0, weight), (1, weight2)):
                    link(dve.tensor_tensor(w_[:], expert_ids[:], best_id[:, :, k:k + 1].to_broadcast([P, NT, E]), ALU.is_equal))
                for k, w_ in ((0, weight), (1, weight2)):
                    link(dve.tensor_tensor(w_[:], w_[:], pw[:, 2 + k, :].unsqueeze(2).to_broadcast([P, NT, E]), ALU.mult))
                link(dve.tensor_tensor(weight[:], weight[:], weight2[:], ALU.add))
                dve.nop().then_inc(s["weights_ready"], 1)
                for t in range(NT):
                    dve.wait_ge(s["y_done"], b * NT + t + 1)
                    a = (t % 2) * BANK
                    wt = weighted[:, t % 2, :]
                    link(dve.tensor_tensor(wt.rearrange("p (e c) -> p e c", e=E),
                                           p_y[:, a:a + BANK].rearrange("p (e c) -> p e c", e=E),
                                           weight[:, t, :].unsqueeze(2).to_broadcast([P, E, C]), ALU.mult))
                    link(dve.tensor_reduce(y[:, t, :], wt.rearrange("p (e c) -> p c e", e=E), AX_X, ALU.add))
                    dve.nop().then_inc(s["y_read"], 1)
                    if t == BIAS_AFTER:
                        dve.wait_ge(s["weights_turned"], b + 1)
                        dve.tensor_copy(weight_t[:], p_h[0:NT * E, 0:P]).then_inc(s["weights_copied"], 1)
                link(dve.tensor_tensor(y[:], y[:], hb, ALU.add))
                dve.wait_ge(s["bias_done"], b + 1)
                link(dve.tensor_tensor(hb, y[:], p_h[0:P, BANK:BANK + NT * C].rearrange("p (t c) -> p t c", c=C), ALU.add))
                assert link.n == CHAIN, (link.n, CHAIN)

        @block.scalar
        def _(act):
            act.wait_ge(s["loaded"], LOADED)
            with act.Fori(0, batches) as b:
                for k in range(2):
                    act.wait_ge(s["var_ready"], b * 2 + k + 1)
                    act.activation(stat[:, 2, :], stat[:, 1, :], ACT.Sqrt).then_inc(s["root_ready"], 1)
                for e in range(E):
                    act.wait_ge(s["h_done"], b * E + e + 1)
                    act.activation(hidden[:, e, :].rearrange("p (h n) -> p h n", h=2),
                                   ap(p_h, 0, HID, (e % 2) * 2 * BANK, [[BANK, 2], [1, HALF]]), ACT.Gelu,
                                   bias=b1[:, e:e + 1]).then_inc(s["gelu_done"], 1)
                act.wait_ge(s["pair_diff"], b + 1)
                act.activation(pw[:, 1, :], pw[:, 0, :], ACT.Exp).then_inc(s["pair_exp"], 1)

def density_attention(nc, H, ident, w_qkv, w_proj, b_proj, batches=N_B):
    HD, BAND, N_TOKENS = C // HEADS, 16, N_B * W
    ITEMS = HEADS * NT
    with ExitStack() as ctx:
        m = Memory(nc, ctx, "den")
        xn = m.sb("xn", [P, TILES, C])
        before = m.sb("before", [P, TILES, C])
        stat = m.sb("stat", [P, 9, TILES])
        col = m.sb("col", [128, 8])
        ones = m.sb("ones", [P, 128])
        closed = m.sb("closed", [P, TILES])
        pause = m.sb("pause", [P, 1])
        qkv_in = m.sb("qkv_in", [C, 3, HEADS, HD])
        wqk = m.sb("wqk", [C, 2, 2, 4, 32])
        sum_groups = m.sb("sum_groups", [128, HD + 1])
        wproj = m.sb("wproj", [C + 1, C])
        outside = m.sb("outside", [P, NT, W])
        mask = m.sb("mask", [P, NT, W])
        xt = m.sb("xt", [C, W])
        xstage = m.sb("xstage", [P, NT, C])
        closed_wide = m.sb("closed_wide", [P, NT, P])
        closed_row = m.sb("closed_row", [P, W])
        key = m.sb("key", [128, 2, W])
        query = m.sb("query", [128, HEADS, W])
        val = m.sb("val", [P, NT, HEADS, 32])
        probs = m.sb("probs", [P, 4, W])
        neg_max = m.sb("neg_max", [P, ITEMS])
        top = m.sb("top", [P, ITEMS])
        total = m.sb("total", [P, HEADS, NT])
        turned = m.sb("turned", [P, 2, NT, W])
        sums = m.sb("sums", [128, 2, 4 * P])
        o = m.sb("o", [P, NT, C])
        ot = m.sb("ot", [C + 1, W])
        p_s = m.ps("p_s", [128, 4 * BANK])
        p_t = m.ps("p_t", [128, 2 * BANK])
        p_o = m.ps("p_o", [128, BANK])
        p_x = m.ps("p_x", [P, BANK])
        PARTS = ((0, 4), (4, NT - 4))
        names = ("loaded shifted xn_out var_ready root_ready sums_ready sums_done "
                 "consts x_ready xt_done xt_ready closed_done proj_done qk_v qk_a v_done v_copied mask_ready "
                 "s_done max_done neg_done exp_done turned_done copied_v copied_a pv_done sums_copied sums_turned o_ready ot_done "
                 "ot_ready out_done chain_c chain_b band ").split()
        s = {n: m.sem(n) for n in names}
        LOADED = 3 * 16
        block = ctx.enter_context(nc.Block())

        @block.sync
        def _(sp):
            sp.dma_start(qkv_in[:].rearrange("p a h c -> p (a h c)"), w_qkv).then_inc(s["loaded"], 16)
            sp.dma_start(wproj[0:C, :], w_proj).then_inc(s["loaded"], 16)
            sp.dma_start(wproj[C:C + 1, :], b_proj.rearrange("(a n) -> a n", a=1)).then_inc(s["loaded"], 16)
            sp.wait_ge(s["xn_out"], 1)
            sp.dma_start(before[1:P, :, :], xn[0:P - 1, :, :]).then_inc(s["shifted"], 16)
            seam = lambda t, p, k, n: ap(t, p, 1, k * C, [[NT * C, N_B], [1, n * C]])
            sp.dma_start(seam(before, 0, 1, NT - 1), seam(xn, P - 1, 0, NT - 1)).then_inc(s["shifted"], 16)
            sp.dma_start(seam(before, 0, 0, 1), seam(xn, 0, 0, 1)).then_inc(s["shifted"], 16)

        @block.gpsimd
        def _(pool):
            pool.memset(outside[:], 1.0).then_inc(s["band"], 1)
            for k, sign in enumerate((1, -1)):
                pool.wait_ge(s["band"], k + 1)
                pool.affine_select(out=outside[:], in_=outside[:], compare_op=ALU.is_gt, fill=0.0, base=BAND,
                                   pattern=[[sign * P, NT], [-sign, W]], channel_multiplier=sign).then_inc(s["band"], 1)

        @block.tensor
        def _(pe):
            for k in range(2):
                pe.wait_ge(s["sums_ready"], k + 1)
                pe.matmul(p_x[:, k:k + 1], ones[:, 0:P], col[0:P, k:k + 1], start=True, stop=True).then_inc(s["sums_done"], 1)
            pe.wait_ge(s["consts"], 1)

            def scores(b, i):
                h, t = divmod(i, NT)
                if i >= 2:
                    pe.wait_ge(s["max_done"], b * ITEMS + i - 1)
                for half in range(2):
                    a = (i % 2) * 2 * BANK + half * BANK
                    last = pe.matmul(p_s[0:P, a:a + HALF], query[:, h, t * P:(t + 1) * P],
                                     key[:, h // 4, half * HALF:(half + 1) * HALF], start=True, stop=True)
                last.then_inc(s["s_done"], 1)

            def weigh(b, h, part):
                t0, n = PARTS[part]
                if part:
                    pe.wait_ge(s["sums_copied"], b * 2 * HEADS + 2 * h + 1)
                elif h:
                    pe.wait_ge(s["sums_copied"], b * 2 * HEADS + 2 * h)
                for k in range(NT):
                    g = 32 * (k % 4)
                    last = pe.matmul(p_o[g:g + 32, 0:n * P], val[:, k, h, :],
                                     turned[:, h % 2, k, t0 * P:(t0 + n) * P], start=(k < 4), stop=(k + 4 >= NT),
                                     skip_group_check=True)
                last.then_inc(s["pv_done"], 1)

            def turn_sums(b, h, part):
                t0, n = PARTS[part]
                pe.wait_ge(s["sums_copied"], b * 2 * HEADS + 2 * h + part + 1)
                for t in range(t0, t0 + n):
                    c0 = (h * NT + t) * (HD + 1)
                    last = pe.matmul(p_x[:, c0:c0 + HD + 1], sums[:, part, (t - t0) * P:(t - t0 + 1) * P], sum_groups[:],
                                     start=True, stop=True)
                last.then_inc(s["sums_turned"], 1)

            def finish(b, h, step):
                if step == 1:
                    weigh(b, h, 0)
                elif step == 3:
                    turn_sums(b, h, 0)
                    weigh(b, h, 1)
                elif step == 5:
                    turn_sums(b, h, 1)

            with pe.Fori(0, batches) as b:
                pe.wait_ge(s["x_ready"], b + 1)
                turn_tiles(pe, p_t, xstage, ident).then_inc(s["xt_done"], 1)
                for t in range(NT):
                    c0 = (t // 4) * BANK + (t % 4) * P
                    last = pe.matmul(p_s[0:P, c0:c0 + P], closed_wide[:, t, :], ident[0:P, 0:P], start=True, stop=True)
                last.then_inc(s["closed_done"], 1)
                pe.wait_ge(s["xt_ready"], b + 1)
                for t in range(NT):
                    last = pe.matmul(p_x[:, t * C:(t + 1) * C], xt[:, t * P:(t + 1) * P],
                                     qkv_in[:, 2, :, :].rearrange("p h c -> p (h c)"), start=True, stop=True)
                last.then_inc(s["v_done"], 1)
                for n, (a, j) in enumerate(((0, 0), (1, 0), (0, 1), (1, 1))):
                    buf = 1 if n % 2 == 0 else 0
                    if n == 1:
                        pe.wait_ge(s["mask_ready"], b * 2 + 1)
                    if n >= 2:
                        pe.wait_ge(s["qk_v"] if n % 2 == 0 else s["qk_a"], b * 2 + 1)
                    for half in range(2):
                        c0 = buf * 2 * BANK + half * BANK
                        last = pe.matmul(p_s[:, c0:c0 + HALF], wqk[:, a, j, :, :].rearrange("p g c -> p (g c)"),
                                         xt[:, half * HALF:(half + 1) * HALF], start=True, stop=True)
                    last.then_inc(s["proj_done"], 1)
                pe.wait_ge(s["qk_v"], b * 2 + 2)
                pe.wait_ge(s["qk_a"], b * 2 + 2)
                scores(b, 0)
                scores(b, 1)
                for i in range(ITEMS):
                    h, t = divmod(i, NT)
                    pe.wait_ge(s["exp_done"], b * ITEMS + i + 1)
                    if i:
                        pe.wait_ge(s["copied_v"], b * ITEMS + i)
                        pe.wait_ge(s["copied_a"], b * ITEMS + i)
                    for k in range(NT):
                        c0 = (k // 4) * BANK + (k % 4) * P
                        last = pe.transpose(p_t[0:P, c0:c0 + P], probs[:, i % 4, k * P:(k + 1) * P], ident[0:P, 0:P])
                    last.then_inc(s["turned_done"], 1)
                    if i + 2 < ITEMS:
                        scores(b, i + 2)
                    if h:
                        finish(b, h - 1, t)
                pe.wait_ge(s["copied_v"], b * ITEMS + ITEMS)
                pe.wait_ge(s["copied_a"], b * ITEMS + ITEMS)
                for step in range(NT):
                    finish(b, HEADS - 1, step)
                pe.wait_ge(s["o_ready"], b + 1)
                turn_tiles(pe, p_t, o, ident).then_inc(s["ot_done"], 1)
                pe.wait_ge(s["ot_ready"], b + 1)
                for t in range(NT):
                    last = pe.matmul(p_o[0:P, t * C:(t + 1) * C], ot[:, t * P:(t + 1) * P], wproj[:], start=True, stop=True)
                last.then_inc(s["out_done"], 1)

        @block.vector
        def _(dve):
            link = Chain(dve, s["chain_c"])
            link(dve.memset(ones[:], 1.0))
            link(dve.memset(ot[C:C + 1, :], 1.0))
            link(dve.memset(wqk[:], 0.0))
            link(dve.memset(query[:], 0.0))
            link(dve.memset(val[:], 0.0))
            link(dve.memset(val[:, :, :, HD:HD + 1], 1.0))
            link(dve.tensor_tensor(sum_groups[:], ident[:, 0:HD + 1], ident[:, 32:32 + HD + 1], ALU.add))
            for g in (2, 3):
                link(dve.tensor_tensor(sum_groups[:], sum_groups[:], ident[:, 32 * g:32 * g + HD + 1], ALU.add))
            norm_tiles(dve, link, H[:], xn[:], before[:], stat, s["var_ready"], s["root_ready"], 1)
            dve.nop().then_inc(s["xn_out"], 1)
            mean, var, root, rstd, tmp, safe, grad, dens, work = (stat[:, k, :] for k in range(9))
            wide = [P, TILES, C]
            dve.wait_ge(s["shifted"], 3 * 16)
            link(dve.tensor_tensor(before[:], xn[:], before[:], ALU.subtract))
            link(dve.tensor_reduce(grad, before[:], AX_X, ALU.add, apply_absolute_value=True))
            link(dve.tensor_reduce(mean, xn[:], AX_X, ALU.add))
            link(dve.tensor_scalar(mean, mean, 1.0 / C, None, ALU.mult))
            link(dve.tensor_tensor(before[:], xn[:], mean.unsqueeze(2).to_broadcast(wide), ALU.subtract))
            link(dve.tensor_tensor(before[:], before[:], before[:], ALU.mult))
            link(dve.tensor_reduce(work, before[:], AX_X, ALU.add))
            link(dve.tensor_scalar(work, work, 1.0 / (C - 1), None, ALU.mult))
            dve.tensor_scalar(var, work, 1e-30, None, ALU.max).then_inc(s["var_ready"], 1)
            dve.wait_ge(s["root_ready"], 2)
            newton_rsqrt(dve, link, var, root, rstd, tmp)
            link(dve.tensor_tensor(work, work, rstd, ALU.mult))
            link(dve.tensor_scalar(grad, grad, 1.0 / C, None, ALU.mult))
            link(dve.tensor_tensor(dens, work, grad, ALU.add))
            link(dve.tensor_scalar(dens, dens, 0.5, None, ALU.mult))
            dve.tensor_reduce(col[0:P, 0:1], dens, AX_X, ALU.add).then_inc(s["sums_ready"], 1)
            dve.wait_ge(s["sums_done"], 1)
            link(dve.tensor_scalar(col[0:P, 2:3], p_x[:, 0:1], 1.0 / N_TOKENS, None, ALU.mult))
            link(dve.tensor_scalar(work, dens, col[0:P, 2:3], None, ALU.subtract))
            link(dve.tensor_tensor(work, work, work, ALU.mult))
            dve.tensor_reduce(col[0:P, 1:2], work, AX_X, ALU.add).then_inc(s["sums_ready"], 1)
            dve.wait_ge(s["sums_done"], 2)
            link(dve.tensor_scalar(col[0:P, 3:4], p_x[:, 1:2], 1.0 / (N_TOKENS - 1), None, ALU.mult))
            dve.tensor_scalar(var[:, 0:1], col[0:P, 3:4], 1e-30, None, ALU.max).then_inc(s["var_ready"], 1)
            dve.wait_ge(s["root_ready"], 3)
            newton_rsqrt(dve, link, var[:, 0:1], root[:, 0:1], rstd[:, 0:1], tmp[:, 0:1])
            link(dve.tensor_tensor(col[0:P, 4:5], col[0:P, 3:4], rstd[:, 0:1], ALU.mult))
            link(dve.tensor_scalar(col[0:P, 4:5], col[0:P, 4:5], 0.5, None, ALU.mult))
            link(dve.tensor_tensor(col[0:P, 4:5], col[0:P, 4:5], col[0:P, 2:3], ALU.add))
            link(dve.tensor_scalar(closed[:], dens, col[0:P, 4:5], -1e10, ALU.is_le, ALU.mult))
            dve.wait_ge(s["band"], 3)
            link(dve.tensor_scalar(outside[:], outside[:], -1.0, 1.0, ALU.mult, ALU.add))
            dve.wait_ge(s["loaded"], LOADED)
            for a in range(2):
                for j in range(2):
                    last = dve.tensor_copy(wqk[:, a, j, :, 0:HD], qkv_in[:, a, 4 * j:4 * j + 4, :])
            link(last)
            dve.nop().then_inc(s["consts"], 1)

            def row_max(b, i):
                t = i % NT
                dve.wait_ge(s["s_done"], b * ITEMS + i + 1)
                if i >= 4:
                    dve.wait_ge(s["turned_done"], b * ITEMS + i - 3)
                dve.memset(pause[:], 0.0)
                dve.tensor_tensor_reduce(probs[:, i % 4, :].rearrange("p (h n) -> p h n", h=2),
                                         ap(p_s, 0, P, (i % 2) * 2 * BANK, [[BANK, 2], [1, HALF]]),
                                         mask[:, t, :].rearrange("p (h n) -> p h n", h=2),
                                         1.0, -3e38, ALU.add, ALU.max, top[:, i:i + 1]).then_inc(s["max_done"], 1)
                dve.wait_ge(s["max_done"], b * ITEMS + i + 1)
                dve.tensor_scalar(neg_max[:, i:i + 1], top[:, i:i + 1], -1.0, None, ALU.mult).then_inc(s["neg_done"], 1)

            CHAIN = 9
            with dve.Fori(0, batches) as b:
                link = Chain(dve, s["chain_b"], b * CHAIN)
                hb = H[:, bass.ds(b * NT, NT), :]
                dve.tensor_copy(xstage[:], xn[:, bass.ds(b * NT, NT), :])
                dve.tensor_scalar(closed_wide[:], closed[:, bass.ds(b * NT, NT)].unsqueeze(2).to_broadcast([P, NT, P]),
                                  1.0, None, ALU.mult).then_inc(s["x_ready"], 1)
                dve.wait_ge(s["xt_done"], b + 1)
                link(dve.tensor_copy(xt[:, 0:4 * P], p_t[0:C, 0:4 * P]))
                link(dve.tensor_copy(xt[:, 4 * P:W], p_t[0:C, BANK:BANK + 3 * P]))
                dve.nop().then_inc(s["xt_ready"], 1)
                dve.wait_ge(s["closed_done"], b + 1)
                link(dve.tensor_copy(closed_row[:, 0:4 * P], p_s[0:P, 0:4 * P]))
                link(dve.tensor_copy(closed_row[:, 4 * P:W], p_s[0:P, BANK:BANK + 3 * P]))
                dve.nop().then_inc(s["mask_ready"], 1)
                link(dve.tensor_tensor(mask[:], outside[:], closed_row[:].unsqueeze(1).to_broadcast([P, NT, W]), ALU.mult))
                dve.nop().then_inc(s["mask_ready"], 1)
                dve.wait_ge(s["v_done"], b + 1)
                dve.tensor_copy(val[:, :, :, 0:HD], p_x[:, 0:NT * C].rearrange("p (t h c) -> p t h c", h=HEADS, c=HD))\
                   .then_inc(s["v_copied"], 1)
                for j in range(2):
                    dve.wait_ge(s["proj_done"], b * 4 + 2 * j + 1)
                    for g in range(4):
                        last = dve.tensor_scalar(
                            query[32 * g:32 * g + HD, 4 * j + g, :].rearrange("p (h n) -> p h n", h=2),
                            ap(p_s, 32 * g, HD, 2 * BANK, [[BANK, 2], [1, HALF]]), HD ** -0.5, None, ALU.mult)
                    last.then_inc(s["qk_v"], 1)
                row_max(b, 0)
                for i in range(ITEMS):
                    if i + 1 < ITEMS:
                        row_max(b, i + 1)
                    dve.wait_ge(s["turned_done"], b * ITEMS + i + 1)
                    h, t = divmod(i, NT)
                    if t == 0 and h >= 2:
                        dve.wait_ge(s["pv_done"], b * 2 * HEADS + 2 * h - 2)
                    dve.tensor_copy(turned[:, h % 2, 0:4, t * P:(t + 1) * P],
                                    p_t[0:P, 0:4 * P].rearrange("p (k q) -> p k q", q=P)).then_inc(s["copied_v"], 1)
                dve.wait_ge(s["sums_turned"], b * 2 * HEADS + 2 * HEADS)
                by_head = p_x[:, 0:HEADS * NT * (HD + 1)].rearrange("p (h t c) -> p h t c", h=HEADS, c=HD + 1)
                link(dve.reciprocal(total[:], by_head[:, :, :, HD:HD + 1].rearrange("p h t c -> p h (t c)")))
                dve.tensor_tensor(o[:].rearrange("p t (h c) -> p h t c", c=HD), by_head[:, :, :, 0:HD],
                                  total[:].unsqueeze(3).to_broadcast([P, HEADS, NT, HD]), ALU.mult).then_inc(s["o_ready"], 1)
                dve.wait_ge(s["ot_done"], b + 1)
                link(dve.tensor_copy(ot[0:C, 0:4 * P], p_t[0:C, 0:4 * P]))
                link(dve.tensor_copy(ot[0:C, 4 * P:W], p_t[0:C, BANK:BANK + 3 * P]))
                dve.nop().then_inc(s["ot_ready"], 1)
                dve.wait_ge(s["out_done"], b + 1)
                link(dve.tensor_tensor(hb, hb, p_o[0:P, 0:NT * C].rearrange("p (t c) -> p t c", c=C), ALU.add))
                assert link.n == CHAIN, link.n

        @block.scalar
        def _(act):
            act.wait_ge(s["var_ready"], 1)
            act.activation(stat[:, 2, :], stat[:, 1, :], ACT.Sqrt).then_inc(s["root_ready"], 1)
            act.wait_ge(s["var_ready"], 2)
            act.activation(stat[:, 2, :], stat[:, 1, :], ACT.Sqrt).then_inc(s["root_ready"], 1)
            act.wait_ge(s["var_ready"], 3)
            act.activation(stat[:, 2, 0:1], stat[:, 1, 0:1], ACT.Sqrt).then_inc(s["root_ready"], 1)

            def exponentials(b, i):
                act.wait_ge(s["neg_done"], b * ITEMS + i + 1)
                act.activation(probs[:, i % 4, :], probs[:, i % 4, :], ACT.Exp, bias=neg_max[:, i:i + 1],
).then_inc(s["exp_done"], 1)

            def copy_sums(b, h, part):
                act.wait_ge(s["pv_done"], b * 2 * HEADS + 2 * h + part + 1)
                if h:
                    act.wait_ge(s["sums_turned"], b * 2 * HEADS + 2 * h + part - 1)
                n = PARTS[part][1] * P
                act.activation(sums[:, part, 0:n], p_o[:, 0:n], ACT.Copy).then_inc(s["sums_copied"], 1)

            with act.Fori(0, batches) as b:
                for j in range(2):
                    act.wait_ge(s["proj_done"], b * 4 + 2 * j + 2)
                    act.activation(key[:, j, :].rearrange("p (h n) -> p h n", h=2),
                                   ap(p_s, 0, 128, 0, [[BANK, 2], [1, HALF]]), ACT.Copy).then_inc(s["qk_a"], 1)
                exponentials(b, 0)
                for i in range(ITEMS):
                    if i + 1 < ITEMS:
                        exponentials(b, i + 1)
                    act.wait_ge(s["turned_done"], b * ITEMS + i + 1)
                    h, t = divmod(i, NT)
                    if t == 0 and h >= 2:
                        act.wait_ge(s["pv_done"], b * 2 * HEADS + 2 * h - 2)
                    if h and t in (2, 4):
                        copy_sums(b, h - 1, t // 2 - 1)
                    act.activation(turned[:, h % 2, 4:7, t * P:(t + 1) * P],
                                   p_t[0:P, BANK:BANK + 3 * P].rearrange("p (k q) -> p k q", q=P),
                                   ACT.Copy).then_inc(s["copied_a"], 1)
                for part in range(2):
                    copy_sums(b, HEADS - 1, part)

def memory_attention(nc, H, ident, w_pk, pk_keys, w_q, table, w_o, batches=N_B):
    K1, DK, TOP = 64, 32, 16
    Q = 128
    NQ = -(-W // Q)
    WQ = NQ * Q
    HALF_Q = WQ // 2
    CANDS, n_c = [], 0
    for a0, na in ((0, 1), (1, 1), (2, 1), (3, 1), (4, 1), (5, 3), (8, 8)):
        nb = TOP // (a0 + 1)
        assert TOP // (a0 + na) == nb
        CANDS.append((a0, na, nb, n_c))
        n_c += na * nb
    SLOTS = 4
    assert HEADS % SLOTS == 0
    LOW = -3.0e38
    with ExitStack() as ctx:
        m = Memory(nc, ctx, "mem")
        keys_in = m.sb("keys_in", [K1, 2, HEADS * DK])
        wpk = m.sb("wpk", [C, 4, 128])
        wq = m.sb("wq", [C, 4, 128])
        wo = m.sb("wo", [128, 4, C])
        keys_bd = m.sb("keys_bd", [128, 4, 4 * K1])
        causal = m.sb("causal", [Q, Q])
        cand_int = m.sb("cand_int", [Q, n_c], mybir.dt.int32)
        cand_no = m.sb("cand_no", [Q, n_c])
        head_int = m.sb("head_int", [Q, HEADS], mybir.dt.int32)
        head_off = m.sb("head_off", [Q, HEADS])
        pause = m.sb("pause", [Q, 1])
        xn = m.sb("xn", [P, NT, C])
        square = m.sb("square", [P, NT, C])
        stat = m.sb("stat", [P, 5, NT])
        xt = m.sb("xt", [C, WQ])
        qpk = m.sb("qpk", [128, 4, WQ])
        qat = m.sb("qat", [128, 4, WQ])
        kat = m.sb("kat", [128, 4, WQ])
        sim = m.sb("sim", [Q, 2, HEADS, K1])
        rest = m.sb("rest", [Q, 2, HEADS, K1])
        s16 = m.sb("s16", [Q, 2, HEADS, TOP])
        i16 = m.sb("i16", [Q, 2, HEADS, TOP], U32)
        f16 = m.sb("f16", [Q, 2, HEADS, TOP])
        cand = m.sb("cand", [Q, HEADS, n_c])
        cand_rest = m.sb("cand_rest", [Q, HEADS, n_c])
        cand_row = m.sb("cand_row", [Q, HEADS, n_c])
        best = m.sb("best", [Q, HEADS, TOP])
        best_at = m.sb("best_at", [Q, HEADS, TOP], U32)
        best_no = m.sb("best_no", [Q, HEADS, TOP])
        match = m.sb("match", [Q, HEADS * TOP, n_c])
        rows_f = m.sb("rows_f", [Q, HEADS, TOP])
        expo = m.sb("expo", [Q, HEADS, TOP])
        esum = m.sb("esum", [Q, HEADS])
        rows = m.sb("rows", [Q, NQ, HEADS, TOP], U32)
        share = m.sb("share", [Q, NQ, HEADS, TOP])
        got = m.sb("got", [Q, SLOTS, TOP, 2 * C])
        kv = m.sb("kv", [Q, NQ, 2, HEADS, C])
        probs = m.sb("probs", [Q, 2, WQ])
        top = m.sb("top", [Q, NQ, HEADS])
        total = m.sb("total", [Q, NQ, HEADS])
        turned = m.sb("turned", [Q, 2, NQ, Q])
        o = m.sb("o", [Q, 4, 2 * C])
        ot = m.sb("ot", [128, 4, Q])
        result = m.sb("result", [C, W])
        p_s = m.ps("p_s", [128, 4 * BANK])
        p_t = m.ps("p_t", [128, 2 * BANK])
        p_o = m.ps("p_o", [Q, BANK])
        p_x = m.ps("p_x", [128, BANK])
        names = ("loaded made ready_c keys_turned var_ready root_ready xn_ready xt_done xt_ready proj_done proj_copied "
                 "x_done x_read fin_diff fin_exp rows_ready sums_done kat_ready s_done neg_done exp_done turned_done "
                 "slots_taken result_ready turned_copied pv_done o_ready ot_done ot_ready chain_c chain_b").split()
        s = {n: m.sem(n) for n in names}
        got_in = [m.sem(f"got_in{k}") for k in range(SLOTS)]
        LOADED = 4 * 16
        X_USES = 4 * NQ + 1
        SELECT_AFTER = 2
        block = ctx.enter_context(nc.Block())

        @block.sync
        def _(sp):
            sp.dma_start(keys_in[:], pk_keys.rearrange("p k h d -> k p (h d)")).then_inc(s["loaded"], 16)
            sp.dma_start(wpk[:].rearrange("p a n -> p (a n)"), w_pk).then_inc(s["loaded"], 16)
            sp.dma_start(wq[:].rearrange("p a n -> p (a n)"), w_q).then_inc(s["loaded"], 16)
            sp.dma_start(wo[:], w_o.rearrange("(a p) n -> p a n", p=128)).then_inc(s["loaded"], 16)

        @block.gpsimd
        def _(pool):
            pool.memset(causal[:], 0.0).then_inc(s["made"], 1)
            pool.iota(cand_int[:], [[1, n_c]], base=0, channel_multiplier=0).then_inc(s["made"], 1)
            pool.iota(head_int[:], [[K1 * K1, HEADS]], base=0, channel_multiplier=0).then_inc(s["made"], 1)
            pool.wait_ge(s["made"], 3)
            pool.affine_select(out=causal[:], in_=causal[:], compare_op=ALU.is_ge, fill=-1e30, base=0,
                               pattern=[[-1, Q]], channel_multiplier=1).then_inc(s["made"], 1)
            pool.sem_inc(s["sums_done"], SLOTS)
            with pool.Fori(0, batches) as b:
                for t in range(NQ):
                    pool.wait_ge(s["rows_ready"], b * NQ + t + 1)
                    for h in range(HEADS):
                        pool.wait_ge(s["sums_done"], (b * NQ + t) * HEADS + h + 1)
                        pool.sem_inc(s["slots_taken"], 1)
                        for k in range(TOP):
                            pool.indirect_dma_start(got[:, h % SLOTS, k, :], None, table,
                                                    bass.IndirectOffsetOnAxis(ap=rows[:, t, h, k:k + 1], axis=0))\
                                .then_inc(got_in[h % SLOTS], 16)

        @block.tensor
        def _(pe):
            pe.wait_ge(s["loaded"], LOADED)
            for a in range(4):
                last = pe.transpose(p_x[:, a * K1:(a + 1) * K1], keys_in[:, a // 2, (a % 2) * 128:(a % 2) * 128 + 128],
                                    ident[0:K1, 0:K1])
            last.then_inc(s["keys_turned"], 1)
            pe.wait_ge(s["ready_c"], 1)
            x_use = [0]

            def x_bank(b):
                pe.wait_ge(s["x_read"], b * X_USES + x_use[0] + 1)
                x_use[0] += 1

            def similarities(b, t):
                for p in range(2):
                    x_bank(b)
                    for c in range(2):
                        last = pe.matmul(p_x[0:Q, c * 256:(c + 1) * 256], qpk[:, 2 * p + c, t * Q:(t + 1) * Q],
                                         keys_bd[:, 2 * p + c, :], start=True, stop=True)
                    last.then_inc(s["x_done"], 1)

            def scores(b, t, h):
                it = b * NQ + t
                if h >= 2:
                    pe.wait_ge(s["exp_done"], it * HEADS + h - 1)
                r, n = C * (h % 2), (t + 1) * Q
                base = (h % 2) * 2 * BANK
                parts = ((base, 0, Q),) if t == 0 else ((base, 0, n // 2), (base + BANK, n // 2, n // 2))
                for c0, k0, w_ in parts:
                    last_part = k0 + w_ == n
                    pe.matmul(p_s[0:Q, c0:c0 + w_], qat[r:r + C, h // 2, t * Q:(t + 1) * Q],
                              kat[r:r + C, h // 2, k0:k0 + w_], start=True, stop=not last_part, skip_group_check=True)
                pe.matmul(p_s[0:Q, c0 + w_ - Q:c0 + w_], ident[0:Q, 0:Q], causal[:], start=False, stop=True,
                          skip_group_check=True).then_inc(s["s_done"], 1)

            def turn(b, t, h):
                it = b * NQ + t
                pe.wait_ge(s["exp_done"], it * HEADS + h + 1)
                pe.wait_ge(s["turned_copied"], it * HEADS + h + 1)
                for k in range(t + 1):
                    c0 = (k // 4) * BANK + (k % 4) * Q
                    last = pe.transpose(p_t[0:Q, c0:c0 + Q], probs[:, h % 2, k * Q:(k + 1) * Q], ident[0:Q, 0:Q])
                last.then_inc(s["turned_done"], 1)

            def weigh(b, t, h):
                it = b * NQ + t
                pe.wait_ge(s["turned_copied"], it * HEADS + h + 2)
                if h == 0:
                    pe.wait_ge(s["o_ready"], it + 1)
                for k in range(t + 1):
                    last = pe.matmul(p_o[:, h * C:(h + 1) * C], turned[:, h % 2, k, :], kv[:, k, 1, h, :],
                                     start=(k == 0), stop=(k == t))
                last.then_inc(s["pv_done"], 1)

            def attend(b, t, next_tile):
                it = b * NQ + t
                pe.wait_ge(s["kat_ready"], it + 1)
                scores(b, t, 0)
                for h in range(HEADS):
                    if h + 1 < HEADS:
                        scores(b, t, h + 1)
                    turn(b, t, h)
                    if h == SELECT_AFTER and next_tile is not None:
                        similarities(b, next_tile)
                    if h:
                        weigh(b, t, h - 1)
                weigh(b, t, HEADS - 1)
                pe.wait_ge(s["o_ready"], it + 2)
                for a in range(4):
                    last = pe.transpose(p_t[:, a * Q:(a + 1) * Q], o[:, a, :], ident[0:Q, 0:Q])
                last.then_inc(s["ot_done"], 1)
                x_bank(b)
                pe.wait_ge(s["ot_ready"], it + 1)
                for a in range(4):
                    last = pe.matmul(p_x[0:C, 0:Q], wo[:, a, :], ot[:, a, :], start=(a == 0), stop=(a == 3))
                last.then_inc(s["x_done"], 1)

            def project(b, first):
                for a in range(first, first + 4):
                    w_ = wpk[:, a, :] if a < 4 else wq[:, a - 4, :]
                    if a >= 2:
                        pe.wait_ge(s["proj_copied"], b * 8 + a - 1)
                    for half in range(2):
                        c0 = (a % 2) * 2 * BANK + half * BANK
                        last = pe.matmul(p_s[:, c0:c0 + HALF_Q], w_, xt[:, half * HALF_Q:(half + 1) * HALF_Q], start=True, stop=True)
                    last.then_inc(s["proj_done"], 1)
                pe.wait_ge(s["proj_copied"], b * 8 + first + 4)

            def prepare(b):
                pe.wait_ge(s["xn_ready"], b + 1)
                turn_tiles(pe, p_t, xn, ident).then_inc(s["xt_done"], 1)
                pe.wait_ge(s["xt_ready"], b + 1)
                project(b, 0)

            def turn_keys(b, t):
                x_bank(b)
                pe.wait_ge(s["sums_done"], (b * NQ + t + 1) * HEADS + SLOTS)
                for a in range(4):
                    last = pe.transpose(p_x[:, a * Q:(a + 1) * Q],
                                        kv[:, t, 0, 2 * a:2 * a + 2, :].rearrange("p h c -> p (h c)"), ident[0:Q, 0:Q])
                last.then_inc(s["x_done"], 1)

            def batch(b, is_last):
                x_use[0] = 2
                project(b, 4)
                for t in range(NQ + 1):
                    if t == 0:
                        similarities(b, 1)
                    else:
                        attend(b, t - 1, t + 1 if t + 1 < NQ else 0 if t + 1 == NQ and not is_last else None)
                    if t < NQ:
                        turn_keys(b, t)
                    if t == NQ - 2 and not is_last:
                        prepare(b + 1)
                x_bank(b)
                pe.wait_ge(s["result_ready"], b + 1)
                turn_back(pe, p_x, result, ident).then_inc(s["x_done"], 1)
                assert is_last or x_use[0] == X_USES + 2

            prepare(0)
            similarities(0, 0)
            with pe.Fori(0, batches - 1) as b:
                batch(b, False)
            batch(batches - 1, True)

        @block.vector
        def _(dve):
            link = Chain(dve, s["chain_c"])
            link(dve.memset(keys_bd[:], 0.0))
            link(dve.memset(xt[:], 0.0))
            dve.wait_ge(s["keys_turned"], 1)
            for g in range(4):
                link(dve.tensor_copy(keys_bd[DK * g:DK * g + DK, :, K1 * g:K1 * g + K1],
                                     ap(p_x, DK * g, DK, 0, [[K1, 4], [1, K1]])))
            dve.wait_ge(s["made"], 4)
            link(dve.tensor_copy(cand_no[:], cand_int[:]))
            link(dve.tensor_copy(head_off[:], head_int[:]))
            dve.nop().then_inc(s["x_read"], 1)
            dve.nop().then_inc(s["ready_c"], 1)
            dve.nop().then_inc(s["o_ready"], 1)

            def flat(v):
                return v.rearrange("p a b -> p (a b)")

            def top16(link, values, left, out, at, n):
                dve.memset(pause[:], 0.0)
                for v, w_ in zip(values, out):
                    last = dve.max(w_[:, 0:8], v)
                link(last)
                dve.memset(pause[:], 0.0)
                for v, r, w_ in zip(values, left, out):
                    last = dve.match_replace(r, w_[:, 0:8], v, LOW)
                link(last)
                dve.memset(pause[:], 0.0)
                for r, w_ in zip(left, out):
                    last = dve.max(w_[:, 8:16], r)
                link(last)
                dve.memset(pause[:], 0.0)
                for v, r, w_, i in zip(values, left, out, at):
                    dve.max_index(i[:, 0:8], w_[:, 0:8], v)
                    last = dve.max_index(i[:, 8:16], w_[:, 8:16], r)
                link(last)

            x_seen = [0]

            def x_wait(b):
                dve.wait_ge(s["x_done"], b * X_USES + x_seen[0] + 1)
                x_seen[0] += 1

            def select(b, t, link, it):
                for p in range(2):
                    x_wait(b)
                    dve.tensor_copy(sim[:, p, :, :], p_x[0:Q, :].rearrange("p (h k) -> p h k", h=HEADS)).then_inc(s["x_read"], 1)
                dve.wait_ge(s["x_read"], b * X_USES + x_seen[0] + 1)
                ph = [(p, h) for p in range(2) for h in range(HEADS)]
                top16(link, [sim[:, p, h, :] for p, h in ph], [rest[:, p, h, :] for p, h in ph],
                      [s16[:, p, h, :] for p, h in ph], [i16[:, p, h, :] for p, h in ph], K1)
                link(dve.tensor_copy(f16[:], i16[:]))
                link(dve.scalar_tensor_tensor(out=f16[:, 1, :, :], in0=f16[:, 1, :, :], scalar=float(K1),
                                              in1=head_off[:].unsqueeze(2).to_broadcast([Q, HEADS, TOP]),
                                              op0=ALU.mult, op1=ALU.add))
                for src, dst in ((s16, cand), (f16, cand_row)):
                    for a0, na, nb, at in CANDS:
                        first = ap(src, 0, Q, a0, [[TOP, HEADS], [1, na], [0, nb]])
                        second = ap(src, 0, Q, HEADS * TOP, [[TOP, HEADS], [0, na], [1, nb]])
                        last = dve.tensor_tensor(ap(dst, 0, Q, at, [[n_c, HEADS], [nb, na], [1, nb]]), first, second, ALU.add)
                link(last)
                hs_ = range(HEADS)
                top16(link, [cand[:, h, :] for h in hs_], [cand_rest[:, h, :] for h in hs_],
                      [best[:, h, :] for h in hs_], [best_at[:, h, :] for h in hs_], n_c)
                dve.tensor_tensor(expo[:], best[:], best[:, :, 0:1].to_broadcast([Q, HEADS, TOP]), ALU.subtract).then_inc(s["fin_diff"], 1)
                link(dve.tensor_copy(best_no[:], best_at[:]))
                link(dve.tensor_tensor(match[:], cand_no[:].unsqueeze(1).to_broadcast([Q, HEADS * TOP, n_c]),
                                       flat(best_no[:]).unsqueeze(2).to_broadcast([Q, HEADS * TOP, n_c]), ALU.is_equal))
                link(dve.tensor_tensor(match[:].rearrange("p (h k) c -> p h k c", h=HEADS),
                                       match[:].rearrange("p (h k) c -> p h k c", h=HEADS),
                                       cand_row[:].unsqueeze(2).to_broadcast([Q, HEADS, TOP, n_c]), ALU.mult))
                link(dve.tensor_reduce(flat(rows_f[:]), match[:], AX_X, ALU.add))
                dve.tensor_copy(rows[:, t, :, :], rows_f[:]).then_inc(s["rows_ready"], 1)
                dve.wait_ge(s["fin_exp"], it + 1)
                link(dve.tensor_reduce(esum[:], expo[:], AX_X, ALU.add))
                link(dve.reciprocal(esum[:], esum[:]))
                link(dve.tensor_tensor(share[:, t, :, :], expo[:], esum[:].unsqueeze(2).to_broadcast([Q, HEADS, TOP]), ALU.mult))

            def sum_rows(b, t, h, link):
                dve.wait_ge(got_in[h % SLOTS], ((b * NQ + t) * (HEADS // SLOTS) + h // SLOTS + 1) * 16 * TOP)
                g = got[:, h % SLOTS, :, :]
                link(dve.tensor_tensor(g, g, share[:, t, h, :].unsqueeze(2).to_broadcast([Q, TOP, 2 * C]), ALU.mult))
                dve.tensor_reduce(ap(kv, 0, Q, (t * 2 * HEADS + h) * C, [[HEADS * C, 2], [1, C]]),
                                  g.rearrange("p k (a c) -> p a c k", a=2), AX_X, ALU.add).then_inc(s["sums_done"], 1)

            def row_max(b, t, h):
                it = b * NQ + t
                dve.wait_ge(s["s_done"], it * HEADS + h + 1)
                n, base = (t + 1) * Q, (h % 2) * 2 * BANK
                src = p_s[0:Q, base:base + Q] if t == 0 else ap(p_s, 0, Q, base, [[BANK, 2], [1, n // 2]])
                axis = AX_X if t == 0 else mybir.AxisListType.XY
                dve.tensor_reduce(top[:, t, h:h + 1], src, axis, ALU.max, negate=True).then_inc(s["neg_done"], 1)

            def prepare(b, link):
                hb = H[:, bass.ds(b * NT, NT), :]
                norm_tiles(dve, link, hb, xn[:], square[:], stat, s["var_ready"], s["root_ready"], b + 1)
                dve.nop().then_inc(s["xn_ready"], 1)
                dve.wait_ge(s["xt_done"], b + 1)
                link(dve.tensor_copy(xt[:, 0:4 * P], p_t[0:C, 0:4 * P]))
                link(dve.tensor_copy(xt[:, 4 * P:W], p_t[0:C, BANK:BANK + 3 * P]))
                dve.nop().then_inc(s["xt_ready"], 1)

            def finish_tile(b, t, link):
                it = b * NQ + t
                dve.wait_ge(s["exp_done"], it * HEADS + HEADS)
                link(dve.reciprocal(total[:, t, :], total[:, t, :]))
                dve.wait_ge(s["pv_done"], it * HEADS + HEADS)
                dve.tensor_tensor(o[:].rearrange("p a (h c) -> p (a h) c", c=C),
                                  p_o[:].rearrange("p (h c) -> p h c", h=HEADS),
                                  total[:, t, :].unsqueeze(2).to_broadcast([Q, HEADS, C]), ALU.mult).then_inc(s["o_ready"], 1)
                x_wait(b)
                n = min(Q, W - t * Q)
                dve.tensor_copy(result[:, t * Q:t * Q + n], p_x[0:C, 0:n]).then_inc(s["x_read"], 1)

            def copy_keys(b, t):
                x_wait(b)
                dve.tensor_copy(kat[:, :, t * Q:(t + 1) * Q],
                                p_x[:, 0:4 * Q].rearrange("p (a q) -> p a q", a=4)).then_inc(s["x_read"], 1)
                dve.wait_ge(s["x_read"], b * X_USES + x_seen[0] + 1)
                dve.nop().then_inc(s["kat_ready"], 1)

            lead = Chain(dve, s["chain_b"])
            prepare(0, lead)
            select(0, 0, lead, 0)
            CHAIN = NORM_CHAIN + 2 + NQ * 27

            def batch(b, is_last):
                x_seen[0] = 2
                link = Chain(dve, s["chain_b"], lead.n + b * CHAIN)
                for t in range(NQ + 1):
                    for h in range(HEADS):
                        if t:
                            row_max(b, t - 1, h)
                        if t < NQ:
                            sum_rows(b, t, h, link)
                        if h == SELECT_AFTER and (t + 1 < NQ or t + 1 == NQ and not is_last):
                            select(b, (t + 1) % NQ, link, b * NQ + t + 1)
                    if t:
                        finish_tile(b, t - 1, link)
                    if t < NQ:
                        copy_keys(b, t)
                    if t == NQ - 2 and not is_last:
                        prepare(b + 1, link)
                dve.wait_ge(s["x_read"], b * X_USES + x_seen[0] + 1)
                dve.nop().then_inc(s["result_ready"], 1)
                x_wait(b)
                hb = H[:, bass.ds(b * NT, NT), :]
                dve.tensor_tensor(hb, hb, p_x[0:P, 0:NT * C].rearrange("p (t c) -> p t c", c=C), ALU.add)\
                   .then_inc(s["x_read"], 1)
                assert is_last or link.n == CHAIN, link.n

            with dve.Fori(0, batches - 1) as b:
                batch(b, False)
            batch(batches - 1, True)

        @block.scalar
        def _(act):
            def final_exp(it):
                act.wait_ge(s["fin_diff"], it + 1)
                act.activation(expo[:], expo[:], ACT.Exp).then_inc(s["fin_exp"], 1)

            def copy_projections(b, first):
                for a in range(first, first + 4):
                    act.wait_ge(s["proj_done"], b * 8 + a + 1)
                    dst = qpk[:, a, :] if a < 4 else qat[:, a - 4, :]
                    act.activation(dst.rearrange("p (h n) -> p h n", h=2),
                                   ap(p_s, 0, 128, (a % 2) * 2 * BANK, [[BANK, 2], [1, HALF_Q]]), ACT.Copy,
                                   scale=1.0 if a < 4 else C ** -0.5).then_inc(s["proj_copied"], 1)

            def prepare(b):
                act.wait_ge(s["var_ready"], b + 1)
                act.activation(stat[:, 2, :], stat[:, 1, :], ACT.Sqrt).then_inc(s["root_ready"], 1)
                copy_projections(b, 0)

            def exponentials(b, q, h):
                it, n = b * NQ + q, (q + 1) * Q
                act.wait_ge(s["neg_done"], it * HEADS + h + 1)
                if h >= 2:
                    act.wait_ge(s["turned_done"], it * HEADS + h - 1)
                base = (h % 2) * 2 * BANK
                if q == 0:
                    dst, src = probs[:, h % 2, 0:Q], p_s[0:Q, base:base + Q]
                else:
                    dst = probs[:, h % 2, 0:n].rearrange("p (h n) -> p h n", h=2)
                    src = ap(p_s, 0, Q, base, [[BANK, 2], [1, n // 2]])
                act.activation(dst, src, ACT.Exp, bias=top[:, q, h:h + 1],
                               accum_out=total[:, q, h:h + 1]).then_inc(s["exp_done"], 1)

            def copy_turned(b, q, h):
                it = b * NQ + q
                act.wait_ge(s["turned_done"], it * HEADS + h + 1)
                if h >= 2:
                    act.wait_ge(s["pv_done"], it * HEADS + h - 1)
                for k, n in ((0, min(q + 1, 4)), (4, q + 1 - 4)):
                    if n > 0:
                        last = act.activation(turned[:, h % 2, k:k + n, :],
                                              p_t[0:Q, k // 4 * BANK:k // 4 * BANK + n * Q].rearrange("p (k q) -> p k q", q=Q),
                                              ACT.Copy)
                last.then_inc(s["turned_copied"], 1)

            def batch(b, is_last):
                copy_projections(b, 4)
                for t in range(NQ + 1):
                    for h in range(HEADS):
                        if t:
                            exponentials(b, t - 1, h)
                            copy_turned(b, t - 1, h)
                        if h == SELECT_AFTER and (t + 1 < NQ or t + 1 == NQ and not is_last):
                            final_exp(b * NQ + t + 1)
                    if t:
                        act.wait_ge(s["ot_done"], b * NQ + t)
                        act.activation(ot[:], p_t[:, 0:4 * Q].rearrange("p (a q) -> p a q", a=4), ACT.Copy).then_inc(s["ot_ready"], 1)
                    if t == NQ - 2 and not is_last:
                        prepare(b + 1)

            act.sem_inc(s["turned_copied"], 1)
            prepare(0)
            final_exp(0)
            with act.Fori(0, batches - 1) as b:
                batch(b, False)
            batch(batches - 1, True)

def audio_tower(nc, out, x, tok, l1, ffn, density, memory):
    with ExitStack() as ctx:
        H = ctx.enter_context(nc.sbuf_tensor("H", [P, TILES, C], F32))
        ident = ctx.enter_context(nc.sbuf_tensor("ident", [128, 128], F32))
        out_written = ctx.enter_context(nc.semaphore("out_written"))
        local_attention(nc, H, ident, x, *tok)
        l1_attention(nc, H, ident, *l1)
        expert_ffn(nc, H, ident, *ffn)
        density_attention(nc, H, ident, *density)
        memory_attention(nc, H, ident, *memory)
        with nc.Block() as block:
            @block.sync
            def _(sp):
                sp.dma_start(out.rearrange("b (t p) c -> p (b t) c", p=P), H[:]).then_inc(out_written, 16)
                sp.wait_ge(out_written, 16)


STAGE_INPUTS = [
    ("L0_tok_W_qry", "L0_tok_W_key", "L0_tok_v", "L0_tok_b"),
    ("L0_attn_wqv_w", "L0_attn_wqv_b", "L0_attn_wk", "L0_attn_fanin_w", "L0_attn_fanin_b"),
    ("L0_ffn_gamma", "L0_ffn_beta", "L0_ffn_Wr", "L0_ffn_br", "L0_ffn_W1", "L0_ffn_b1", "L0_ffn_W2", "L0_ffn_b2"),
    ("L1_attn_w_qkv", "L1_attn_w_proj", "L1_attn_b_proj"),
    ("L1_ffn_Wq_pk", "L1_ffn_pk_keys", "L1_ffn_Wq", "L1_ffn_table", "L1_ffn_Wo")]


def kernel(**inputs):
    import concourse.bacc as bacc
    from concourse.bass_utils import run_bass_kernel_spmd

    inputs = dict(inputs)
    inputs["L1_ffn_table"] = np.concatenate([np.asarray(inputs.pop("L1_ffn_keys_table")),
                                             np.asarray(inputs.pop("L1_ffn_values_table"))], axis=1)
    nc = bacc.Bacc("TRN2", target_bir_lowering=False, num_devices=1)
    arrays, drams = {}, {}
    for name in ["x"] + [n for names in STAGE_INPUTS for n in names]:
        a = np.ascontiguousarray(inputs[name])
        arrays[f"in_{name}_dram"] = a
        drams[name] = nc.dram_tensor(f"in_{name}_dram", a.shape, mybir.dt.from_np(a.dtype), kind="ExternalInput").ap()
    out = nc.dram_tensor("out_dram", (N_B, W, C), F32, kind="ExternalOutput").ap()
    audio_tower(nc, out, drams["x"], *[[drams[n] for n in names] for names in STAGE_INPUTS])
    r = run_bass_kernel_spmd(nc, [arrays], core_ids=[0])
    return r.results[0]["out_dram"]
```
